# Optimizing a Trainium2 kernel written in Bass

```python
import numpy as np
import jax
import jax.numpy as jnp

def _softmax(x, axis=-1):
    return jax.nn.softmax(x, axis=axis)

def _gelu(x):
    return jax.nn.gelu(x, approximate=True)

def _silu(x):
    return jax.nn.silu(x)

def _sigmoid(x):
    return jax.nn.sigmoid(x)

def _layernorm(x, axis=-1, eps=1e-05):
    m = jnp.mean(x, axis=axis, keepdims=True)
    v = jnp.var(x, axis=axis, keepdims=True)
    return (x - m) / jnp.sqrt(v + eps)

def _scatter_add(tgt, idx, src, axis=0):
    return tgt.at[idx].add(src)

def _segment_sum(src, seg, n):
    return jax.ops.segment_sum(src, seg, n)
kernel_name = 'mk_decoder_preln_d2_seqx_r2_6e9c13'

def setup_inputs(seed: int=0):
    np.random.seed(seed)
    _w = jnp.asarray

    def _rec_inputs():
        import jax
        import jax.numpy as jnp
        _rk = jax.random.key(seed)
        x = 7.22e-05 + 1 * jax.random.normal(jax.random.fold_in(_rk, 1), (8, 100, 512), jnp.float32)
        _lenS = 100 - jax.random.randint(jax.random.fold_in(_rk, 7), (8,), 0, max(1, 100 // 4) + 1, jnp.int32)
        _lenS2 = 722 - jax.random.randint(jax.random.fold_in(_rk, 8), (8,), 0, max(1, 722 // 4) + 1, jnp.int32)
        _ctx_768P = jax.random.normal(jax.random.fold_in(_rk, 11), (8, 16, 384), jnp.float32)
        _ctx_768c = jax.random.dirichlet(jax.random.fold_in(_rk, 511), 0.3 * jnp.ones((16,), jnp.float32), (8, 722))
        _ctx_768t = jnp.einsum('bsk,bkd->bsd', _ctx_768c, _ctx_768P)
        _ctx_768t = _ctx_768t * jax.lax.rsqrt(jnp.mean(jnp.square(_ctx_768t)) + 1e-12) * 0.953939
        ctx_768 = -0.000191848 + 0.999787 * (_ctx_768t + 0.3 * jax.random.normal(jax.random.fold_in(_rk, 611), (8, 722, 384), jnp.float32))
        return (x, ctx_768)
    x, ctx_768 = _rec_inputs()

    def _L0_attn_setup():
        import jax, jax.numpy as jnp
        import numpy as np
        LN_EPS = 1e-05
        NEG_INF = -1e+38

        def _layer_norm(x, g, b):
            mu = x.mean(-1, keepdims=True)
            var = ((x - mu) ** 2).mean(-1, keepdims=True)
            return (x - mu) * jax.lax.rsqrt(var + LN_EPS) * g + b

        def _wkv(w, u, k, v):
            B, T, C = k.shape
            kt = jnp.swapaxes(k, 0, 1)
            vt = jnp.swapaxes(v, 0, 1)
            aa0 = jnp.zeros((B, C), k.dtype)
            bb0 = jnp.zeros((B, C), k.dtype)
            pp0 = jnp.full((B, C), NEG_INF, k.dtype)

            def step(carry, inp):
                aa, bb, pp = carry
                kk, vv = inp
                p = jnp.maximum(pp, u + kk)
                e1 = jnp.exp(pp - p)
                e2 = jnp.exp(u + kk - p)
                y = (e1 * aa + e2 * vv) / (e1 + e2)
                p2 = jnp.maximum(pp + w, w + kk)
                e1u = jnp.exp(pp + w - p2)
                e2u = jnp.exp(w + kk - p2)
                aa2 = e1u * aa + e2u * vv
                bb2 = e1u + e2u
                pp2 = p2 + jnp.log(bb2)
                return ((aa2, bb2, pp2), y)
            _, ys = jax.lax.scan(step, (aa0, bb0, pp0), (kt, vt))
            return jnp.swapaxes(ys, 0, 1)

        def _shift(h):
            return jnp.pad(h[:, :-1, :], ((0, 0), (1, 0), (0, 0)))
        key = jax.random.key(seed)
        B, T, C = (8, 1024, 512)
        ks = jax.random.split(key, 12)
        s = 0.02
        return {'x': jax.random.normal(ks[0], (B, T, C), jnp.float32), 'time_decay': jax.random.normal(ks[1], (C,), jnp.float32) * 0.01, 'time_first': jax.random.normal(ks[2], (C,), jnp.float32) * 0.01, 'w_tk': jax.random.normal(ks[3], (C, C), jnp.float32) * s, 'w_tv': jax.random.normal(ks[4], (C, C), jnp.float32) * s, 'w_tr': jax.random.normal(ks[5], (C, C), jnp.float32) * s, 'w_ck': jax.random.normal(ks[6], (C, 4 * C), jnp.float32) * s, 'w_cv': jax.random.normal(ks[7], (4 * C, C), jnp.float32) * s, 'w_cr': jax.random.normal(ks[8], (C, C), jnp.float32) * s, 'ln1_g': jnp.ones((C,), jnp.float32), 'ln1_b': jnp.zeros((C,), jnp.float32), 'ln2_g': jnp.ones((C,), jnp.float32), 'ln2_b': jnp.zeros((C,), jnp.float32), 'mix_k': jnp.ones((1, 1, C), jnp.float32), 'mix_v': jnp.ones((1, 1, C), jnp.float32), 'mix_r': jnp.ones((1, 1, C), jnp.float32), 'cmix_k': jnp.ones((1, 1, C), jnp.float32), 'cmix_r': jnp.ones((1, 1, C), jnp.float32)}
    _L0_attn_all = _L0_attn_setup()
    _L0_attn_in = {k: v for k, v in _L0_attn_all.items() if k in ('time_decay', 'time_first', 'w_tk', 'w_tv', 'w_tr', 'w_ck', 'w_cv', 'w_cr', 'ln1_g', 'ln1_b', 'ln2_g', 'ln2_b', 'mix_k', 'mix_v', 'mix_r', 'cmix_k', 'cmix_r')}
    del _L0_attn_all

    def _L0_xattn_setup():
        import jax, jax.numpy as jnp
        import numpy as np
        NUM_HEADS = 16
        CLAMP = 10000.0
        key = jax.random.key(seed)
        ks = jax.random.split(key, 8)
        B, Nq, Nkv, Cq, Ckv = (4, 1024, 1024, 512, 384)
        s_q = 1.0 / np.sqrt(Cq)
        s_kv = 1.0 / np.sqrt(Ckv)
        return {'query': jax.random.normal(ks[0], (B, Nq, Cq), jnp.float32), 'key_value': jax.random.normal(ks[1], (B, Nkv, Ckv), jnp.float32), 'Wq': jax.random.normal(ks[2], (Cq, Cq), jnp.float32) * s_q, 'bq': jnp.zeros((Cq,), jnp.float32), 'Wk': jax.random.normal(ks[3], (Ckv, Cq), jnp.float32) * s_kv, 'bk': jnp.zeros((Cq,), jnp.float32), 'Wv': jax.random.normal(ks[4], (Ckv, Cq), jnp.float32) * s_kv, 'bv': jnp.zeros((Cq,), jnp.float32), 'Wo': jax.random.normal(ks[5], (Cq, Cq), jnp.float32) * s_q, 'bo': jnp.zeros((Cq,), jnp.float32)}
    _L0_xattn_all = _L0_xattn_setup()
    _L0_xattn_in = {k: v for k, v in _L0_xattn_all.items() if k in ('Wq', 'bq', 'Wk', 'bk', 'Wv', 'bv', 'Wo', 'bo')}
    del _L0_xattn_all

    def _L0_ffn_setup():
        import jax, jax.numpy as jnp
        import numpy as np
        E = 8
        TOP_K = 2
        D = 512
        DFF = 4 * D
        key = jax.random.key(seed)
        ks = jax.random.split(key, 6)
        b, s = (4, 512)
        x = jax.random.normal(ks[0], (b, s, D), dtype=jnp.float32)
        centroids = jax.random.normal(ks[1], (E, D), dtype=jnp.float32)
        W1 = jax.random.normal(ks[2], (E, D, DFF), dtype=jnp.float32) * (1.0 / np.sqrt(D))
        b1 = jax.random.normal(ks[3], (E, DFF), dtype=jnp.float32) * 0.01
        W2 = jax.random.normal(ks[4], (E, DFF, D), dtype=jnp.float32) * (1.0 / np.sqrt(DFF))
        b2 = jax.random.normal(ks[5], (E, D), dtype=jnp.float32) * 0.01
        return {'x': x, 'centroids': centroids, 'W1': W1, 'b1': b1, 'W2': W2, 'b2': b2}
    _L0_ffn_all = _L0_ffn_setup()
    _L0_ffn_in = {k: v for k, v in _L0_ffn_all.items() if k in ('centroids', 'W1', 'b1', 'W2', 'b2')}
    del _L0_ffn_all

    def _L1_attn_setup():
        import jax, jax.numpy as jnp
        import numpy as np
        GAMMA = 0.96875
        H = 512
        B = 4
        L = 1024
        key = jax.random.key(seed)
        k0, k1, k2, k3, k4 = jax.random.split(key, 5)
        x = jax.random.normal(k0, (B, L, H), dtype=jnp.float32)
        weight_q = jax.random.normal(k1, (H, H), dtype=jnp.float32) / H
        weight_k = jax.random.normal(k2, (H, H), dtype=jnp.float32) / H
        weight_v = jax.random.normal(k3, (H, H), dtype=jnp.float32) / H
        theta = jax.random.normal(k4, (H,), dtype=jnp.float32) / H
        return {'x': x, 'weight_q': weight_q, 'weight_k': weight_k, 'weight_v': weight_v, 'theta': theta}
    _L1_attn_all = _L1_attn_setup()
    _L1_attn_in = {k: v for k, v in _L1_attn_all.items() if k in ('weight_q', 'weight_k', 'weight_v', 'theta')}
    del _L1_attn_all

    def _L1_xattn_setup():
        import jax, jax.numpy as jnp
        import numpy as np
        HEADS = 16
        DIM_HEAD = 64
        SCALE = DIM_HEAD ** (-0.5)
        key = jax.random.key(seed)
        ks = jax.random.split(key, 6)
        B, N, C = (4, 2048, 512)
        M, Cc = (256, 384)
        inner = HEADS * DIM_HEAD
        s = lambda d: d ** (-0.5)
        return {'x': jax.random.normal(ks[0], (B, N, C), jnp.float32), 'context': jax.random.normal(ks[1], (B, M, Cc), jnp.float32), 'Wq': jax.random.normal(ks[2], (C, inner), jnp.float32) * s(C), 'Wk': jax.random.normal(ks[3], (Cc, inner), jnp.float32) * s(Cc), 'Wv': jax.random.normal(ks[4], (Cc, inner), jnp.float32) * s(Cc), 'Wo': jax.random.normal(ks[5], (inner, C), jnp.float32) * s(inner), 'bo': jnp.zeros((C,), jnp.float32)}
    _L1_xattn_all = _L1_xattn_setup()
    _L1_xattn_in = {k: v for k, v in _L1_xattn_all.items() if k in ('Wq', 'Wk', 'Wv', 'Wo', 'bo')}
    del _L1_xattn_all

    def _L1_ffn_setup():
        import jax, jax.numpy as jnp
        import numpy as np
        GROUP = 16
        EPS = 1e-05

        def _dequant(q, scale):
            w = q.astype(jnp.float32) / 7.5 - 1.0
            return w * jnp.repeat(scale, GROUP, axis=1)

        def _qlora_linear(x, q, scale, bias, la, lb):
            w = _dequant(q, scale)
            base = jnp.einsum('btd,od->bto', x, w) + bias
            lora = jnp.einsum('btr,or->bto', jnp.einsum('btd,rd->btr', x, la), lb)
            return base + lora

        def _layernorm(x, g, b):
            mu = jnp.mean(x, axis=-1, keepdims=True)
            var = jnp.mean(jnp.square(x - mu), axis=-1, keepdims=True)
            return (x - mu) * jax.lax.rsqrt(var + EPS) * g + b
        key = jax.random.key(seed)
        ks = jax.random.split(key, 6)
        D, R, B, T = (512, 32, 8, 2048)
        x = jax.random.normal(ks[0], (B, T, D), dtype=jnp.float32)
        qweights = jax.random.randint(ks[1], (6, D, D), 0, 16, dtype=jnp.int32)
        scales = jax.random.uniform(ks[2], (6, D, D // GROUP), dtype=jnp.float32)
        biases = jax.random.normal(ks[3], (6, D), dtype=jnp.float32) * 0.02
        lora_a = jax.random.normal(ks[4], (6, R, D), dtype=jnp.float32) * 0.02
        lora_b = jax.random.normal(ks[5], (6, D, R), dtype=jnp.float32) * 0.02
        ln_gamma = jnp.ones((3, D), dtype=jnp.float32)
        ln_beta = jnp.zeros((3, D), dtype=jnp.float32)
        return {'x': x, 'qweights': qweights, 'scales': scales, 'biases': biases, 'lora_a': lora_a, 'lora_b': lora_b, 'ln_gamma': ln_gamma, 'ln_beta': ln_beta}
    _L1_ffn_all = _L1_ffn_setup()
    _L1_ffn_in = {k: v for k, v in _L1_ffn_all.items() if k in ('qweights', 'scales', 'biases', 'lora_a', 'lora_b', 'ln_gamma', 'ln_beta')}
    del _L1_ffn_all
    return {'x': x, 'ctx_768': ctx_768, 'L0_attn_time_decay': _L0_attn_in['time_decay'], 'L0_attn_time_first': _L0_attn_in['time_first'], 'L0_attn_w_tk': _L0_attn_in['w_tk'], 'L0_attn_w_tv': _L0_attn_in['w_tv'], 'L0_attn_w_tr': _L0_attn_in['w_tr'], 'L0_attn_w_ck': _L0_attn_in['w_ck'], 'L0_attn_w_cv': _L0_attn_in['w_cv'], 'L0_attn_w_cr': _L0_attn_in['w_cr'], 'L0_attn_ln1_g': _L0_attn_in['ln1_g'], 'L0_attn_ln1_b': _L0_attn_in['ln1_b'], 'L0_attn_ln2_g': _L0_attn_in['ln2_g'], 'L0_attn_ln2_b': _L0_attn_in['ln2_b'], 'L0_attn_mix_k': _L0_attn_in['mix_k'], 'L0_attn_mix_v': _L0_attn_in['mix_v'], 'L0_attn_mix_r': _L0_attn_in['mix_r'], 'L0_attn_cmix_k': _L0_attn_in['cmix_k'], 'L0_attn_cmix_r': _L0_attn_in['cmix_r'], 'L0_xattn_Wq': _L0_xattn_in['Wq'], 'L0_xattn_bq': _L0_xattn_in['bq'], 'L0_xattn_Wk': _L0_xattn_in['Wk'], 'L0_xattn_bk': _L0_xattn_in['bk'], 'L0_xattn_Wv': _L0_xattn_in['Wv'], 'L0_xattn_bv': _L0_xattn_in['bv'], 'L0_xattn_Wo': _L0_xattn_in['Wo'], 'L0_xattn_bo': _L0_xattn_in['bo'], 'L0_ffn_centroids': _L0_ffn_in['centroids'], 'L0_ffn_W1': _L0_ffn_in['W1'], 'L0_ffn_b1': _L0_ffn_in['b1'], 'L0_ffn_W2': _L0_ffn_in['W2'], 'L0_ffn_b2': _L0_ffn_in['b2'], 'L1_attn_weight_q': _L1_attn_in['weight_q'], 'L1_attn_weight_k': _L1_attn_in['weight_k'], 'L1_attn_weight_v': _L1_attn_in['weight_v'], 'L1_attn_theta': _L1_attn_in['theta'], 'L1_xattn_Wq': _L1_xattn_in['Wq'], 'L1_xattn_Wk': _L1_xattn_in['Wk'], 'L1_xattn_Wv': _L1_xattn_in['Wv'], 'L1_xattn_Wo': _L1_xattn_in['Wo'], 'L1_xattn_bo': _L1_xattn_in['bo'], 'L1_ffn_qweights': _L1_ffn_in['qweights'], 'L1_ffn_scales': _L1_ffn_in['scales'], 'L1_ffn_biases': _L1_ffn_in['biases'], 'L1_ffn_lora_a': _L1_ffn_in['lora_a'], 'L1_ffn_lora_b': _L1_ffn_in['lora_b'], 'L1_ffn_ln_gamma': _L1_ffn_in['ln_gamma'], 'L1_ffn_ln_beta': _L1_ffn_in['ln_beta']}

def reference(x, ctx_768, L0_attn_time_decay, L0_attn_time_first, L0_attn_w_tk, L0_attn_w_tv, L0_attn_w_tr, L0_attn_w_ck, L0_attn_w_cv, L0_attn_w_cr, L0_attn_ln1_g, L0_attn_ln1_b, L0_attn_ln2_g, L0_attn_ln2_b, L0_attn_mix_k, L0_attn_mix_v, L0_attn_mix_r, L0_attn_cmix_k, L0_attn_cmix_r, L0_xattn_Wq, L0_xattn_bq, L0_xattn_Wk, L0_xattn_bk, L0_xattn_Wv, L0_xattn_bv, L0_xattn_Wo, L0_xattn_bo, L0_ffn_centroids, L0_ffn_W1, L0_ffn_b1, L0_ffn_W2, L0_ffn_b2, L1_attn_weight_q, L1_attn_weight_k, L1_attn_weight_v, L1_attn_theta, L1_xattn_Wq, L1_xattn_Wk, L1_xattn_Wv, L1_xattn_Wo, L1_xattn_bo, L1_ffn_qweights, L1_ffn_scales, L1_ffn_biases, L1_ffn_lora_a, L1_ffn_lora_b, L1_ffn_ln_gamma, L1_ffn_ln_beta):
    import jax
    import jax.numpy as jnp

    def _L0_attn_ref(x, time_decay, time_first, w_tk, w_tv, w_tr, w_ck, w_cv, w_cr, ln1_g, ln1_b, ln2_g, ln2_b, mix_k, mix_v, mix_r, cmix_k, cmix_r):
        import jax, jax.numpy as jnp
        import numpy as np
        LN_EPS = 1e-05
        NEG_INF = -1e+38

        def _layer_norm(x, g, b):
            mu = x.mean(-1, keepdims=True)
            var = ((x - mu) ** 2).mean(-1, keepdims=True)
            return (x - mu) * jax.lax.rsqrt(var + LN_EPS) * g + b

        def _wkv(w, u, k, v):
            B, T, C = k.shape
            kt = jnp.swapaxes(k, 0, 1)
            vt = jnp.swapaxes(v, 0, 1)
            aa0 = jnp.zeros((B, C), k.dtype)
            bb0 = jnp.zeros((B, C), k.dtype)
            pp0 = jnp.full((B, C), NEG_INF, k.dtype)

            def step(carry, inp):
                aa, bb, pp = carry
                kk, vv = inp
                p = jnp.maximum(pp, u + kk)
                e1 = jnp.exp(pp - p)
                e2 = jnp.exp(u + kk - p)
                y = (e1 * aa + e2 * vv) / (e1 + e2)
                p2 = jnp.maximum(pp + w, w + kk)
                e1u = jnp.exp(pp + w - p2)
                e2u = jnp.exp(w + kk - p2)
                aa2 = e1u * aa + e2u * vv
                bb2 = e1u + e2u
                pp2 = p2 + jnp.log(bb2)
                return ((aa2, bb2, pp2), y)
            _, ys = jax.lax.scan(step, (aa0, bb0, pp0), (kt, vt))
            return jnp.swapaxes(ys, 0, 1)

        def _shift(h):
            return jnp.pad(h[:, :-1, :], ((0, 0), (1, 0), (0, 0)))
        h = _layer_norm(x, ln1_g, ln1_b)
        hp = _shift(h)
        xk = h * mix_k + hp * (1.0 - mix_k)
        xv = h * mix_v + hp * (1.0 - mix_v)
        xr = h * mix_r + hp * (1.0 - mix_r)
        k = xk @ w_tk
        v = xv @ w_tv
        r = jax.nn.sigmoid(xr @ w_tr)
        y = _wkv(time_decay, time_first, k, v)
        x = x + r * y
        h2 = _layer_norm(x, ln2_g, ln2_b)
        hp2 = _shift(h2)
        ck = h2 * cmix_k + hp2 * (1.0 - cmix_k)
        cr = h2 * cmix_r + hp2 * (1.0 - cmix_r)
        kk = jnp.square(jax.nn.relu(ck @ w_ck))
        x = x + jax.nn.sigmoid(cr @ w_cr) * (kk @ w_cv)
        return x

    def _L0_xattn_ref(query, key_value, Wq, bq, Wk, bk, Wv, bv, Wo, bo):
        import jax, jax.numpy as jnp
        import numpy as np
        NUM_HEADS = 16
        CLAMP = 10000.0
        B, Nq, Cq = query.shape
        Nkv = key_value.shape[1]
        H = NUM_HEADS
        D = Cq // H
        scale = D ** (-0.5)
        q = (query @ Wq + bq).reshape(B, Nq, H, D).transpose(0, 2, 1, 3)
        k = (key_value @ Wk + bk).reshape(B, Nkv, H, D).transpose(0, 2, 1, 3)
        v = (key_value @ Wv + bv).reshape(B, Nkv, H, D).transpose(0, 2, 1, 3)
        attn = jnp.einsum('bhqd,bhkd->bhqk', q, k) * scale
        attn = jnp.clip(attn, -CLAMP, CLAMP)
        attn = jax.nn.softmax(attn, axis=-1)
        attn = jnp.where(jnp.any(jnp.isnan(attn)), jnp.asarray(1.0 / Nkv, attn.dtype), attn)
        x = jnp.einsum('bhqk,bhkd->bqhd', attn, v).reshape(B, Nq, Cq)
        return x @ Wo + bo

    def _L0_ffn_ref(x, centroids, W1, b1, W2, b2):
        import jax, jax.numpy as jnp
        import numpy as np
        E = 8
        TOP_K = 2
        D = 512
        DFF = 4 * D
        b, s, d = x.shape
        u = x.reshape(b * s, d)
        n = u.shape[0]
        gates = jax.nn.sigmoid(u @ centroids.T)
        if TOP_K < E:
            topk_vals, topk_idx = jax.lax.top_k(gates, TOP_K)
            mask = jnp.zeros_like(gates).at[jnp.arange(n)[:, None], topk_idx].set(topk_vals)
            gates = mask / jnp.sum(mask, axis=-1, keepdims=True)
        h = jax.nn.gelu(jnp.einsum('nd,edf->enf', u, W1) + b1[:, None, :], approximate=False)
        outs = jnp.einsum('enf,efd->end', h, W2) + b2[:, None, :]
        out = jnp.einsum('ne,end->nd', gates, outs)
        return out.reshape(b, s, d)

    def _L1_attn_ref(x, weight_q, weight_k, weight_v, theta):
        import jax, jax.numpy as jnp
        import numpy as np
        GAMMA = 0.96875
        H = 512
        B = 4
        L = 1024
        Bb, Ll, Hh = x.shape
        dt = x.dtype
        seq = jnp.arange(1, Ll + 1, dtype=dt)
        zero = jnp.asarray(0.0, dtype=dt)
        thetas = jnp.exp(zero * seq[:, None] * theta[None, :])
        theta_conj = thetas
        q = jnp.matmul(x, weight_q) * thetas[None]
        k = jnp.matmul(x, weight_k) * theta_conj[None]
        v = jnp.matmul(x, weight_v)
        n = jnp.arange(Ll)
        diff = n[:, None] - n[None, :]
        D = jnp.where(diff >= 0, jnp.asarray(GAMMA, dt) ** diff.astype(dt), jnp.zeros((), dt))
        scores = jnp.einsum('bid,bjd->bij', q, k) * D[None]
        return jnp.einsum('bij,bjd->bid', scores, v)

    def _L1_xattn_ref(x, context, Wq, Wk, Wv, Wo, bo):
        import jax, jax.numpy as jnp
        import numpy as np
        HEADS = 16
        DIM_HEAD = 64
        SCALE = DIM_HEAD ** (-0.5)
        B, N, _ = x.shape
        M = context.shape[1]
        q = (x @ Wq).reshape(B, N, HEADS, DIM_HEAD).transpose(0, 2, 1, 3)
        k = (context @ Wk).reshape(B, M, HEADS, DIM_HEAD).transpose(0, 2, 1, 3)
        v = (context @ Wv).reshape(B, M, HEADS, DIM_HEAD).transpose(0, 2, 1, 3)
        dots = jnp.einsum('bhnd,bhmd->bhnm', q, k) * SCALE
        attn = jax.nn.softmax(dots, axis=-1)
        out = jnp.einsum('bhnm,bhmd->bhnd', attn, v)
        out = out.transpose(0, 2, 1, 3).reshape(B, N, HEADS * DIM_HEAD)
        return out @ Wo + bo

    def _L1_ffn_ref(x, qweights, scales, biases, lora_a, lora_b, ln_gamma, ln_beta):
        import jax, jax.numpy as jnp
        import numpy as np
        GROUP = 16
        EPS = 1e-05

        def _dequant(q, scale):
            w = q.astype(jnp.float32) / 7.5 - 1.0
            return w * jnp.repeat(scale, GROUP, axis=1)

        def _qlora_linear(x, q, scale, bias, la, lb):
            w = _dequant(q, scale)
            base = jnp.einsum('btd,od->bto', x, w) + bias
            lora = jnp.einsum('btr,or->bto', jnp.einsum('btd,rd->btr', x, la), lb)
            return base + lora

        def _layernorm(x, g, b):
            mu = jnp.mean(x, axis=-1, keepdims=True)
            var = jnp.mean(jnp.square(x - mu), axis=-1, keepdims=True)
            return (x - mu) * jax.lax.rsqrt(var + EPS) * g + b
        h = x
        for blk in range(3):
            i0, i1 = (2 * blk, 2 * blk + 1)
            y = _qlora_linear(h, qweights[i0], scales[i0], biases[i0], lora_a[i0], lora_b[i0])
            y = _layernorm(y, ln_gamma[blk], ln_beta[blk])
            y = jax.nn.gelu(y, approximate=False)
            y = _qlora_linear(y, qweights[i1], scales[i1], biases[i1], lora_a[i1], lora_b[i1])
            h = y + h
        return h
    x = x + _L0_attn_ref(_layernorm(x, axis=-1), L0_attn_time_decay, L0_attn_time_first, L0_attn_w_tk, L0_attn_w_tv, L0_attn_w_tr, L0_attn_w_ck, L0_attn_w_cv, L0_attn_w_cr, L0_attn_ln1_g, L0_attn_ln1_b, L0_attn_ln2_g, L0_attn_ln2_b, L0_attn_mix_k, L0_attn_mix_v, L0_attn_mix_r, L0_attn_cmix_k, L0_attn_cmix_r)
    x = x + _L0_xattn_ref(_layernorm(x, axis=-1), ctx_768, L0_xattn_Wq, L0_xattn_bq, L0_xattn_Wk, L0_xattn_bk, L0_xattn_Wv, L0_xattn_bv, L0_xattn_Wo, L0_xattn_bo)
    x = x + _L0_ffn_ref(_layernorm(x, axis=-1), L0_ffn_centroids, L0_ffn_W1, L0_ffn_b1, L0_ffn_W2, L0_ffn_b2)
    x = x + _L1_attn_ref(_layernorm(x, axis=-1), L1_attn_weight_q, L1_attn_weight_k, L1_attn_weight_v, L1_attn_theta)
    x = x + _L1_xattn_ref(_layernorm(x, axis=-1), ctx_768, L1_xattn_Wq, L1_xattn_Wk, L1_xattn_Wv, L1_xattn_Wo, L1_xattn_bo)
    x = x + _L1_ffn_ref(_layernorm(x, axis=-1), L1_ffn_qweights, L1_ffn_scales, L1_ffn_biases, L1_ffn_lora_a, L1_ffn_lora_b, L1_ffn_ln_gamma, L1_ffn_ln_beta)
    return x

_drawn_inputs = setup_inputs


def setup_inputs(seed=0):
    import zlib

    import numpy as np

    out = dict(_drawn_inputs(seed))
    spreads = {'L0_attn_ln1_g': (1.0, 0.2),
     'L0_attn_ln1_b': (0.0, 0.1),
     'L0_attn_ln2_g': (1.0, 0.2),
     'L0_attn_ln2_b': (0.0, 0.443),
     'L0_attn_mix_k': (1.0, 0.2),
     'L0_attn_mix_v': (1.0, 0.2),
     'L0_attn_mix_r': (1.0, 0.2),
     'L0_attn_cmix_k': (1.0, 0.2),
     'L0_attn_cmix_r': (1.0, 0.6),
     'L0_xattn_bq': (0.0, 0.279),
     'L0_xattn_bk': (0.0, 2.0),
     'L0_xattn_bv': (0.0, 0.1),
     'L0_xattn_bo': (0.0, 0.1),
     'L1_xattn_bo': (0.0, 0.345),
     'L1_ffn_ln_gamma': (1.0, 0.2),
     'L1_ffn_ln_beta': (0.0, 0.1)}
    factors = {'L0_attn_time_first': 49.65,
     'L0_ffn_b1': 8.0,
     'L0_ffn_b2': 8.0,
     'L1_attn_weight_q': 8.0,
     'L1_attn_weight_k': 8.0,
     'L1_attn_weight_v': 8.0,
     'L1_ffn_biases': 8.0,
     'L1_ffn_lora_a': 4.751,
     'L1_ffn_lora_b': 4.678}
    for name, (base, spread) in spreads.items():
        noise = np.random.default_rng([zlib.crc32(name.encode()), seed]).standard_normal(out[name].shape)
        drawn = base * np.exp(spread * noise) if base else spread * noise
        out[name] = jnp.asarray(drawn.astype(out[name].dtype))
    for name, factor in factors.items():
        out[name] = (out[name] * factor).astype(out[name].dtype)
    return out
```

```python
from contextlib import ExitStack

import concourse.bass as bass
from concourse import mybir
from concourse.alu_op_type import AluOpType as ALU

F32 = mybir.dt.float32
I32 = mybir.dt.int32
ACT = mybir.ActivationFunctionType
AX = mybir.AxisListType

P = 128
B, S, C = 8, 100, 512
T = B * S
KC = C // P
HT = T // 2
NKV, CKV = 722, 384
KX = CKV // P
HKV = NKV // 2
KVC = -(-NKV // P)
KVR = NKV - (KVC - 1) * P
HEADS = 16
FF = 4 * C
E = 8
RING = 8
BANK = 512
EPS = 1e-5
NEG_INF = -1e38
CLAMP = 1e4

PARAMS = [("time_decay", KC), ("time_first", KC), ("ln1_g", KC), ("ln1_b", KC), ("ln2_g", KC), ("ln2_b", KC),
          ("mix_k", KC), ("mix_v", KC), ("mix_r", KC), ("cmix_k", KC), ("cmix_r", KC),
          ("bq", KC), ("bk", KC), ("bv", KC), ("bo", KC), ("theta", KC), ("xbo", KC),
          ("b1", E * FF // P), ("qbias", 6 * KC), ("gamma", 3 * KC), ("beta", 3 * KC)]
COL, _n = {}, 0
for _name, _w in PARAMS:
    COL[_name] = _n
    _n += _w
N_PARAMS = _n


class Signal:

    def __init__(self, ctx, nc, name):
        self.sem = ctx.enter_context(nc.semaphore(name))
        self.base = 0

    def advance(self, n):
        self.base += n


class Decoder:

    def __init__(self, nc, ctx, d):
        self.nc, self.d = nc, d
        self.ps = ctx.enter_context(nc.psum_tensor("ps", [P, 8, BANK], F32))
        self.x = ctx.enter_context(nc.sbuf_tensor("x", [P, KC, T], F32))
        self.ring = ctx.enter_context(nc.sbuf_tensor("ring", [P, RING, KC, C], F32))
        self.par = ctx.enter_context(nc.sbuf_tensor("par", [P, N_PARAMS], F32))
        self.mean_w = ctx.enter_context(nc.sbuf_tensor("mean_w", [P, P], F32))
        self.eps = ctx.enter_context(nc.sbuf_tensor("eps", [P, 1], F32))
        self.ident = ctx.enter_context(nc.sbuf_tensor("ident", [P, P], F32))
        names = ("param_load x_load const_load ctx_load store mm act_out dve_out dve_chain ln_cen ln_sq ln_std b1_copy"
                 " k_out v_out q_copy s_mm s_clip s_max p_exp p_norm p_turn pt_out o_mm o_out act_hid hid_out y_out"
                 " qa_out w_scale setup").split()
        self.sig = {n: Signal(ctx, nc, n) for n in names}
        self.block_load = [Signal(ctx, nc, f"block_load{i}") for i in range(RING)]
        self.blocks = []
        self.loaded = 0
        self.used = 0
        self.free_at = []

    def column(self, name, i):
        c = COL[name] + i
        return self.par[:, c:c + 1]


    def add_block(self, source, kc=KC, dtype=F32):
        self.blocks.append((source, kc, dtype))

    def slot(self, w):
        return self.ring[:, w % RING]

    def wait_block(self, eng, w):
        eng.wait_ge(self.block_load[w % RING].sem, 16 * (w // RING + 1))

    def load_blocks(self, sp, until):
        until = min(until, len(self.blocks))
        while self.loaded < until:
            w = self.loaded
            source, kc, dtype = self.blocks[w]
            if w >= RING and self.free_at[w - RING] is not None:
                sp.wait_ge(self.sig["mm"].sem, self.free_at[w - RING])
            dst = self.slot(w)[:, 0:kc, :]
            if dtype != F32:
                dst = dst.bitcast(dtype)
            sp.dma_start(dst, source).then_inc(self.block_load[w % RING].sem, 16)
            self.loaded += 1


def rows(w, r0, c0, kc=KC, cols=C):
    return w[r0:r0 + kc * P, c0:c0 + cols].rearrange("(k p) n -> p k n", p=P)


def halves(n):
    return slice(n * HT, (n + 1) * HT)


def mlp_order():
    return [(0, 0), (0, 1), (1, 0), (0, 2), (1, 1), (0, 3), (1, 2), (1, 3)]


def layer_norm(m, src, dst, tmp, std, gain=None, bias=None, func=None, gi=0):
    nc, ps, g = m.nc, m.ps, m.sig
    mm, cen, sq, sd, out, ch = g["mm"], g["ln_cen"], g["ln_sq"], g["ln_std"], g["dve_out"], g["dve_chain"]
    with nc.Block() as block:

        @block.tensor
        def _(pe):
            for n in range(2):
                for k in range(KC):
                    last = pe.matmul(ps[:, n, 0:HT], m.mean_w[:, :], src[:, k, halves(n)], start=k == 0, stop=k == KC - 1)
                last.then_inc(mm.sem, 1)
            for n in range(2):
                pe.wait_ge(sq.sem, sq.base + n + 1)
                for k in range(KC):
                    last = pe.matmul(ps[:, 2 + n, 0:HT], m.mean_w[:, :], tmp[:, k, halves(n)], start=k == 0, stop=k == KC - 1)
                last.then_inc(mm.sem, 1)

        @block.vector
        def _(dve):
            for n in range(2):
                dve.wait_ge(mm.sem, mm.base + n + 1)
                dve.tensor_tensor(dst[:, :, halves(n)], src[:, :, halves(n)],
                                  ps[:, n, 0:HT].unsqueeze(1).to_broadcast([P, KC, HT]), ALU.subtract).then_inc(cen.sem, 1)
            for n in range(2):
                dve.wait_ge(sd.sem, sd.base + n + 1)
                dve.reciprocal(std[:, halves(n)], std[:, halves(n)]).then_inc(ch.sem, 1)
                dve.wait_ge(ch.sem, ch.base + n + 1)
                dve.tensor_tensor(dst[:, :, halves(n)], dst[:, :, halves(n)],
                                  std[:, halves(n)].unsqueeze(1).to_broadcast([P, KC, HT]), ALU.mult).then_inc(out.sem, 1)

        @block.scalar
        def _(act):
            for n in range(2):
                act.wait_ge(cen.sem, cen.base + n + 1)
                act.activation(tmp[:, :, halves(n)], dst[:, :, halves(n)], ACT.Square).then_inc(sq.sem, 1)
            for n in range(2):
                act.wait_ge(mm.sem, mm.base + n + 3)
                act.activation(std[:, halves(n)], ps[:, 2 + n, 0:HT], ACT.Sqrt, bias=m.eps[:, 0:1]).then_inc(sd.sem, 1)
            if gain is not None:
                for n in range(2):
                    act.wait_ge(out.sem, out.base + n + 1)
                    for k in range(KC):
                        act.activation(dst[:, k, halves(n)], dst[:, k, halves(n)], func or ACT.Identity,
                                       scale=m.column(gain, gi + k), bias=m.column(bias, gi + k))

    for s, n in ((mm, 4), (cen, 2), (sq, 2), (sd, 2), (out, 2), (ch, 2)):
        s.advance(n)


def linear(m, src, blocks, evac, engine="scalar", prep=None):
    nc, ps, mm = m.nc, m.ps, m.sig["mm"]
    done = m.sig["act_out"] if engine == "scalar" else m.sig["dve_out"]
    groups = [(i, c, n) for i in range(len(blocks)) for c in range(KC) for n in range(2)]
    last_used = {}
    for i, parts in enumerate(blocks):
        for w, _ in parts:
            last_used[w] = mm.base + 2 * KC * (i + 1)
    for w in sorted(last_used):
        assert w == len(m.free_at)
        m.free_at.append(last_used[w])
    m.used = len(m.free_at)
    with nc.Block() as block:

        @block.sync
        def _(sp):
            m.load_blocks(sp, m.used + RING)

        @block.tensor
        def _(pe):
            for j, (i, c, n) in enumerate(groups):
                if c == 0 and n == 0:
                    for w, _ in blocks[i]:
                        m.wait_block(pe, w)
                if j >= 8:
                    pe.wait_ge(done.sem, done.base + j - 7)
                terms = [(w, k, src[s0 + k]) for w, s0 in blocks[i] for k in range(KC)]
                for t, (w, k, s) in enumerate(terms):
                    last = pe.matmul(ps[:, j % 8, 0:HT], m.slot(w)[:, k, c * P:(c + 1) * P], s[:, halves(n)],
                                     start=t == 0, stop=t == len(terms) - 1)
                last.then_inc(mm.sem, 1)

        def drain(eng):
            if prep is not None:
                prep(eng)
            for j, (i, c, n) in enumerate(groups):
                eng.wait_ge(mm.sem, mm.base + j + 1)
                evac(eng, i * KC + c, n, ps[:, j % 8, 0:HT]).then_inc(done.sem, 1)

        if engine == "scalar":
            block.scalar(drain)
        else:
            block.vector(drain)
    mm.advance(len(groups))
    done.advance(len(groups))


def chunks(t, n=KC):
    return [t[:, k, :] for k in range(n)]


def shift_mix(m, h, mixes, keep):
    nc, tok = m.nc, m.sig["act_out"]
    ch = m.sig["dve_chain"]
    with nc.Block() as block:

        @block.scalar
        def _(act):
            for name, dst in mixes:
                for k in range(KC):
                    act.activation(dst[:, k, :], h[:, k, :], ACT.Identity, scale=m.column(name, k)).then_inc(tok.sem, 1)

        @block.vector
        def _(dve):
            for i, (name, dst) in enumerate(mixes):
                c = COL[name]
                dve.tensor_scalar(keep[:, i * KC:(i + 1) * KC], m.par[:, c:c + KC], -1.0, 1.0, ALU.mult, ALU.add).then_inc(ch.sem, 1)
            dve.wait_ge(ch.sem, ch.base + len(mixes))
            for i, (name, dst) in enumerate(mixes):
                for k in range(KC):
                    dve.wait_ge(tok.sem, tok.base + i * KC + k + 1)
                    to = dst[:, k, :].rearrange("p (b s) -> p b s", s=S)
                    of = h[:, k, :].rearrange("p (b s) -> p b s", s=S)
                    dve.scalar_tensor_tensor(to[:, :, 1:S], of[:, :, 0:S - 1], keep[:, i * KC + k:i * KC + k + 1],
                                             to[:, :, 1:S], ALU.mult, ALU.add)

    tok.advance(KC * len(mixes))
    ch.advance(len(mixes))


def wkv(m, k_, v_, r_, xl, sb):
    nc, dv, ac = m.nc, m.sig["dve_chain"], m.sig["act_out"]
    mx, qq, aa = (sb(n, [P, KC, B, S + 1], F32) for n in ("wkv_m", "wkv_q", "wkv_a"))
    t1, t2 = (sb(n, [P, KC, B, S], F32) for n in ("wkv_t1", "wkv_t2"))
    t3 = qq[:, :, :, 1:]

    def bs(t, c):
        return t[:, c, :].rearrange("p (b s) -> p b s", s=S)

    with nc.Block() as block:

        @block.vector
        def _(dve):
            n = 0

            def out(ins):
                nonlocal n
                n += 1
                ins.then_inc(dv.sem, 1)

            def own():
                dve.wait_ge(dv.sem, dv.base + n)

            def after_act(count):
                dve.wait_ge(ac.sem, ac.base + count)

            out(dve.memset(mx[:, :, :, 0:1], NEG_INF))
            out(dve.memset(qq[:, :, :, 0:1], 1.0))
            out(dve.memset(aa[:, :, :, 0:1], 0.0))
            own()
            for c in range(KC):
                for b in range(B):
                    out(dve.tensor_tensor_scan(mx[:, c, b, 1:], k_[:, c, b * S:(b + 1) * S],
                                               m.column("time_decay", c).to_broadcast([P, S]), NEG_INF, ALU.max, ALU.add))
            own()
            for c in range(KC):
                out(dve.tensor_tensor(t1[:, c], mx[:, c, :, 0:S], mx[:, c, :, 1:], ALU.subtract))
                out(dve.tensor_tensor(t2[:, c], bs(k_, c), mx[:, c, :, 1:], ALU.subtract))
            for c in range(KC):
                after_act(2 * c + 2)
                for b in range(B):
                    out(dve.tensor_tensor_scan(qq[:, c, b, 1:], t1[:, c, b, :], t2[:, c, b, :], 1.0, ALU.mult, ALU.add))
            for c in range(KC):
                after_act(2 * KC + c + 1)
                out(dve.tensor_tensor(mx[:, c], mx[:, c], qq[:, c], ALU.add))
            own()
            for c in range(KC):
                out(dve.tensor_tensor(t3[:, c], mx[:, c, :, 0:S], bs(k_, c), ALU.max))
            own()
            for c in range(KC):
                out(dve.tensor_tensor(t1[:, c], mx[:, c, :, 0:S], t3[:, c], ALU.subtract))
                out(dve.tensor_tensor(t2[:, c], bs(k_, c), t3[:, c], ALU.subtract))
            for c in range(KC):
                after_act(3 * KC + 2 * c + 2)
                out(dve.tensor_tensor(t2[:, c], t2[:, c], bs(v_, c), ALU.mult))
            own()
            for c in range(KC):
                for b in range(B):
                    out(dve.tensor_tensor_scan(aa[:, c, b, 1:], t1[:, c, b, :], t2[:, c, b, :], 0.0, ALU.mult, ALU.add))
            for c in range(KC):
                out(dve.tensor_scalar(k_[:, c, :], k_[:, c, :], m.column("time_first", c), None, ALU.add))
            own()
            for c in range(KC):
                out(dve.tensor_tensor(t3[:, c], mx[:, c, :, 0:S], bs(k_, c), ALU.max))
            own()
            for c in range(KC):
                out(dve.tensor_tensor(t1[:, c], mx[:, c, :, 0:S], t3[:, c], ALU.subtract))
                out(dve.tensor_tensor(t2[:, c], bs(k_, c), t3[:, c], ALU.subtract))
            for c in range(KC):
                after_act(5 * KC + 2 * c + 2)
                out(dve.tensor_tensor(t3[:, c], t1[:, c], t2[:, c], ALU.add))
            own()
            for c in range(KC):
                out(dve.reciprocal(t3[:, c], t3[:, c]))
                out(dve.tensor_tensor(t1[:, c], t1[:, c], aa[:, c, :, 0:S], ALU.mult))
                out(dve.tensor_tensor(t2[:, c], t2[:, c], bs(v_, c), ALU.mult))
            own()
            for c in range(KC):
                out(dve.tensor_tensor(t1[:, c], t1[:, c], t2[:, c], ALU.add))
                out(dve.tensor_tensor(t3[:, c], t3[:, c], bs(r_, c), ALU.mult))
            own()
            for c in range(KC):
                out(dve.tensor_tensor(t1[:, c], t1[:, c], t3[:, c], ALU.mult))
            own()
            for c in range(KC):
                out(dve.tensor_tensor(bs(xl, c), bs(xl, c), t1[:, c], ALU.add))
            wkv.dve_count = n

        @block.scalar
        def _(act):
            scans = B * KC
            d1 = dv.base + 3 + scans
            for c in range(KC):
                for i, t in enumerate((t1, t2)):
                    act.wait_ge(dv.sem, d1 + 2 * c + i + 1)
                    act.activation(t[:, c], t[:, c], ACT.Exp, bias=m.column("time_decay", c)).then_inc(ac.sem, 1)
            d2 = d1 + 2 * KC
            for c in range(KC):
                act.wait_ge(dv.sem, d2 + B * (c + 1))
                act.activation(qq[:, c], qq[:, c], ACT.Ln).then_inc(ac.sem, 1)
            d3 = d2 + scans + 2 * KC
            for c in range(KC):
                for i, t in enumerate((t1, t2)):
                    act.wait_ge(dv.sem, d3 + 2 * c + i + 1)
                    act.activation(t[:, c], t[:, c], ACT.Exp).then_inc(ac.sem, 1)
            d4 = d3 + 2 * KC + KC + scans + 2 * KC
            for c in range(KC):
                for i, t in enumerate((t1, t2)):
                    act.wait_ge(dv.sem, d4 + 2 * c + i + 1)
                    act.activation(t[:, c], t[:, c], ACT.Exp).then_inc(ac.sem, 1)

    dv.advance(wkv.dve_count)
    ac.advance(7 * KC)


def mlp(m, src, y, hid, experts, gate=None, b1=None, clear=True):
    nc, ps = m.nc, m.ps
    mm, ah, ho, yo, ch = (m.sig[s] for s in ("mm", "act_hid", "hid_out", "y_out", "dve_chain"))
    bc = m.sig["b1_copy"]
    order = mlp_order()
    G = 2 * KC
    per = len(order) * G
    half = per // 2
    w0 = m.used
    assert w0 % RING == 0 or experts == 1

    def spans(block):
        kinds = [k for k, _ in order[:block]]
        return block * G, kinds.count(order[block][0]) * G

    for e in range(experts):
        for i in range(len(order)):
            m.free_at.append(mm.base + e * per + (i + 1) * G)
    m.used = len(m.free_at)

    def run(eng, body):
        if experts == 1:
            body(0)
        else:
            with eng.Fori(0, experts) as e:
                body(e)

    with nc.Block() as block:

        @block.sync
        def _(sp):
            if experts > 1:
                assert m.loaded == w0 + RING
                with sp.Fori(0, experts - 1) as e:
                    for i, (second, j) in enumerate(order):
                        sp.wait_ge(mm.sem, mm.base + e * per + (i + 1) * G)
                        w = m.d["W2"] if second else m.d["W1"]
                        part = w[e + 1, j * C:(j + 1) * C, :] if second else w[e + 1, :, j * C:(j + 1) * C]
                        sp.dma_start(m.slot(w0 + i), part.rearrange("(k p) n -> p k n", p=P)).then_inc(m.block_load[i].sem, 16)
                m.loaded += RING * (experts - 1)
            m.load_blocks(sp, m.used + RING)

        @block.tensor
        def _(pe):
            def body(e):
                for i, (second, j) in enumerate(order):
                    pe.wait_ge(m.block_load[(w0 + i) % RING].sem, 16 * ((w0 + i) // RING + 1) + e * 16)
                    done, of_kind = spans(i)
                    for g in range(G):
                        c, n = divmod(g, 2)
                        if second:
                            bank = 4 + (of_kind + g) % 4
                            if g == 0:
                                pe.wait_ge(ho.sem, ho.base + e * half + (j + 1) * G)
                            free = of_kind + g - 3
                            if free > 0 or experts > 1:
                                pe.wait_ge(yo.sem, yo.base + e * half + free if free > 0 else _last(yo.base, e, half, free))
                        else:
                            bank = (of_kind + g) % 4
                            free = of_kind + g - 3
                            if free > 0 or experts > 1:
                                pe.wait_ge(ah.sem, ah.base + e * half + free if free > 0 else _last(ah.base, e, half, free))
                        for k in range(KC):
                            rhs = hid[:, j % 2, k, halves(n)] if second else src[:, k, halves(n)]
                            last = pe.matmul(ps[:, bank, 0:HT], m.slot(w0 + i)[:, k, c * P:(c + 1) * P], rhs,
                                             start=k == 0, stop=k == KC - 1)
                        last.then_inc(mm.sem, 1)
            run(pe, body)

        @block.scalar
        def _(act):
            def body(e):
                if gate is not None:
                    act.wait_ge(bc.sem, bc.base + e + 1)
                for i, (second, j) in enumerate(order):
                    if second:
                        continue
                    done, of_kind = spans(i)
                    if j >= 2:
                        act.wait_ge(mm.sem, mm.base + e * per + (order.index((1, j - 2)) + 1) * G)
                    for g in range(G):
                        c, n = divmod(g, 2)
                        act.wait_ge(mm.sem, mm.base + e * per + done + g + 1)
                        to = hid[:, j % 2, c, halves(n)]
                        pin = ps[:, (of_kind + g) % 4, 0:HT]
                        if gate is None:
                            ins = act.activation(to, pin, ACT.Relu)
                        else:
                            ins = act.activation(to, pin, ACT.Gelu, bias=b1[:, j * KC + c:j * KC + c + 1])
                        ins.then_inc(ah.sem, 1)
            run(act, body)

        @block.vector
        def _(dve):
            if clear:
                dve.memset(y[:, :, :], 0.0).then_inc(ch.sem, 1)
                dve.wait_ge(ch.sem, ch.base + 1)

            def copy_b1(e):
                at = COL["b1"] + e * (FF // P)
                dve.tensor_scalar(b1[:, :], m.par[:, bass.ds(at, FF // P)], 1.0, None, ALU.mult).then_inc(bc.sem, 1)

            if gate is not None:
                copy_b1(0)

            def body(e):
                for i, (second, j) in enumerate(order):
                    done, of_kind = spans(i)
                    if gate is not None and (second, j) == (1, 2):
                        dve.wait_ge(ah.sem, ah.base + e * half + half)
                        copy_b1(e + 1)
                    for g in range(G):
                        c, n = divmod(g, 2)
                        if second:
                            dve.wait_ge(mm.sem, mm.base + e * per + done + g + 1)
                            if of_kind + g >= 2 * KC or experts > 1:
                                back = of_kind + g - 2 * KC + 1
                                dve.wait_ge(yo.sem, yo.base + e * half + back if back > 0 else _last(yo.base, e, half, back))
                            yy = y[:, c, halves(n)]
                            dve.tensor_tensor(yy, ps[:, 4 + (of_kind + g) % 4, 0:HT], yy, ALU.add).then_inc(yo.sem, 1)
                        else:
                            dve.wait_ge(ah.sem, ah.base + e * half + of_kind + g + 1)
                            hh = hid[:, j % 2, c, halves(n)]
                            by = hh if gate is None else gate[:, bass.ds(n * HT + e * T, HT)]
                            dve.tensor_tensor(hh, hh, by, ALU.mult).then_inc(ho.sem, 1)
            run(dve, body)

    bc.advance(experts + 1 if gate is not None else 0)
    mm.advance(experts * per)
    ah.advance(experts * half)
    ho.advance(experts * half)
    yo.advance(experts * half)
    ch.advance(1 if clear else 0)


def _last(base, e, per, back):
    assert base + back >= 0, "the stage before has to have signalled as often"
    return base + back + e * per


def attention(m, q, o, layer, sb):
    nc, ps = m.nc, m.ps
    D = 32 if layer == 0 else 64
    NC_ = HEADS * D // P
    HPC = P // D
    VB = HEADS * D // C
    wk = [m.used + i for i in range(VB)]
    wv = [m.used + VB + i for i in range(VB)]
    for _ in range(2 * VB):
        m.free_at.append(None)
    m.used = len(m.free_at)
    NP_ = 3
    ctx_t = sb(f"ctx{layer}", [P, KX, NKV], F32)
    kt = sb(f"kt{layer}", [P, NC_, NKV], F32)
    vv = sb(f"vv{layer}", [P, KVC, HEADS * D], F32)
    qb = sb(f"qb{layer}", [P, NC_, S], F32)
    pr = sb(f"pr{layer}", [S, NP_, KVC * P], F32)
    pt = sb(f"pt{layer}", [P, 2, KVC, S], F32)
    smax = sb(f"smax{layer}", [S, 2, 4], F32)
    ssum = sb(f"ssum{layer}", [S, NP_], F32)
    sg = m.sig
    mm = sg["mm"]
    KG, VG = 2 * NC_, KVC * VB
    LAG_T, LAG_O = 2, 3
    PROJ = KG + VG

    def s_banks(h):
        return ps[0:S, 2 * (h % 2):2 * (h % 2) + 2, 0:HKV]

    def proj_bank(i):
        return i % 4

    with nc.Block() as block:

        @block.sync
        def _(sp):
            m.load_blocks(sp, m.used - 2 * VB + RING)
            with sp.Fori(0, B) as b:
                sp.wait_ge(mm.sem, mm.base + b * PROJ)
                sp.dma_start(ctx_t[:, :, :], m.d["ctx"][b]).then_inc(sg["ctx_load"].sem, 16)

        @block.tensor
        def _(pe):
            for w in wk + wv:
                m.wait_block(pe, w)
            with pe.Fori(0, B) as b:
                pe.wait_ge(sg["ctx_load"].sem, sg["ctx_load"].base + b * 16 + 16)
                pe.wait_ge(sg["p_exp"].sem, sg["p_exp"].base + b * HEADS)
                for i in range(PROJ):
                    if i >= 4:
                        if i - 4 < KG:
                            pe.wait_ge(sg["k_out"].sem, sg["k_out"].base + b * KG + i - 3)
                        else:
                            pe.wait_ge(sg["v_out"].sem, sg["v_out"].base + b * VG + i - 3 - KG)
                    if i < KG:
                        c, n = divmod(i, 2)
                        for k in range(KX):
                            last = pe.matmul(ps[:, proj_bank(i), 0:HKV],
                                             m.slot(wk[c // KC])[:, k, (c % KC) * P:(c % KC + 1) * P],
                                             ctx_t[:, k, n * HKV:(n + 1) * HKV], start=k == 0, stop=k == KX - 1)
                    else:
                        c, n = divmod(i - KG, VB)
                        r = P if c < KVC - 1 else KVR
                        for k in range(KX):
                            last = pe.matmul(ps[0:r, proj_bank(i), 0:C], ctx_t[:, k, c * P:c * P + r],
                                             m.slot(wv[n])[:, k, :], start=k == 0, stop=k == KX - 1)
                    last.then_inc(mm.sem, 1)
                pe.wait_ge(sg["k_out"].sem, sg["k_out"].base + b * KG + KG)
                pe.wait_ge(sg["v_out"].sem, sg["v_out"].base + b * VG + VG)
                pe.wait_ge(sg["q_copy"].sem, sg["q_copy"].base + b + 1)
                for i in range(HEADS + LAG_O):
                    if i < HEADS:
                        c, r = i // HPC, (i % HPC) * D
                        if i >= 2:
                            pe.wait_ge(sg["p_exp"].sem, sg["p_exp"].base + b * HEADS + i - 1)
                        for n in range(2):
                            last = pe.matmul(ps[0:S, 2 * (i % 2) + n, 0:HKV], qb[r:r + D, c, :],
                                             kt[r:r + D, c, n * HKV:(n + 1) * HKV], start=True, stop=True)
                        last.then_inc(sg["s_mm"].sem, 1)
                    h = i - LAG_T
                    if 0 <= h < HEADS:
                        pe.wait_ge(sg["p_norm"].sem, sg["p_norm"].base + b * HEADS + h + 1)
                        pe.wait_ge(sg["pt_out"].sem, sg["pt_out"].base + b * HEADS + h)
                        for c in range(KVC):
                            last = pe.transpose(ps[:, 4 + c // 3, (c % 3) * S:(c % 3 + 1) * S],
                                                pr[:, h % NP_, c * P:(c + 1) * P], m.ident[0:S, 0:S])
                        last.then_inc(sg["p_turn"].sem, 1)
                    h = i - LAG_O
                    if 0 <= h < HEADS:
                        c, r = h // HPC, (h % HPC) * D
                        pe.wait_ge(sg["pt_out"].sem, sg["pt_out"].base + b * HEADS + h + 1)
                        if h % HPC == 0:
                            if c >= 2:
                                pe.wait_ge(sg["o_out"].sem, sg["o_out"].base + b * NC_ + c - 1)
                            else:
                                pe.wait_ge(sg["o_out"].sem, sg["o_out"].base + b * NC_)
                        for k in range(KVC):
                            last = pe.matmul(ps[r:r + D, 6 + c % 2, 0:S], vv[:, k, h * D:(h + 1) * D],
                                             pt[:, h % 2, k, :], start=k == 0, stop=k == KVC - 1)
                        last.then_inc(sg["o_mm"].sem, 1)

        @block.scalar
        def _(act):
            with act.Fori(0, B) as b:
                for i in range(KG):
                    c, n = divmod(i, 2)
                    act.wait_ge(mm.sem, mm.base + b * PROJ + i + 1)
                    if layer == 0:
                        ins = act.activation(kt[:, c, n * HKV:(n + 1) * HKV], ps[:, proj_bank(i), 0:HKV], ACT.Identity,
                                             bias=m.column("bk", c))
                    else:
                        ins = act.activation(kt[:, c, n * HKV:(n + 1) * HKV], ps[:, proj_bank(i), 0:HKV], ACT.Copy)
                    ins.then_inc(sg["k_out"].sem, 1)
                for i in range(HEADS + LAG_T):
                    if i < HEADS:
                        act.wait_ge(sg["s_max"].sem, sg["s_max"].base + b * HEADS + i + 1)
                        if i >= NP_:
                            act.wait_ge(sg["p_turn"].sem, sg["p_turn"].base + b * HEADS + i - NP_ + 1)
                        to = pr[:, i % NP_, 0:NKV].rearrange("s (n k) -> s n k", n=2)
                        fr = to if layer == 0 else s_banks(i)
                        act.activation(to, fr, ACT.Exp, bias=smax[:, i % 2, 1:2],
                                       accum_out=ssum[:, i % NP_:i % NP_ + 1]).then_inc(sg["p_exp"].sem, 1)
                    h = i - LAG_T
                    if 0 <= h < HEADS:
                        act.wait_ge(sg["p_turn"].sem, sg["p_turn"].base + b * HEADS + h + 1)
                        if h >= 2:
                            act.wait_ge(sg["o_mm"].sem, sg["o_mm"].base + b * HEADS + h - 1)
                        act.activation(pt[:, h % 2].rearrange("p (n k) s -> p n (k s)", n=2), ps[:, 4:6, 0:3 * S],
                                       ACT.Copy).then_inc(sg["pt_out"].sem, 1)

        @block.vector
        def _(dve):
            ch = sg["dve_chain"]
            dve.memset(pr[:, :, NKV:], 0.0).then_inc(ch.sem, 1)
            dve.memset(vv[:, KVC - 1, :], 0.0).then_inc(ch.sem, 1)
            dve.wait_ge(ch.sem, ch.base + 2)
            with dve.Fori(0, B) as b:
                dve.wait_ge(sg["s_mm"].sem, sg["s_mm"].base + b * HEADS)
                dve.tensor_copy(qb[:, :, :], q[:, :, bass.ds(b * S, S)]).then_inc(sg["q_copy"].sem, 1)
                for i in range(VG):
                    c, n = divmod(i, VB)
                    r = P if c < KVC - 1 else KVR
                    dve.wait_ge(mm.sem, mm.base + b * PROJ + KG + i + 1)
                    dve.tensor_copy(vv[0:r, c, n * C:(n + 1) * C], ps[0:r, proj_bank(KG + i), 0:C]).then_inc(sg["v_out"].sem, 1)

                def output(c):
                    dve.wait_ge(sg["o_mm"].sem, sg["o_mm"].base + b * HEADS + (c + 1) * HPC)
                    to = o[:, c, bass.ds(b * S, S)]
                    if layer == 0:
                        ins = dve.tensor_scalar(to, ps[:, 6 + c % 2, 0:S], m.column("bv", c), None, ALU.add)
                    else:
                        ins = dve.tensor_copy(to, ps[:, 6 + c % 2, 0:S])
                    ins.then_inc(sg["o_out"].sem, 1)

                for i in range(HEADS + 1):
                    if i < HEADS:
                        dve.wait_ge(sg["s_mm"].sem, sg["s_mm"].base + b * HEADS + i + 1)
                        t = smax[:, i % 2]
                        x_ = sg["s_clip"]
                        per = 3 if layer == 0 else 0
                        if layer == 0:
                            to = pr[:, i % NP_, 0:NKV].rearrange("s (n k) -> s n k", n=2)
                            if i >= NP_:
                                dve.wait_ge(sg["p_turn"].sem, sg["p_turn"].base + b * HEADS + i - NP_ + 1)
                            dve.tensor_scalar(to, s_banks(i), -CLAMP, None, ALU.max, ALU.max,
                                              accum_out=t[:, 0:1]).then_inc(x_.sem, 1)
                            dve.wait_ge(x_.sem, x_.base + (b * HEADS + i) * 2 + 1)
                            dve.tensor_scalar(pr[:, i % NP_, 0:NKV], pr[:, i % NP_, 0:NKV], CLAMP, None, ALU.min).then_inc(x_.sem, 1)
                            dve.wait_ge(x_.sem, x_.base + (b * HEADS + i) * 2 + 2)
                            dve.tensor_scalar(t[:, 1:2], t[:, 0:1], CLAMP, -1.0, ALU.min, ALU.mult).then_inc(sg["s_max"].sem, 1)
                        else:
                            dve.tensor_reduce(t[:, 1:2], s_banks(i), AX.XY, ALU.max, negate=True).then_inc(sg["s_max"].sem, 1)
                    h = i - 1
                    if 0 <= h < HEADS:
                        dve.wait_ge(sg["p_exp"].sem, sg["p_exp"].base + b * HEADS + h + 1)
                        s_ = ssum[:, h % NP_:h % NP_ + 1]
                        q_ = sg["qa_out"]
                        dve.reciprocal(s_, s_).then_inc(q_.sem, 1)
                        dve.wait_ge(q_.sem, q_.base + b * HEADS + h + 1)
                        dve.tensor_scalar(pr[:, h % NP_, 0:NKV], pr[:, h % NP_, 0:NKV], s_, None, ALU.mult).then_inc(sg["p_norm"].sem, 1)
                    done = i - 1 - LAG_O
                    if done >= 0 and (done + 1) % HPC == 0:
                        output(done // HPC)
                for c in range(max(0, (HEADS - LAG_O) // HPC), NC_):
                    output(c)

    mm.advance(B * PROJ)
    for s, n in (("ctx_load", 16 * B), ("k_out", B * KG), ("v_out", B * VG), ("q_copy", B), ("s_mm", B * HEADS),
                 ("s_clip", 2 * B * HEADS if layer == 0 else 0), ("s_max", B * HEADS), ("p_exp", B * HEADS),
                 ("p_norm", B * HEADS), ("qa_out", B * HEADS), ("p_turn", B * HEADS), ("pt_out", B * HEADS),
                 ("o_mm", B * HEADS), ("o_out", B * NC_), ("dve_chain", 2)):
        sg[s].advance(n)


def gates(m, u, gate, y, sb):
    nc, ps, g = m.nc, m.ps, m.sig
    mm, dv, ac = g["mm"], g["dve_chain"], g["act_out"]
    cen = sb("cen", [P, KC, E], F32)
    b2 = sb("b2", [E, C], F32)
    before = sb("before", [P, E, E], F32)
    pick = sb("pick", [E, E, P], F32)
    sc = sb("sc", [S, B, E], F32)
    cmp = sb("cmp", [S, B, E, E], F32)
    eq = sb("eq", [S, B, E, E], F32)
    rank = sb("rank", [S, B, E], F32)
    den = sb("den", [S, B], F32)
    gt = sb("gt", [E, T], F32)
    with nc.Block() as block:

        @block.sync
        def _(sp):
            ld = g["const_load"]
            sp.dma_start(cen[:, :, :], m.d["centroids"]).then_inc(ld.sem, 16)
            sp.dma_start(b2[:, :], m.d["b2"]).then_inc(ld.sem, 16)
            sp.dma_start(before[:, :, :], m.d["before"]).then_inc(ld.sem, 16)
            sp.dma_start(pick[:, :, :], m.d["pick"]).then_inc(ld.sem, 16)

        @block.tensor
        def _(pe):
            ld = g["const_load"]
            pe.wait_ge(ld.sem, ld.base + 64)
            for b in range(B):
                for k in range(KC):
                    last = pe.matmul(ps[0:S, 0, b * E:(b + 1) * E], u[:, k, b * S:(b + 1) * S], cen[:, k, :],
                                     start=k == 0, stop=k == KC - 1)
            last.then_inc(mm.sem, 1)
            pe.wait_ge(dv.sem, dv.base + 12)
            for b in range(B):
                last = pe.transpose(ps[0:E, 1 + b // 4, (b % 4) * S:(b % 4 + 1) * S], rank[:, b, :], m.ident[0:S, 0:S])
            last.then_inc(mm.sem, 1)
            pe.wait_ge(dv.sem, dv.base + 14)
            for j in range(2 * E):
                e, n = divmod(j, 2)
                if j >= 4:
                    pe.wait_ge(ac.sem, ac.base + 1 + j - 3)
                pe.matmul(ps[:, 3 + j % 4, 0:HT], pick[:, e, :], gt[:, halves(n)], start=True, stop=True).then_inc(mm.sem, 1)
            for j in range(2 * KC):
                c, n = divmod(j, 2)
                if j < 4:
                    pe.wait_ge(ac.sem, ac.base + 1 + 2 * E - 3 + j)
                else:
                    pe.wait_ge(dv.sem, dv.base + 14 + j - 3)
                pe.matmul(ps[:, 3 + j % 4, 0:HT], b2[:, c * P:(c + 1) * P], gt[:, halves(n)], start=True, stop=True).then_inc(mm.sem, 1)

        @block.scalar
        def _(act):
            act.wait_ge(mm.sem, mm.base + 1)
            act.activation(sc[:, :, :], ps[0:S, 0, 0:B * E].rearrange("s (b e) -> s b e", e=E), ACT.Exp, scale=-1.0).then_inc(ac.sem, 1)
            for j in range(2 * E):
                e, n = divmod(j, 2)
                act.wait_ge(mm.sem, mm.base + 3 + j)
                act.activation(gate[:, e * T + n * HT:e * T + (n + 1) * HT], ps[:, 3 + j % 4, 0:HT], ACT.Copy).then_inc(ac.sem, 1)

        @block.vector
        def _(dve):
            n = 0

            def step(ins):
                nonlocal n
                n += 1
                ins.then_inc(dv.sem, 1)
                dve.wait_ge(dv.sem, dv.base + n)

            dve.wait_ge(g["const_load"].sem, g["const_load"].base + 64)
            dve.wait_ge(ac.sem, ac.base + 1)
            step(dve.tensor_scalar(sc[:, :, :], sc[:, :, :], 1.0, None, ALU.add))
            step(dve.reciprocal(sc[:, :, :], sc[:, :, :]))
            for b in range(B):
                mine = sc[:, b, :].unsqueeze(2).to_broadcast([S, E, E])
                other = sc[:, b, :].unsqueeze(1).to_broadcast([S, E, E])
                dve.tensor_tensor(cmp[:, b], other, mine, ALU.is_gt)
                ins = dve.tensor_tensor(eq[:, b], other, mine, ALU.is_equal)
            step(ins)
            step(dve.tensor_tensor(eq[:, :, :, :], eq[:, :, :, :],
                                   before[0:S].unsqueeze(1).to_broadcast([S, B, E, E]), ALU.mult))
            step(dve.tensor_tensor(cmp[:, :, :, :], cmp[:, :, :, :], eq[:, :, :, :], ALU.add))
            step(dve.tensor_reduce(rank[:, :, :], cmp[:, :, :, :], AX.X, ALU.add))
            step(dve.tensor_scalar(rank[:, :, :], rank[:, :, :], 1.5, None, ALU.is_lt))
            step(dve.tensor_tensor(rank[:, :, :], rank[:, :, :], sc[:, :, :], ALU.mult))
            step(dve.tensor_reduce(den[:, :], rank[:, :, :], AX.X, ALU.add))
            step(dve.reciprocal(den[:, :], den[:, :]))
            step(dve.tensor_tensor(rank[:, :, :], rank[:, :, :], den[:, :].unsqueeze(2).to_broadcast([S, B, E]), ALU.mult))
            step(dve.engine_nop())
            dve.wait_ge(mm.sem, mm.base + 2)
            for i in range(2):
                dve.tensor_copy(gt[:, halves(i)], ps[0:E, 1 + i, 0:HT]).then_inc(dv.sem, 1)
            for j in range(2 * KC):
                c, i = divmod(j, 2)
                dve.wait_ge(mm.sem, mm.base + 3 + 2 * E + j)
                dve.tensor_copy(y[:, c, halves(i)], ps[:, 3 + j % 4, 0:HT]).then_inc(dv.sem, 1)

    mm.advance(2 + 2 * E + 2 * KC)
    ac.advance(1 + 2 * E)
    dv.advance(14 + 2 * KC)
    g["const_load"].advance(64)


def values(m, u, v, w):
    nc, ps, mm, done = m.nc, m.ps, m.sig["mm"], m.sig["act_out"]
    assert w == len(m.free_at)
    m.free_at.append(mm.base + B)
    m.used = len(m.free_at)
    with nc.Block() as block:

        @block.sync
        def _(sp):
            m.load_blocks(sp, m.used + RING)

        @block.tensor
        def _(pe):
            m.wait_block(pe, w)
            for b in range(B):
                for k in range(KC):
                    last = pe.matmul(ps[0:S, b, 0:C], u[:, k, b * S:(b + 1) * S], m.slot(w)[:, k, :],
                                     start=k == 0, stop=k == KC - 1)
                last.then_inc(mm.sem, 1)

        @block.scalar
        def _(act):
            for b in range(B):
                act.wait_ge(mm.sem, mm.base + b + 1)
                act.activation(v[:, b, :], ps[0:S, b, 0:C], ACT.Copy).then_inc(done.sem, 1)

    mm.advance(B)
    done.advance(B)


def retention(m, q, k_, v, st, decay):
    nc, ps, mm, dv = m.nc, m.ps, m.sig["mm"], m.sig["dve_out"]
    x = m.x
    with nc.Block() as block:

        @block.tensor
        def _(pe):
            for b in range(B):
                for k in range(KC):
                    last = pe.matmul(ps[0:S, b // 4, (b % 4) * S:(b % 4 + 1) * S], k_[:, k, b * S:(b + 1) * S],
                                     q[:, k, b * S:(b + 1) * S], start=k == 0, stop=k == KC - 1)
                last.then_inc(mm.sem, 1)
            for b in range(B):
                pe.wait_ge(dv.sem, dv.base + 1 + b // 4)
                if b >= 4:
                    pe.wait_ge(dv.sem, dv.base + 2 + b - 3)
                for c in range(KC):
                    last = pe.matmul(ps[:, 4 + b % 4, c * S:(c + 1) * S], v[:, b, c * P:(c + 1) * P], st[:, b, :],
                                     start=True, stop=True)
                last.then_inc(mm.sem, 1)

        @block.vector
        def _(dve):
            for n in range(2):
                dve.wait_ge(mm.sem, mm.base + 4 * (n + 1))
                dve.tensor_tensor(st[:, 4 * n:4 * n + 4, :], ps[0:S, n, 0:HT].rearrange("s (b t) -> s b t", t=S),
                                  decay[:, :].unsqueeze(1).to_broadcast([S, 4, S]), ALU.mult).then_inc(dv.sem, 1)
            for b in range(B):
                dve.wait_ge(mm.sem, mm.base + B + b + 1)
                xb = x[:, :, b * S:(b + 1) * S]
                dve.tensor_tensor(xb, ps[:, 4 + b % 4, 0:HT].rearrange("p (c t) -> p c t", t=S), xb, ALU.add).then_inc(dv.sem, 1)

    mm.advance(2 * B)
    dv.advance(2 + B)


def dequantise(m, i, raw, w, sc, la, lb):
    nc, ps, mm, dv = m.nc, m.ps, m.sig["mm"], m.sig["dve_chain"]
    ld = m.sig["const_load"]
    assert raw == len(m.free_at)
    m.free_at.append(None)
    m.used = len(m.free_at)
    with nc.Block() as block:

        @block.sync
        def _(sp):
            m.load_blocks(sp, m.used - 1 + RING)
            for k in range(KC):
                part = m.d["scales"][i, 8 * k:8 * k + 8, :].unsqueeze(1).to_broadcast([8, 16, C])
                sp.dma_start(sc[:, k, :], part).then_inc(ld.sem, 16)
            sp.dma_start(la[:, :], m.d["lora_a"][i]).then_inc(ld.sem, 16)
            sp.dma_start(lb[:, :], m.d["lora_b"][i]).then_inc(ld.sem, 16)

        @block.tensor
        def _(pe):
            pe.wait_ge(ld.sem, ld.base + 96)
            for k in range(KC):
                pe.matmul(ps[:, k, 0:C], la[:, k * P:(k + 1) * P], lb[:, :], start=True, stop=True).then_inc(mm.sem, 1)

        @block.vector
        def _(dve):
            m.wait_block(dve, raw)
            dve.wait_ge(ld.sem, ld.base + 96)
            for k in range(KC):
                dve.tensor_scalar(w[:, k, :], m.slot(raw)[:, k, :].bitcast(I32), 1 / 7.5, -1.0, ALU.mult, ALU.add).then_inc(dv.sem, 1)
            for k in range(KC):
                dve.wait_ge(dv.sem, dv.base + k + 1)
                dve.tensor_tensor(w[:, k, :], w[:, k, :], sc[:, k, :], ALU.mult).then_inc(dv.sem, 1)
            for k in range(KC):
                dve.wait_ge(dv.sem, dv.base + KC + k + 1)
                dve.wait_ge(mm.sem, mm.base + k + 1)
                dve.tensor_tensor(w[:, k, :], w[:, k, :], ps[:, k, 0:C], ALU.add).then_inc(dv.sem, 1)

    mm.advance(KC)
    dv.advance(3 * KC)
    ld.advance(96)


def dense(m, src, w, evac, engine):
    nc, ps, mm = m.nc, m.ps, m.sig["mm"]
    done = m.sig["act_out"] if engine == "scalar" else m.sig["dve_out"]
    with nc.Block() as block:

        @block.tensor
        def _(pe):
            for j in range(2 * KC):
                c, n = divmod(j, 2)
                for k in range(KC):
                    last = pe.matmul(ps[:, j, 0:HT], w[:, k, c * P:(c + 1) * P], src[:, k, halves(n)],
                                     start=k == 0, stop=k == KC - 1)
                last.then_inc(mm.sem, 1)

        def drain(eng):
            for j in range(2 * KC):
                c, n = divmod(j, 2)
                eng.wait_ge(mm.sem, mm.base + j + 1)
                evac(eng, c, n, ps[:, j, 0:HT]).then_inc(done.sem, 1)

        if engine == "scalar":
            block.scalar(drain)
        else:
            block.vector(drain)
    mm.advance(2 * KC)
    done.advance(2 * KC)


def build(nc, d):
    with ExitStack() as ctx:
        m = Decoder(nc, ctx, d)
        x, par, g = m.x, m.par, m.sig

        def buffers(stack):
            return lambda name, shape, dt: stack.enter_context(nc.sbuf_tensor(name, shape, dt))

        for n in ("w_tk", "w_tv", "w_tr", "w_cr"):
            m.add_block(rows(d[n], 0, 0))
        for second, j in mlp_order():
            m.add_block(rows(d["w_cv"], j * C, 0) if second else rows(d["w_ck"], 0, j * C))
        m.add_block(rows(d["Wq"], 0, 0))
        m.add_block(rows(d["Wk"], 0, 0, KX), KX)
        m.add_block(rows(d["Wv"], 0, 0, KX), KX)
        m.add_block(rows(d["Wo"], 0, 0))
        for e in range(E):
            for second, j in mlp_order():
                m.add_block(rows(d["W2"][e], j * C, 0) if second else rows(d["W1"][e], 0, j * C))
        for n in ("rq", "rk", "rv"):
            m.add_block(rows(d[n], 0, 0))
        for j in range(2):
            m.add_block(rows(d["xWq"], 0, j * C))
        for n in ("xWk", "xWv"):
            for j in range(2):
                m.add_block(rows(d[n], 0, j * C, KX), KX)
        for j in range(2):
            m.add_block(rows(d["xWo"], j * C, 0))
        for i in range(6):
            m.add_block(rows(d["qw"][i], 0, 0), KC, I32)

        free = {"tensor": ("s_mm",), "scalar": ("p_exp", "pt_out"), "vector": ("o_out",)}
        with nc.Block() as block:

            @block.tensor
            def _(pe):
                for s in free["tensor"]:
                    pe.sem_inc(g[s].sem, 1)

            @block.scalar
            def _(act):
                for s in free["scalar"]:
                    act.sem_inc(g[s].sem, 1)

            @block.sync
            def _(sp):
                sp.dma_start(x[:, :, :], d["x"]).then_inc(g["x_load"].sem, 16)
                sp.dma_start(par[:, :], d["params"]).then_inc(g["param_load"].sem, 16)
                sp.dma_start(m.ident[:, :], d["ident"]).then_inc(g["const_load"].sem, 16)
                m.load_blocks(sp, RING)

            @block.vector
            def _(dve):
                for s in free["vector"]:
                    dve.sem_inc(g[s].sem, 1)
                dve.memset(m.mean_w[:, :], 1.0 / C)
                dve.memset(m.eps[:, :], EPS)
                dve.wait_ge(g["x_load"].sem, 16)
                dve.wait_ge(g["param_load"].sem, 16)
                dve.wait_ge(g["const_load"].sem, 16)

        g["const_load"].advance(16)
        for names in free.values():
            for s in names:
                g[s].advance(1)

        def add_to(dst, bias=None, bi=0):
            def evac(dve, c, n, bank):
                to = dst[:, c, halves(n)]
                if bias is None:
                    return dve.tensor_tensor(to, bank, to, ALU.add)
                return dve.scalar_tensor_tensor(to, bank, m.column(bias, bi + c), to, ALU.add, ALU.add)
            return evac

        def copy_to(dst, func=ACT.Copy, **kw):
            def evac(act, c, n, bank):
                return act.activation(dst[:, c, halves(n)], bank, func, **{k: (v(c) if callable(v) else v) for k, v in kw.items()})
            return evac

        with ExitStack() as st:
            sb = buffers(st)
            xl, h, a_, b_ = (sb(n, [P, KC, T], F32) for n in ("xl", "h", "ta", "tb"))
            std = sb("std", [P, T], F32)
            keep = sb("keep", [P, 3 * KC], F32)
            with ExitStack() as st2:
                sb2 = buffers(st2)
                layer_norm(m, x, xl, a_, std)
                layer_norm(m, xl, h, a_, std, "ln1_g", "ln1_b")
                k_, v_ = a_, b_
                c_, = (sb2(n, [P, KC, T], F32) for n in ("tc",))
                for name, w, dst, f in (("mix_k", 0, k_, ACT.Copy), ("mix_v", 1, v_, ACT.Copy)):
                    shift_mix(m, h, [(name, c_)], keep)
                    linear(m, chunks(c_), [[(w, 0)]], copy_to(dst, f))
                shift_mix(m, h, [("mix_r", c_)], keep)
                linear(m, chunks(c_), [[(2, 0)]], copy_to(h, ACT.Sigmoid))
            with ExitStack() as st2:
                wkv(m, k_, v_, h, xl, buffers(st2))
            with ExitStack() as st2:
                sb2 = buffers(st2)
                layer_norm(m, xl, h, a_, std, "ln2_g", "ln2_b")
                hid = sb2("hid", [P, 2, KC, T], F32)
                shift_mix(m, h, [("cmix_r", a_)], keep)
                linear(m, chunks(a_), [[(3, 0)]], copy_to(b_, ACT.Sigmoid))
                shift_mix(m, h, [("cmix_k", a_)], keep)
                mlp(m, a_, h, hid, 1)
                with nc.Block() as block:
                    ch = g["dve_chain"]

                    @block.vector
                    def _(dve):
                        dve.tensor_tensor(h[:, :, :], h[:, :, :], b_[:, :, :], ALU.mult).then_inc(ch.sem, 1)
                        dve.tensor_tensor(x[:, :, :], x[:, :, :], xl[:, :, :], ALU.add).then_inc(ch.sem, 1)
                        dve.wait_ge(ch.sem, ch.base + 2)
                        dve.tensor_tensor(x[:, :, :], x[:, :, :], h[:, :, :], ALU.add)
                ch.advance(2)
        if STAGES <= 1:
            return finish(m)

        def cross(layer):
            n_c = KC * (layer + 1)
            D = 32 << layer
            with ExitStack() as st:
                sb = buffers(st)
                q = sb(f"q{layer}", [P, n_c, T], F32)
                with ExitStack() as st2:
                    sb2 = buffers(st2)
                    u, tmp = (sb2(f"{n}{layer}", [P, KC, T], F32) for n in ("xu", "xt"))
                    std = sb2(f"xs{layer}", [P, T], F32)
                    layer_norm(m, x, u, tmp, std)
                    w = m.used
                    if layer == 0:
                        bq = sb2("bqs", [P, KC], F32)
                        with nc.Block() as block:
                            @block.vector
                            def _(dve):
                                dve.tensor_scalar(bq[:, :], par[:, COL["bq"]:COL["bq"] + KC], D ** -0.5, None, ALU.mult)
                        linear(m, chunks(u), [[(w, 0)]], copy_to(q, ACT.Identity, scale=D ** -0.5, bias=lambda c: bq[:, c:c + 1]))
                    else:
                        linear(m, chunks(u), [[(w, 0)], [(w + 1, 0)]], copy_to(q, ACT.Copy, scale=D ** -0.5))
                o = sb(f"o{layer}", [P, n_c, T], F32)
                with ExitStack() as st2:
                    attention(m, q, o, layer, buffers(st2))
                w = m.used
                parts = [(w + i, KC * i) for i in range(layer + 1)]
                linear(m, chunks(o, n_c), [parts], add_to(x, "xbo" if layer else "bo"), "vector")

        cross(0)
        if STAGES <= 2:
            return finish(m)

        with ExitStack() as st:
            sb = buffers(st)
            u, y = (sb(n, [P, KC, T], F32) for n in ("eu", "ey"))
            gate = sb("gate", [P, E * T], F32)
            with ExitStack() as st2:
                sb2 = buffers(st2)
                std = sb2("es", [P, T], F32)
                layer_norm(m, x, u, y, std)
                gates(m, u, gate, y, sb2)
            hid = sb("ehid", [P, 2, KC, T], F32)
            b1 = sb("b1", [P, FF // P], F32)
            mlp(m, u, y, hid, E, gate, b1, clear=False)
            with nc.Block() as block:
                @block.vector
                def _(dve):
                    dve.tensor_tensor(x[:, :, :], x[:, :, :], y[:, :, :], ALU.add)
        if STAGES <= 3:
            return finish(m)

        with ExitStack() as st:
            sb = buffers(st)
            u, q, k_ = (sb(n, [P, KC, T], F32) for n in ("ru", "rqt", "rkt"))
            v = sb("rvt", [S, B, C], F32)
            sT = sb("rst", [S, B, S], F32)
            std = sb("rs", [P, T], F32)
            theta = sb("theta", [P, KC], F32)
            decay = sb("decay", [S, S], F32)
            layer_norm(m, x, u, q, std)
            ld = g["const_load"]
            with nc.Block() as block:
                @block.sync
                def _(sp):
                    sp.dma_start(decay[:, :], d["decay"]).then_inc(ld.sem, 16)

                @block.scalar
                def _(act):
                    act.activation(theta[:, :], par[:, COL["theta"]:COL["theta"] + KC], ACT.Exp, scale=0.0)
                    act.wait_ge(ld.sem, ld.base + 16)
            ld.advance(16)
            w = m.used
            scaled = dict(scale=lambda c: theta[:, c:c + 1])
            linear(m, chunks(u), [[(w, 0)]], copy_to(q, ACT.Identity, **scaled))
            linear(m, chunks(u), [[(w + 1, 0)]], copy_to(k_, ACT.Identity, **scaled))
            values(m, u, v, w + 2)
            retention(m, q, k_, v, sT, decay)
        if STAGES <= 4:
            return finish(m)

        cross(1)
        if STAGES <= 5:
            return finish(m)

        with ExitStack() as st:
            sb = buffers(st)
            u, h, t_ = (sb(n, [P, KC, T], F32) for n in ("fu", "fh", "ft"))
            std = sb("fs", [P, T], F32)
            wq = sb("wq", [P, KC, C], F32)
            sc = sb("sc_", [P, KC, C], F32)
            la, lb = (sb(n, [32, C], F32) for n in ("la", "lb"))
            layer_norm(m, x, h, t_, std)
            for blk in range(3):
                for half in range(2):
                    i = 2 * blk + half
                    dequantise(m, i, m.used, wq, sc, la, lb)
                    bias = lambda c, i=i: m.column("qbias", i * KC + c)
                    if half == 0:
                        dense(m, h, wq, copy_to(u, ACT.Identity, bias=bias), "scalar")
                        layer_norm(m, u, u, t_, std, "gamma", "beta", ACT.Gelu, blk * KC)
                    else:
                        dense(m, u, wq, add_to(h, "qbias", i * KC), "vector")
            with nc.Block() as block:
                @block.vector
                def _(dve):
                    dve.tensor_tensor(x[:, :, :], x[:, :, :], h[:, :, :], ALU.add)
        finish(m)


STAGES = 99


def finish(m):
    with m.nc.Block() as block:

        @block.sync
        def _(sp):
            sp.dma_start(m.d["out"], m.x[:, :, :]).then_inc(m.sig["store"].sem, 16)
            sp.wait_ge(m.sig["store"].sem, 16)
            for w in range(m.loaded - RING, m.loaded):
                m.wait_block(sp, w)




def kernel(**inputs):
    import numpy as np
    import concourse.bacc as bacc
    from concourse.bass_utils import run_bass_kernel_spmd

    a = {k: np.asarray(v) for k, v in inputs.items()}

    def cols(v):
        return np.asarray(v).reshape(-1, P).T

    L0, X0, F0, R1, X1, F1 = "L0_attn_", "L0_xattn_", "L0_ffn_", "L1_attn_", "L1_xattn_", "L1_ffn_"
    par = {n: a[L0 + n] for n in ("time_decay", "time_first", "ln1_g", "ln1_b", "ln2_g", "ln2_b",
                                  "mix_k", "mix_v", "mix_r", "cmix_k", "cmix_r")}
    par |= {n: a[X0 + n] for n in ("bq", "bk", "bv", "bo")}
    par |= {"theta": a[R1 + "theta"], "xbo": a[X1 + "bo"], "qbias": a[F1 + "biases"],
            "gamma": a[F1 + "ln_gamma"], "beta": a[F1 + "ln_beta"], "b1": a[F0 + "b1"]}
    diff = np.arange(S)[None, :] - np.arange(S)[:, None]
    decay = np.where(diff >= 0, np.float32(0.96875) ** np.maximum(diff, 0).astype(np.float32), np.float32(0))
    arrays = {
        "x": a["x"].reshape(T, KC, P).transpose(2, 1, 0),
        "ctx": a["ctx_768"].reshape(B, NKV, KX, P).transpose(0, 3, 2, 1),
        "params": np.concatenate([cols(par[n]) for n, _ in PARAMS], axis=1),
        "ident": np.eye(P, dtype=np.float32),
        "before": np.broadcast_to(np.tri(E, E, -1, dtype=np.float32), (P, E, E)),
        "pick": np.broadcast_to(np.eye(E, dtype=np.float32)[:, :, None], (E, E, P)),
        "decay": decay.astype(np.float32),
        "centroids": a[F0 + "centroids"].reshape(E, KC, P).transpose(2, 1, 0),
        "W1": a[F0 + "W1"], "W2": a[F0 + "W2"], "b2": a[F0 + "b2"],
        "rq": a[R1 + "weight_q"], "rk": a[R1 + "weight_k"], "rv": a[R1 + "weight_v"],
        "qw": a[F1 + "qweights"].transpose(0, 2, 1),
        "scales": a[F1 + "scales"].transpose(0, 2, 1),
        "lora_a": a[F1 + "lora_a"], "lora_b": a[F1 + "lora_b"].transpose(0, 2, 1),
    }
    arrays |= {n: a[L0 + n] for n in ("w_tk", "w_tv", "w_tr", "w_ck", "w_cv", "w_cr")}
    arrays |= {n: a[X0 + n] for n in ("Wq", "Wk", "Wv", "Wo")}
    arrays |= {"x" + n: a[X1 + n] for n in ("Wq", "Wk", "Wv", "Wo")}
    nc = bacc.Bacc("TRN2", target_bir_lowering=False, num_devices=1)
    given, d = {}, {}
    for n, v in arrays.items():
        given[f"in_{n}"] = v = np.ascontiguousarray(v)
        d[n] = nc.dram_tensor(f"in_{n}", v.shape, mybir.dt.from_np(v.dtype), kind="ExternalInput").ap()
    d["out"] = nc.dram_tensor("out_x", (P, KC, T), F32, kind="ExternalOutput").ap()
    build(nc, d)
    r = run_bass_kernel_spmd(nc, [given], core_ids=[0])
    out = np.asarray(r.results[0]["out_x"])
    return np.ascontiguousarray(out.transpose(2, 1, 0).reshape(B, S, C))
```

```python
from contextlib import ExitStack

import concourse.bass as bass
from concourse import mybir
from concourse.alu_op_type import AluOpType as ALU

F32 = mybir.dt.float32
F32R = mybir.dt.float32r
I32 = mybir.dt.int32
ACT = mybir.ActivationFunctionType
AX = mybir.AxisListType

P = 128
B, S, C = 8, 100, 512
T = B * S
KC = C // P
HT = T // 2
NKV, CKV = 722, 384
KX = CKV // P
KVC = -(-NKV // P)
KVR = NKV - (KVC - 1) * P
HEADS = 16
FF = 4 * C
E = 8
RING = 4
PAIRS = 2
BANK = 512
EPS = 1e-5
NEG_INF = -1e38
CLAMP = 1e4

PARAMS = [("time_decay", KC), ("time_first", KC), ("ln1_g", KC), ("ln1_b", KC), ("ln2_g", KC), ("ln2_b", KC),
          ("mix_k", KC), ("mix_v", KC), ("mix_r", KC), ("cmix_k", KC), ("cmix_r", KC),
          ("bq", KC), ("bk", KC), ("bv", KC), ("bo", KC), ("theta", KC), ("xbo", KC),
          ("b1", E * FF // P), ("qbias", 6 * KC), ("gamma", 3 * KC), ("beta", 3 * KC)]
COL, _n = {}, 0
for _name, _w in PARAMS:
    COL[_name] = _n
    _n += _w
N_PARAMS = _n


class Signal:

    def __init__(self, ctx, nc, name):
        self.sem = ctx.enter_context(nc.semaphore(name))
        self.base = 0

    def advance(self, n):
        self.base += n


class Decoder:

    def __init__(self, nc, ctx, d):
        self.nc, self.d = nc, d
        self.ps = ctx.enter_context(nc.psum_tensor("ps", [P, 8, BANK], F32))
        self.x = ctx.enter_context(nc.sbuf_tensor("x", [P, KC, T], F32))
        self.ring = ctx.enter_context(nc.sbuf_tensor("ring", [P, RING, KC, C], F32))
        self.par = ctx.enter_context(nc.sbuf_tensor("par", [P, N_PARAMS], F32))
        self.mean_w = ctx.enter_context(nc.sbuf_tensor("mean_w", [P, P], F32))
        self.eps = ctx.enter_context(nc.sbuf_tensor("eps", [P, 1], F32))
        self.ident = ctx.enter_context(nc.sbuf_tensor("ident", [P, P], F32))
        self.pairs = ctx.enter_context(nc.sbuf_tensor("pairs", [P, PAIRS, 2, KC, C], F32R))
        names = ("param_load x_load const_load ctx_load store mm act_out dve_out dve_chain ln_cen ln_sq ln_std b1_copy"
                 " k_out v_out q_copy s_mm s_clip s_max p_exp p_norm p_turn pt_out o_mm o_out act_hid hid_out y_out"
                 " norm_rec w_high w_low in_high in_mid in_low hid_high hid_mul lora_mm lora_out quant_load0 quant_load1 ctx_high ctx_low k_low q_high q_low").split()
        self.sig = {n: Signal(ctx, nc, n) for n in names}
        self.block_load = [Signal(ctx, nc, f"block_load{i}") for i in range(RING)]
        self.blocks = []
        self.loaded = 0
        self.used = 0
        self.free_at = []
        self.high = self.low = 0

    def column(self, name, i):
        c = COL[name] + i
        return self.par[:, c:c + 1]


    def add_block(self, source, kc=KC, dtype=F32):
        self.blocks.append((source, kc, dtype))

    def slot(self, w):
        return self.ring[:, w % RING]

    def wait_block(self, eng, w):
        eng.wait_ge(self.block_load[w % RING].sem, 16 * (w // RING + 1))

    def load_blocks(self, sp, until):
        until = min(until, len(self.blocks))
        while self.loaded < until:
            w = self.loaded
            source, kc, dtype = self.blocks[w]
            if w >= RING:
                sp.wait_ge(self.sig["w_low"].sem, w - RING + 1)
            dst = self.slot(w)[:, 0:kc, :]
            if dtype != F32:
                dst = dst.bitcast(dtype)
            sp.dma_start(dst, source).then_inc(self.block_load[w % RING].sem, 16)
            self.loaded += 1

    def pair(self, w, part):
        return self.pairs[:, w % PAIRS, part]

    def wait_pair(self, eng, w):
        eng.wait_ge(self.sig["w_low"].sem, w + 1)

    def split_high(self, act, until):
        while self.high < min(until, len(self.blocks)) and self.blocks[self.high][2] == F32:
            w = self.high
            kc = self.blocks[w][1]
            self.wait_block(act, w)
            if w >= PAIRS:
                act.wait_ge(self.sig["mm"].sem, self.free_at[w - PAIRS])
            act.activation(self.pair(w, 0)[:, 0:kc], self.slot(w)[:, 0:kc], ACT.Copy).then_inc(self.sig["w_high"].sem, 1)
            self.high += 1

    def split_low(self, dve, until):
        while self.low < min(until, len(self.blocks)) and self.blocks[self.low][2] == F32:
            w = self.low
            kc = self.blocks[w][1]
            dve.wait_ge(self.sig["w_high"].sem, w + 1)
            dve.tensor_tensor(self.pair(w, 1)[:, 0:kc], self.slot(w)[:, 0:kc], self.pair(w, 0)[:, 0:kc].bitcast(F32),
                              ALU.subtract).then_inc(self.sig["w_low"].sem, 1)
            self.low += 1


def rows(w, r0, c0, kc=KC, cols=C):
    return w[r0:r0 + kc * P, c0:c0 + cols].rearrange("(k p) n -> p k n", p=P)


PASSES = ((0, 0), (0, 1), (1, 0))


def product(pe, bank, terms):
    for t, (w, x) in enumerate(terms):
        for i, (a, b) in enumerate(PASSES):
            last = pe.matmul(bank, w(a), x(b), start=t == 0 and i == 0, stop=t == len(terms) - 1 and i == 2)
    return last


def halves(n):
    return slice(n * HT, (n + 1) * HT)


def mlp_order():
    return [(0, 0), (0, 1), (1, 0), (0, 2), (1, 1), (0, 3), (1, 2), (1, 3)]


def layer_norm(m, src, dst, tmp, std, gain=None, bias=None, func=None, gi=0, pair=None):
    nc, ps, g = m.nc, m.ps, m.sig
    mm, cen, sq, sd, out, ch = g["mm"], g["ln_cen"], g["ln_sq"], g["ln_std"], g["dve_out"], g["dve_chain"]
    high, aff = g["in_high"], g["in_mid"]
    with nc.Block() as block:

        @block.tensor
        def _(pe):
            for n in range(2):
                for k in range(KC):
                    last = pe.matmul(ps[:, n, 0:HT], m.mean_w[:, :], src[:, k, halves(n)], start=k == 0, stop=k == KC - 1)
                last.then_inc(mm.sem, 1)
            for n in range(2):
                pe.wait_ge(sq.sem, sq.base + n + 1)
                for k in range(KC):
                    last = pe.matmul(ps[:, 2 + n, 0:HT], m.mean_w[:, :], tmp[:, k, halves(n)], start=k == 0, stop=k == KC - 1)
                last.then_inc(mm.sem, 1)

        @block.vector
        def _(dve):
            for n in range(2):
                dve.wait_ge(mm.sem, mm.base + n + 1)
                dve.tensor_tensor(dst[:, :, halves(n)], src[:, :, halves(n)],
                                  ps[:, n, 0:HT].unsqueeze(1).to_broadcast([P, KC, HT]), ALU.subtract).then_inc(cen.sem, 1)
            for n in range(2):
                dve.wait_ge(sd.sem, sd.base + n + 1)
                dve.reciprocal(std[:, halves(n)], std[:, halves(n)]).then_inc(ch.sem, 1)
                dve.wait_ge(ch.sem, ch.base + n + 1)
                dve.tensor_tensor(dst[:, :, halves(n)], dst[:, :, halves(n)],
                                  std[:, halves(n)].unsqueeze(1).to_broadcast([P, KC, HT]), ALU.mult).then_inc(out.sem, 1)
            if pair is not None:
                for n in range(2):
                    dve.wait_ge(high.sem, high.base + n + 1)
                    dve.tensor_tensor(pair[:, 1, :, halves(n)], dst[:, :, halves(n)],
                                      pair[:, 0, :, halves(n)].bitcast(F32), ALU.subtract)

        @block.scalar
        def _(act):
            for n in range(2):
                act.wait_ge(cen.sem, cen.base + n + 1)
                act.activation(tmp[:, :, halves(n)], dst[:, :, halves(n)], ACT.Square).then_inc(sq.sem, 1)
            for n in range(2):
                act.wait_ge(mm.sem, mm.base + n + 3)
                act.activation(std[:, halves(n)], ps[:, 2 + n, 0:HT], ACT.Sqrt, bias=m.eps[:, 0:1]).then_inc(sd.sem, 1)
            if gain is not None:
                for n in range(2):
                    act.wait_ge(out.sem, out.base + n + 1)
                    for k in range(KC):
                        act.activation(dst[:, k, halves(n)], dst[:, k, halves(n)], func or ACT.Identity,
                                       scale=m.column(gain, gi + k), bias=m.column(bias, gi + k)).then_inc(aff.sem, 1)
            if pair is not None:
                for n in range(2):
                    if gain is None:
                        act.wait_ge(out.sem, out.base + n + 1)
                    else:
                        act.wait_ge(aff.sem, aff.base + KC * (n + 1))
                    act.activation(pair[:, 0, :, halves(n)], dst[:, :, halves(n)], ACT.Copy).then_inc(high.sem, 1)

    if gain is not None:
        aff.advance(2 * KC)
    if pair is not None:
        high.advance(2)
    for s, n in ((mm, 4), (cen, 2), (sq, 2), (sd, 2), (out, 2), (ch, 2)):
        s.advance(n)


def linear(m, src, blocks, evac, engine="scalar", quantised=None, layer=0):
    nc, ps, mm = m.nc, m.ps, m.sig["mm"]
    done = m.sig["act_out"] if engine == "scalar" else m.sig["dve_out"]
    G = 2 * KC
    n_groups = G * len(blocks)
    for i, w in enumerate(blocks):
        assert w == len(m.free_at)
        m.free_at.append(mm.base + G * (i + 1))
    m.used = len(m.free_at)
    more = quantised is not None and layer < 5
    out = m.sig["lora_out"]
    with nc.Block() as block:

        @block.sync
        def _(sp):
            m.load_blocks(sp, m.used + RING)
            if quantised is not None and layer < 4:
                quantised.sync(sp, layer + 2)

        @block.tensor
        def _(pe):
            for j in range(n_groups):
                i, g = divmod(j, G)
                c, n = divmod(g, 2)
                w = blocks[i]
                if g == 0:
                    m.wait_pair(pe, w)
                if j >= 8:
                    pe.wait_ge(done.sem, done.base + j - 7)
                if more and j >= 8 - KC:
                    pe.wait_ge(out.sem, KC * (layer + 1) + j - (8 - KC) + 1)
                product(pe, ps[:, j % 8, 0:HT],
                        [(lambda a, k=k: m.pair(w, a)[:, k, c * P:(c + 1) * P], lambda b, k=k: src[:, b, k, halves(n)])
                         for k in range(KC)]).then_inc(mm.sem, 1)
            if quantised is not None and layer < 4:
                quantised.tensor(pe, layer + 2, lambda k: pe.wait_ge(done.sem, done.base + 8 - KC + k + 1))

        def drain(eng, split):
            split(eng, blocks[0] + 1)
            for i in range(len(blocks)):
                split(eng, blocks[i] + 2)
                for g in range(G):
                    j = i * G + g
                    eng.wait_ge(mm.sem, mm.base + j + 1)
                    evac(eng, i * KC + g // 2, g % 2, ps[:, j % 8, 0:HT]).then_inc(done.sem, 1)
                    if more and engine == "scalar" and g % 2 == 1:
                        quantised.scalar(eng, layer + 1, g // 2)

        @block.scalar
        def _(act):
            if engine == "scalar":
                drain(act, m.split_high)
            else:
                m.split_high(act, m.used + 1)
                if more:
                    for k in range(KC):
                        quantised.scalar(act, layer + 1, k)

        @block.vector
        def _(dve):
            if more:
                quantised.vector(dve, layer + 1)
            if engine == "vector":
                drain(dve, m.split_low)
            else:
                m.split_low(dve, m.used + 1)
            if more:
                quantised.vector_low(dve, layer + 1)

    if more:
        quantised.advance(layer + 1)
    mm.advance(n_groups)
    done.advance(n_groups)


def mix_chunk_scalar(m, act, i, name, h, tmp, pair):
    mid, high, low = m.sig["in_mid"], m.sig["in_high"], m.sig["in_low"]
    scaled = m.sig["hid_mul"]
    for k in range(KC):
        if i > 0:
            act.wait_ge(low.sem, low.base + (i - 1) * KC + k + 1)
        act.activation(tmp[:, k, :], h[:, k, :], ACT.Identity, scale=m.column(name, k)).then_inc(scaled.sem, 1)
    for k in range(KC):
        act.wait_ge(mid.sem, mid.base + i * KC + k + 1)
        act.activation(pair[:, 0, k, :], tmp[:, k, :], ACT.Copy).then_inc(high.sem, 1)


def mix_chunk_vector(m, dve, i, h, tmp, pair, keep):
    mid, high, low = m.sig["in_mid"], m.sig["in_high"], m.sig["in_low"]
    scaled = m.sig["hid_mul"]
    for k in range(KC):
        dve.wait_ge(scaled.sem, scaled.base + i * KC + k + 1)
        to = tmp[:, k, :].rearrange("p (b s) -> p b s", s=S)
        of = h[:, k, :].rearrange("p (b s) -> p b s", s=S)
        dve.scalar_tensor_tensor(to[:, :, 1:S], of[:, :, 0:S - 1], keep[:, i * KC + k:i * KC + k + 1],
                                 to[:, :, 1:S], ALU.mult, ALU.add).then_inc(mid.sem, 1)
    for k in range(KC):
        dve.wait_ge(high.sem, high.base + i * KC + k + 1)
        dve.tensor_tensor(pair[:, 1, k, :], tmp[:, k, :], pair[:, 0, k, :].bitcast(F32), ALU.subtract).then_inc(low.sem, 1)


def mixed_linears(m, h, mixes, pairs, tmp, keep):
    nc, ps, mm, done, low, ch = m.nc, m.ps, m.sig["mm"], m.sig["act_out"], m.sig["in_low"], m.sig["dve_chain"]
    G = 2 * KC
    w0 = m.used
    linears = sum(e is not None for _, e in mixes)
    for i in range(linears):
        m.free_at.append(mm.base + G * (i + 1))
    m.used = len(m.free_at)
    with nc.Block() as block:

        @block.sync
        def _(sp):
            m.load_blocks(sp, m.used + RING)

        @block.tensor
        def _(pe):
            for i in range(linears):
                m.wait_pair(pe, w0 + i)
                pe.wait_ge(low.sem, low.base + KC * (i + 1))
                for g in range(G):
                    c, n = divmod(g, 2)
                    if i > 0:
                        pe.wait_ge(done.sem, done.base + (i - 1) * G + g + 1)
                    product(pe, ps[:, g, 0:HT],
                            [(lambda a, k=k: m.pair(w0 + i, a)[:, k, c * P:(c + 1) * P],
                              lambda b, k=k: pairs[i % 2][:, b, k, halves(n)]) for k in range(KC)]).then_inc(mm.sem, 1)

        def drain(act, i):
            for g in range(G):
                act.wait_ge(mm.sem, mm.base + i * G + g + 1)
                mixes[i][1](act, g // 2, g % 2, ps[:, g, 0:HT]).then_inc(done.sem, 1)

        @block.scalar
        def _(act):
            for i, (name, _) in enumerate(mixes):
                if i >= 2:
                    act.wait_ge(mm.sem, mm.base + G * (i - 1))
                mix_chunk_scalar(m, act, i, name, h, tmp, pairs[i % 2])
                m.split_high(act, w0 + i + 1)
                if i > 0:
                    drain(act, i - 1)
            if linears == len(mixes):
                m.split_high(act, m.used + 1)
                drain(act, linears - 1)

        @block.vector
        def _(dve):
            for i, (name, _) in enumerate(mixes):
                c = COL[name]
                dve.tensor_scalar(keep[:, i * KC:(i + 1) * KC], m.par[:, c:c + KC], -1.0, 1.0, ALU.mult, ALU.add).then_inc(ch.sem, 1)
            dve.wait_ge(ch.sem, ch.base + len(mixes))
            for i in range(len(mixes)):
                mix_chunk_vector(m, dve, i, h, tmp, pairs[i % 2], keep)
                m.split_low(dve, w0 + i + 1)
            if linears == len(mixes):
                m.split_low(dve, m.used + 1)

    for s in ("in_low", "in_mid", "in_high", "hid_mul"):
        m.sig[s].advance(KC * len(mixes))
    ch.advance(len(mixes))
    mm.advance(G * linears)
    done.advance(G * linears)


def wkv(m, k_, v_, r_, xl, sb):
    nc, dv, ac = m.nc, m.sig["dve_chain"], m.sig["act_out"]
    mx, qq, aa = (sb(n, [P, KC, B, S + 1], F32) for n in ("wkv_m", "wkv_q", "wkv_a"))
    t1, t2 = (sb(n, [P, KC, B, S], F32) for n in ("wkv_t1", "wkv_t2"))
    t3 = qq[:, :, :, 1:]

    def bs(t, c):
        return t[:, c, :].rearrange("p (b s) -> p b s", s=S)

    with nc.Block() as block:

        @block.vector
        def _(dve):
            n = 0

            def out(ins):
                nonlocal n
                n += 1
                ins.then_inc(dv.sem, 1)

            def own():
                dve.wait_ge(dv.sem, dv.base + n)

            def after_act(count):
                dve.wait_ge(ac.sem, ac.base + count)

            out(dve.memset(mx[:, :, :, 0:1], NEG_INF))
            out(dve.memset(qq[:, :, :, 0:1], 1.0))
            out(dve.memset(aa[:, :, :, 0:1], 0.0))
            own()
            for c in range(KC):
                for b in range(B):
                    out(dve.tensor_tensor_scan(mx[:, c, b, 1:], k_[:, c, b * S:(b + 1) * S],
                                               m.column("time_decay", c).to_broadcast([P, S]), NEG_INF, ALU.max, ALU.add))
            own()
            for c in range(KC):
                out(dve.tensor_tensor(t1[:, c], mx[:, c, :, 0:S], mx[:, c, :, 1:], ALU.subtract))
                out(dve.tensor_tensor(t2[:, c], bs(k_, c), mx[:, c, :, 1:], ALU.subtract))
            for c in range(KC):
                after_act(2 * c + 2)
                for b in range(B):
                    out(dve.tensor_tensor_scan(qq[:, c, b, 1:], t1[:, c, b, :], t2[:, c, b, :], 1.0, ALU.mult, ALU.add))
            for c in range(KC):
                after_act(2 * KC + c + 1)
                out(dve.tensor_tensor(mx[:, c], mx[:, c], qq[:, c], ALU.add))
            own()
            for c in range(KC):
                out(dve.tensor_tensor(t3[:, c], mx[:, c, :, 0:S], bs(k_, c), ALU.max))
            own()
            for c in range(KC):
                out(dve.tensor_tensor(t1[:, c], mx[:, c, :, 0:S], t3[:, c], ALU.subtract))
                out(dve.tensor_tensor(t2[:, c], bs(k_, c), t3[:, c], ALU.subtract))
            for c in range(KC):
                after_act(3 * KC + 2 * c + 2)
                out(dve.tensor_tensor(t2[:, c], t2[:, c], bs(v_, c), ALU.mult))
            own()
            for c in range(KC):
                for b in range(B):
                    out(dve.tensor_tensor_scan(aa[:, c, b, 1:], t1[:, c, b, :], t2[:, c, b, :], 0.0, ALU.mult, ALU.add))
            for c in range(KC):
                out(dve.tensor_scalar(k_[:, c, :], k_[:, c, :], m.column("time_first", c), None, ALU.add))
            own()
            for c in range(KC):
                out(dve.tensor_tensor(t3[:, c], mx[:, c, :, 0:S], bs(k_, c), ALU.max))
            own()
            for c in range(KC):
                out(dve.tensor_tensor(t1[:, c], mx[:, c, :, 0:S], t3[:, c], ALU.subtract))
                out(dve.tensor_tensor(t2[:, c], bs(k_, c), t3[:, c], ALU.subtract))
            for c in range(KC):
                after_act(5 * KC + 2 * c + 2)
                out(dve.tensor_tensor(t3[:, c], t1[:, c], t2[:, c], ALU.add))
            own()
            for c in range(KC):
                out(dve.reciprocal(t3[:, c], t3[:, c]))
                out(dve.tensor_tensor(t1[:, c], t1[:, c], aa[:, c, :, 0:S], ALU.mult))
                out(dve.tensor_tensor(t2[:, c], t2[:, c], bs(v_, c), ALU.mult))
            own()
            for c in range(KC):
                out(dve.tensor_tensor(t1[:, c], t1[:, c], t2[:, c], ALU.add))
                out(dve.tensor_tensor(t3[:, c], t3[:, c], bs(r_, c), ALU.mult))
            own()
            for c in range(KC):
                out(dve.tensor_tensor(t1[:, c], t1[:, c], t3[:, c], ALU.mult))
            own()
            for c in range(KC):
                out(dve.tensor_tensor(bs(xl, c), bs(xl, c), t1[:, c], ALU.add))
            wkv.dve_count = n

        @block.scalar
        def _(act):
            scans = B * KC
            d1 = dv.base + 3 + scans
            for c in range(KC):
                for i, t in enumerate((t1, t2)):
                    act.wait_ge(dv.sem, d1 + 2 * c + i + 1)
                    act.activation(t[:, c], t[:, c], ACT.Exp, bias=m.column("time_decay", c)).then_inc(ac.sem, 1)
            d2 = d1 + 2 * KC
            for c in range(KC):
                act.wait_ge(dv.sem, d2 + B * (c + 1))
                act.activation(qq[:, c], qq[:, c], ACT.Ln).then_inc(ac.sem, 1)
            d3 = d2 + scans + 2 * KC
            for c in range(KC):
                for i, t in enumerate((t1, t2)):
                    act.wait_ge(dv.sem, d3 + 2 * c + i + 1)
                    act.activation(t[:, c], t[:, c], ACT.Exp).then_inc(ac.sem, 1)
            d4 = d3 + 2 * KC + KC + scans + 2 * KC
            for c in range(KC):
                for i, t in enumerate((t1, t2)):
                    act.wait_ge(dv.sem, d4 + 2 * c + i + 1)
                    act.activation(t[:, c], t[:, c], ACT.Exp).then_inc(ac.sem, 1)

    dv.advance(wkv.dve_count)
    ac.advance(7 * KC)


def mlp(m, src, y, pre, hid, experts, gate=None, b1=None, clear=True):
    nc, ps = m.nc, m.ps
    mm, ah, hm, hh_, ho, yo, ch, bc = (m.sig[s] for s in ("mm", "act_hid", "hid_mul", "hid_high", "hid_out", "y_out", "dve_chain", "b1_copy"))
    order = mlp_order()
    N = len(order)
    G = 2 * KC
    per = N * G
    half = per // 2
    w0 = m.used
    wh, wl = m.sig["w_high"].sem, m.sig["w_low"].sem
    assert w0 % RING == 0 and m.high == m.low == w0 + 1

    def before(i):
        return [k for k, _ in order[:i]].count(order[i][0]) * G

    for e in range(experts):
        for i in range(N):
            m.free_at.append(mm.base + e * per + (i + 1) * G)
    m.used = len(m.free_at)

    def run(eng, body):
        if experts == 1:
            body(0)
        else:
            with eng.Fori(0, experts) as e:
                body(e)

    with nc.Block() as block:

        @block.sync
        def _(sp):
            assert m.loaded == w0 + RING
            if experts > 1:
                with sp.Fori(0, experts - 1) as e:
                    for i in range(N):
                        ahead, (second, j) = (i + RING) // N, order[(i + RING) % N]
                        sp.wait_ge(wl, w0 + i + 1 + e * N)
                        w = m.d["W2"] if second else m.d["W1"]
                        part = w[e + ahead, j * C:(j + 1) * C, :] if second else w[e + ahead, :, j * C:(j + 1) * C]
                        sp.dma_start(m.slot(i), part.rearrange("(k p) n -> p k n", p=P)).then_inc(m.block_load[i % RING].sem, 16)
                m.loaded += N * (experts - 1)
            m.load_blocks(sp, m.used + RING)

        @block.tensor
        def _(pe):
            def body(e):
                for i, (second, j) in enumerate(order):
                    pe.wait_ge(wl, w0 + i + 1 + e * N)
                    if second:
                        pe.wait_ge(ho.sem, ho.base + e * half + (j + 1) * G)
                    used = yo if second else ah
                    for g in range(G):
                        c, n = divmod(g, 2)
                        at = before(i) + g
                        if at >= 4 or experts > 1:
                            pe.wait_ge(used.sem, used.base + e * half + at - 3)
                        if second:
                            x = lambda b, k: hid[:, j % 2, b, k, halves(n)]
                        else:
                            x = lambda b, k: src[:, b, k, halves(n)]
                        product(pe, ps[:, 4 * second + at % 4, 0:HT],
                                [(lambda a, k=k: m.pair(i, a)[:, k, c * P:(c + 1) * P], lambda b, k=k: x(b, k))
                                 for k in range(KC)]).then_inc(mm.sem, 1)
            run(pe, body)

        @block.scalar
        def _(act):
            def split(e, i):
                act.wait_ge(m.block_load[i % RING].sem, 16 * ((w0 + i) // RING + 1) + e * (16 * N // RING))
                act.wait_ge(mm.sem, mm.base + e * per + (i - 1) * G)
                act.activation(m.pair(i, 0), m.slot(i), ACT.Copy).then_inc(wh, 1)

            def body(e):
                if gate is not None:
                    act.wait_ge(bc.sem, bc.base + e + 1)
                for i, (second, j) in enumerate(order):
                    split(e, i + 1)
                    if second:
                        continue

                    def high(g):
                        c, n = divmod(g, 2)
                        act.wait_ge(hm.sem, hm.base + e * half + before(i) + g + 1)
                        act.activation(hid[:, j % 2, 0, c, halves(n)], pre[:, g, :], ACT.Copy).then_inc(hh_.sem, 1)

                    for g in range(G):
                        c, n = divmod(g, 2)
                        at = before(i) + g
                        act.wait_ge(mm.sem, mm.base + e * per + i * G + g + 1)
                        if at >= G or experts > 1:
                            act.wait_ge(ho.sem, ho.base + e * half + at - G + 1)
                        pin = ps[:, at % 4, 0:HT]
                        if gate is None:
                            ins = act.activation(pre[:, g, :], pin, ACT.Relu)
                        else:
                            ins = act.activation(pre[:, g, :], pin, ACT.Gelu, bias=b1[:, j * KC + c:j * KC + c + 1])
                        ins.then_inc(ah.sem, 1)
                        if g == 0 and (j >= 2 or experts > 1):
                            back = (order.index((1, j - 2)) + 1) * G if j >= 2 else (order.index((1, j + 2)) + 1) * G - per
                            act.wait_ge(mm.sem, mm.base + e * per + back)
                        if g > 0:
                            high(g - 1)
                    high(G - 1)
            run(act, body)

        @block.vector
        def _(dve):
            if clear:
                dve.memset(y[:, :, :], 0.0).then_inc(ch.sem, 1)
                dve.wait_ge(ch.sem, ch.base + 1)

            def copy_b1(e):
                at = COL["b1"] + e * (FF // P)
                dve.tensor_scalar(b1[:, :], m.par[:, bass.ds(at, FF // P)], 1.0, None, ALU.mult).then_inc(bc.sem, 1)

            if gate is not None:
                copy_b1(0)

            def body(e):
                for i, (second, j) in enumerate(order):
                    dve.wait_ge(wh, w0 + i + 2 + e * N)
                    dve.tensor_tensor(m.pair(i + 1, 1), m.slot(i + 1), m.pair(i + 1, 0).bitcast(F32), ALU.subtract).then_inc(wl, 1)
                    if gate is not None and (second, j) == (1, 2):
                        dve.wait_ge(ah.sem, ah.base + e * half + half)
                        copy_b1(e + 1)

                    def low(g):
                        c, n = divmod(g, 2)
                        dve.wait_ge(hh_.sem, hh_.base + e * half + before(i) + g + 1)
                        dve.tensor_tensor(hid[:, j % 2, 1, c, halves(n)], pre[:, g, :],
                                          hid[:, j % 2, 0, c, halves(n)].bitcast(F32), ALU.subtract).then_inc(ho.sem, 1)

                    for g in range(G):
                        c, n = divmod(g, 2)
                        at = before(i) + g
                        if second:
                            dve.wait_ge(mm.sem, mm.base + e * per + i * G + g + 1)
                            if at >= G or experts > 1:
                                dve.wait_ge(yo.sem, yo.base + e * half + at - G + 1)
                            yy = y[:, c, halves(n)]
                            dve.tensor_tensor(yy, ps[:, 4 + at % 4, 0:HT], yy, ALU.add).then_inc(yo.sem, 1)
                        else:
                            dve.wait_ge(ah.sem, ah.base + e * half + at + 1)
                            hh = pre[:, g, :]
                            by = hh if gate is None else gate[:, bass.ds(n * HT + e * T, HT)]
                            dve.tensor_tensor(hh, hh, by, ALU.mult).then_inc(hm.sem, 1)
                            if g > 0:
                                low(g - 1)
                    if not second:
                        low(G - 1)
            run(dve, body)

    m.high = m.low = w0 + experts * N + 1
    bc.advance(experts + 1 if gate is not None else 0)
    mm.advance(experts * per)
    for s in (ah, hm, hh_, ho, yo):
        s.advance(experts * half)
    ch.advance(1 if clear else 0)


def attention(m, q, o, D, clip, bias, name, sb):
    nc, ps = m.nc, m.ps
    H = C // D
    HPC = P // D
    NP_ = 4
    LAG_T, LAG_O = 3, 4
    KG, VG = 2 * KC, KVC
    PROJ = KG + VG
    wk, wv = m.used, m.used + 1
    sg = m.sig
    mm = sg["mm"]
    m.free_at += [mm.base + B * PROJ] * 2
    m.used = len(m.free_at)
    ctx_t = sb(f"ctx{name}", [P, KX, NKV], F32)
    ctx_p = sb(f"ctxp{name}", [P, 2, KX, NKV], F32R)
    kt = sb(f"kt{name}", [P, 2, KC, NKV], F32R)
    vv = sb(f"vv{name}", [P, KVC, C], F32)
    qb = sb(f"qb{name}", [P, KC, S], F32)
    qp = sb(f"qp{name}", [P, 2, H, S], F32R)
    pr = sb(f"pr{name}", [S, NP_, KVC * P], F32)
    pt = sb(f"pt{name}", [P, 2, KVC, S], F32)
    smax = sb(f"smax{name}", [S, NP_, 2], F32)
    ssum = sb(f"ssum{name}", [S, NP_], F32)
    spans = (slice(0, BANK), slice(BANK, NKV))

    def at(name, b, per, n):
        return sg[name].base + b * per + n

    def scores(h):
        return ps[0:S, 2 * (h % 2):2 * (h % 2) + 2, :].rearrange("s n k -> s (n k)")[:, 0:NKV]

    def k_bank(i):
        c, n = divmod(i, 2)
        return ps[:, i % 4, 0:spans[n].stop - spans[n].start]

    def v_rows(c):
        return P if c < KVC - 1 else KVR

    def v_bank(c, r):
        return ps[0:r, 4 + c % 4, 0:C]

    def rows_of(ri):
        return slice(ri * D, (ri + 1) * D)

    def padded(part, ri):
        return qp[rows_of(ri), part].rearrange("p (c i) s -> p i c s", i=HPC)[:, ri]

    def loop(eng, body):
        with eng.Fori(0, B - 1) as b:
            body(b, False)
        body(B - 1, True)

    with nc.Block() as block:

        @block.sync
        def _(sp):
            m.load_blocks(sp, wk + RING)
            ld = sg["ctx_load"]
            sp.dma_start(ctx_t[:, :, :], m.d["ctx"][0]).then_inc(ld.sem, 16)
            with sp.Fori(0, B - 1) as b:
                sp.wait_ge(sg["ctx_low"].sem, at("ctx_low", b, 1, 1))
                sp.dma_start(ctx_t[:, :, :], m.d["ctx"][b + 1]).then_inc(ld.sem, 16)
            m.load_blocks(sp, m.used + RING)

        @block.tensor
        def _(pe):
            m.wait_pair(pe, wv)

            def body(b, last):
                pe.wait_ge(sg["ctx_low"].sem, at("ctx_low", b, 1, 1))
                pe.wait_ge(sg["p_exp"].sem, at("p_exp", b, H, 0))
                for i in range(KG):
                    c, n = divmod(i, 2)
                    if i >= 4:
                        pe.wait_ge(sg["k_low"].sem, at("k_low", b, KG, i - 3))
                    product(pe, k_bank(i), [(lambda a, k=k: m.pair(wk, a)[:, k, c * P:(c + 1) * P],
                                             lambda x, k=k: ctx_p[:, x, k, spans[n]]) for k in range(KX)]).then_inc(mm.sem, 1)
                pe.wait_ge(sg["pt_out"].sem, at("pt_out", b, H, 0))
                pe.wait_ge(sg["o_out"].sem, at("o_out", b, KC, 0))
                for c in range(KVC):
                    if c >= 4:
                        pe.wait_ge(sg["v_out"].sem, at("v_out", b, VG, c - 3))
                    r = v_rows(c)
                    product(pe, v_bank(c, r), [(lambda a, k=k: ctx_p[:, a, k, c * P:c * P + r],
                                                lambda x, k=k: m.pair(wv, x)[:, k, :]) for k in range(KX)]).then_inc(mm.sem, 1)
                pe.wait_ge(sg["q_low"].sem, at("q_low", b, 1, 1))
                pe.wait_ge(sg["k_low"].sem, at("k_low", b, KG, KG))
                for i in range(H + LAG_O):
                    if i < H:
                        if i >= 2:
                            if clip:
                                pe.wait_ge(sg["s_clip"].sem, at("s_clip", b, 2 * H, 2 * (i - 2) + 1))
                            else:
                                pe.wait_ge(sg["p_exp"].sem, at("p_exp", b, H, i - 1))
                        for s in spans:
                            last = product(pe, scores(i)[:, s], [(lambda a: qp[:, a, i, :], lambda x: kt[:, x, i // HPC, s])])
                        last.then_inc(sg["s_mm"].sem, 1)
                    h = i - LAG_T
                    if 0 <= h < H:
                        if h == 0:
                            pe.wait_ge(sg["v_out"].sem, at("v_out", b, VG, VG))
                        pe.wait_ge(sg["p_norm"].sem, at("p_norm", b, H, h + 1))
                        pe.wait_ge(sg["pt_out"].sem, at("pt_out", b, H, h))
                        for c in range(KVC):
                            last = pe.transpose(ps[:, 4 + c // 3, (c % 3) * S:(c % 3 + 1) * S],
                                                pr[:, h % NP_, c * P:(c + 1) * P], m.ident[0:S, 0:S])
                        last.then_inc(sg["p_turn"].sem, 1)
                    h = i - LAG_O
                    if 0 <= h < H:
                        c, r = h // HPC, (h % HPC) * D
                        pe.wait_ge(sg["pt_out"].sem, at("pt_out", b, H, h + 1))
                        if h % HPC == 0 and c >= 2:
                            pe.wait_ge(sg["o_out"].sem, at("o_out", b, KC, c - 1))
                        for k in range(KVC):
                            last = pe.matmul(ps[r:r + D, 6 + c % 2, 0:S], vv[:, k, h * D:(h + 1) * D],
                                             pt[:, h % 2, k, :], start=k == 0, stop=k == KVC - 1)
                        last.then_inc(sg["o_mm"].sem, 1)
            loop(pe, body)

        @block.scalar
        def _(act):
            m.split_high(act, wv + 1)

            def split(b):
                act.wait_ge(sg["ctx_load"].sem, at("ctx_load", b, 16, 16))
                act.activation(ctx_p[:, 0], ctx_t[:, :, :], ACT.Copy).then_inc(sg["ctx_high"].sem, 1)

            split(0)

            def body(b, last):
                act.wait_ge(sg["q_copy"].sem, at("q_copy", b, 1, 1))
                for ri in range(HPC):
                    act.activation(padded(0, ri), qb[rows_of(ri)], ACT.Copy).then_inc(sg["q_high"].sem, 1)
                for i in range(KG):
                    c, n = divmod(i, 2)
                    act.wait_ge(mm.sem, mm.base + b * PROJ + i + 1)
                    if bias:
                        ins = act.activation(kt[:, 0, c, spans[n]], k_bank(i), ACT.Identity, bias=m.column("bk", c))
                    else:
                        ins = act.activation(kt[:, 0, c, spans[n]], k_bank(i), ACT.Copy)
                    ins.then_inc(sg["k_out"].sem, 1)
                for c in range(KVC):
                    r = v_rows(c)
                    act.wait_ge(mm.sem, mm.base + b * PROJ + KG + c + 1)
                    act.activation(vv[0:r, c, :], v_bank(c, r), ACT.Copy).then_inc(sg["v_out"].sem, 1)
                for i in range(H + LAG_T):
                    h = i - LAG_T
                    if 0 <= h < H:
                        act.wait_ge(sg["p_turn"].sem, at("p_turn", b, H, h + 1))
                        if h >= 2:
                            act.wait_ge(sg["o_mm"].sem, at("o_mm", b, H, h - 1))
                        act.activation(pt[:, h % 2].rearrange("p (n k) s -> p n (k s)", n=2), ps[:, 4:6, 0:3 * S],
                                       ACT.Copy).then_inc(sg["pt_out"].sem, 1)
                    if i < H:
                        act.wait_ge(sg["s_max"].sem, at("s_max", b, H, i + 1))
                        if i >= NP_:
                            act.wait_ge(sg["p_turn"].sem, at("p_turn", b, H, i - NP_ + 1))
                        to = pr[:, i % NP_, 0:NKV]
                        act.activation(to, to if clip else scores(i), ACT.Exp, bias=smax[:, i % NP_, 1:2],
                                       accum_out=ssum[:, i % NP_:i % NP_ + 1]).then_inc(sg["p_exp"].sem, 1)
                    if i == 3 and not last:
                        split(b + 1)
            loop(act, body)
            m.split_high(act, m.used + 1)

        @block.vector
        def _(dve):
            m.split_low(dve, wv + 1)
            ch = sg["dve_chain"]
            dve.memset(pr[:, :, NKV:], 0.0).then_inc(ch.sem, 1)
            dve.memset(vv[:, KVC - 1, :], 0.0).then_inc(ch.sem, 1)
            dve.memset(qp[:, :, :, :].bitcast(F32), 0.0).then_inc(ch.sem, 1)
            dve.wait_ge(ch.sem, ch.base + 3)

            def split(b):
                dve.wait_ge(sg["ctx_high"].sem, at("ctx_high", b, 1, 1))
                dve.tensor_tensor(ctx_p[:, 1], ctx_t[:, :, :], ctx_p[:, 0].bitcast(F32), ALU.subtract).then_inc(sg["ctx_low"].sem, 1)

            split(0)

            def body(b, last):
                dve.wait_ge(sg["s_mm"].sem, at("s_mm", b, H, 0))
                dve.tensor_scalar(qb[:, :, :], q[:, :, bass.ds(b * S, S)], 1.0, None, ALU.mult).then_inc(sg["q_copy"].sem, 1)
                for ri in range(HPC):
                    dve.wait_ge(sg["q_high"].sem, at("q_high", b, HPC, ri + 1))
                    ins = dve.tensor_tensor(padded(1, ri), qb[rows_of(ri)], padded(0, ri).bitcast(F32), ALU.subtract)
                ins.then_inc(sg["q_low"].sem, 1)
                for i in range(KG):
                    c, n = divmod(i, 2)
                    dve.wait_ge(sg["k_out"].sem, at("k_out", b, KG, i + 1))
                    hi = kt[:, 0, c, spans[n]].bitcast(F32)
                    if bias:
                        ins = dve.scalar_tensor_tensor(kt[:, 1, c, spans[n]], k_bank(i), m.column("bk", c), hi, ALU.add, ALU.subtract)
                    else:
                        ins = dve.tensor_tensor(kt[:, 1, c, spans[n]], k_bank(i), hi, ALU.subtract)
                    ins.then_inc(sg["k_low"].sem, 1)

                def output(c):
                    dve.wait_ge(sg["o_mm"].sem, at("o_mm", b, H, (c + 1) * HPC))
                    to = o[:, c, bass.ds(b * S, S)]
                    if bias:
                        ins = dve.tensor_scalar(to, ps[:, 6 + c % 2, 0:S], m.column("bv", c), None, ALU.add)
                    else:
                        ins = dve.tensor_scalar(to, ps[:, 6 + c % 2, 0:S], 1.0, None, ALU.mult)
                    ins.then_inc(sg["o_out"].sem, 1)

                def recip(h):
                    if h < 0:
                        return
                    dve.wait_ge(sg["p_exp"].sem, at("p_exp", b, H, h + 1))
                    s_ = ssum[:, h % NP_:h % NP_ + 1]
                    dve.reciprocal(s_, s_).then_inc(sg["norm_rec"].sem, 1)

                outputs = 0
                for i in range(H + 1):
                    if i < H:
                        dve.wait_ge(sg["s_mm"].sem, at("s_mm", b, H, i + 1))
                        t = smax[:, i % NP_]
                        if clip:
                            x_, n0 = sg["s_clip"], at("s_clip", b, 2 * H, 2 * i)
                            to = pr[:, i % NP_, 0:NKV]
                            if i >= NP_:
                                dve.wait_ge(sg["p_turn"].sem, at("p_turn", b, H, i - NP_ + 1))
                            dve.tensor_scalar(to, scores(i), -CLAMP, None, ALU.max, ALU.max, accum_out=t[:, 0:1]).then_inc(x_.sem, 1)
                            recip(i - 1)
                            dve.wait_ge(x_.sem, n0 + 1)
                            dve.tensor_scalar(t[:, 1:2], t[:, 0:1], CLAMP, -1.0, ALU.min, ALU.mult).then_inc(x_.sem, 1)
                            dve.tensor_scalar(to, to, CLAMP, None, ALU.min).then_inc(sg["s_max"].sem, 1)
                        else:
                            if i >= NP_:
                                dve.wait_ge(sg["p_turn"].sem, at("p_turn", b, H, i - NP_ + 1))
                            dve.tensor_reduce(t[:, 1:2], scores(i), AX.X, ALU.max, negate=True).then_inc(sg["s_max"].sem, 1)
                            recip(i - 1)
                    else:
                        recip(i - 1)
                    h = i - 1
                    if 0 <= h < H:
                        s_ = ssum[:, h % NP_:h % NP_ + 1]
                        dve.wait_ge(sg["norm_rec"].sem, at("norm_rec", b, H, h + 1))
                        dve.tensor_scalar(pr[:, h % NP_, 0:NKV], pr[:, h % NP_, 0:NKV], s_, None, ALU.mult).then_inc(sg["p_norm"].sem, 1)
                    if i == 4 and not last:
                        split(b + 1)
                    if i - 1 - LAG_O >= (outputs + 1) * HPC - 1:
                        output(outputs)
                        outputs += 1
                for c in range(outputs, KC):
                    output(c)
            loop(dve, body)
            m.split_low(dve, m.used + 1)

    mm.advance(B * PROJ)
    for s, n in (("ctx_load", 16 * B), ("ctx_high", B), ("ctx_low", B), ("k_out", B * KG), ("k_low", B * KG), ("v_out", B * VG),
                 ("q_copy", B), ("q_high", B * HPC), ("q_low", B), ("s_mm", B * H),
                 ("s_clip", 2 * B * H if clip else 0), ("s_max", B * H), ("p_exp", B * H),
                 ("p_norm", B * H), ("norm_rec", B * H), ("p_turn", B * H), ("pt_out", B * H),
                 ("o_mm", B * H), ("o_out", B * KC), ("dve_chain", 3)):
        sg[s].advance(n)


def split_pair(m, t, pair):
    high = m.sig["in_high"]
    with m.nc.Block() as block:

        @block.scalar
        def _(act):
            for k in range(KC):
                act.activation(pair[:, 0, k], t[:, k], ACT.Copy).then_inc(high.sem, 1)

        @block.vector
        def _(dve):
            for k in range(KC):
                dve.wait_ge(high.sem, high.base + k + 1)
                dve.tensor_tensor(pair[:, 1, k], t[:, k], pair[:, 0, k].bitcast(F32), ALU.subtract)

    high.advance(KC)


def gates(m, u, gate, y, sb):
    nc, ps, g = m.nc, m.ps, m.sig
    mm, dv, ac = g["mm"], g["dve_chain"], g["act_out"]
    cen = sb("cen", [P, KC, E], F32)
    b2 = sb("b2", [E, C], F32)
    before = sb("before", [P, E, E], F32)
    pick = sb("pick", [E, E, P], F32)
    sc = sb("sc", [S, B, E], F32)
    cmp = sb("cmp", [S, B, E, E], F32)
    eq = sb("eq", [S, B, E, E], F32)
    rank = sb("rank", [S, B, E], F32)
    den = sb("den", [S, B], F32)
    gt = sb("gt", [E, T], F32)
    with nc.Block() as block:

        @block.sync
        def _(sp):
            ld = g["const_load"]
            sp.dma_start(cen[:, :, :], m.d["centroids"]).then_inc(ld.sem, 16)
            sp.dma_start(b2[:, :], m.d["b2"]).then_inc(ld.sem, 16)
            sp.dma_start(before[:, :, :], m.d["before"]).then_inc(ld.sem, 16)
            sp.dma_start(pick[:, :, :], m.d["pick"]).then_inc(ld.sem, 16)

        @block.tensor
        def _(pe):
            ld = g["const_load"]
            pe.wait_ge(ld.sem, ld.base + 64)
            for b in range(B):
                for k in range(KC):
                    last = pe.matmul(ps[0:S, 0, b * E:(b + 1) * E], u[:, k, b * S:(b + 1) * S], cen[:, k, :],
                                     start=k == 0, stop=k == KC - 1)
            last.then_inc(mm.sem, 1)
            pe.wait_ge(dv.sem, dv.base + 12)
            for b in range(B):
                last = pe.transpose(ps[0:E, 1 + b // 4, (b % 4) * S:(b % 4 + 1) * S], rank[:, b, :], m.ident[0:S, 0:S])
            last.then_inc(mm.sem, 1)
            pe.wait_ge(dv.sem, dv.base + 14)
            for j in range(2 * E):
                e, n = divmod(j, 2)
                if j >= 4:
                    pe.wait_ge(ac.sem, ac.base + 1 + j - 3)
                pe.matmul(ps[:, 3 + j % 4, 0:HT], pick[:, e, :], gt[:, halves(n)], start=True, stop=True).then_inc(mm.sem, 1)
            for j in range(2 * KC):
                c, n = divmod(j, 2)
                if j < 4:
                    pe.wait_ge(ac.sem, ac.base + 1 + 2 * E - 3 + j)
                else:
                    pe.wait_ge(dv.sem, dv.base + 14 + j - 3)
                pe.matmul(ps[:, 3 + j % 4, 0:HT], b2[:, c * P:(c + 1) * P], gt[:, halves(n)], start=True, stop=True).then_inc(mm.sem, 1)

        @block.scalar
        def _(act):
            act.wait_ge(mm.sem, mm.base + 1)
            act.activation(sc[:, :, :], ps[0:S, 0, 0:B * E].rearrange("s (b e) -> s b e", e=E), ACT.Exp, scale=-1.0).then_inc(ac.sem, 1)
            for j in range(2 * E):
                e, n = divmod(j, 2)
                act.wait_ge(mm.sem, mm.base + 3 + j)
                act.activation(gate[:, e * T + n * HT:e * T + (n + 1) * HT], ps[:, 3 + j % 4, 0:HT], ACT.Copy).then_inc(ac.sem, 1)

        @block.vector
        def _(dve):
            n = 0

            def step(ins):
                nonlocal n
                n += 1
                ins.then_inc(dv.sem, 1)
                dve.wait_ge(dv.sem, dv.base + n)

            dve.wait_ge(g["const_load"].sem, g["const_load"].base + 64)
            dve.wait_ge(ac.sem, ac.base + 1)
            step(dve.tensor_scalar(sc[:, :, :], sc[:, :, :], 1.0, None, ALU.add))
            step(dve.reciprocal(sc[:, :, :], sc[:, :, :]))
            for b in range(B):
                mine = sc[:, b, :].unsqueeze(2).to_broadcast([S, E, E])
                other = sc[:, b, :].unsqueeze(1).to_broadcast([S, E, E])
                dve.tensor_tensor(cmp[:, b], other, mine, ALU.is_gt)
                ins = dve.tensor_tensor(eq[:, b], other, mine, ALU.is_equal)
            step(ins)
            step(dve.tensor_tensor(eq[:, :, :, :], eq[:, :, :, :],
                                   before[0:S].unsqueeze(1).to_broadcast([S, B, E, E]), ALU.mult))
            step(dve.tensor_tensor(cmp[:, :, :, :], cmp[:, :, :, :], eq[:, :, :, :], ALU.add))
            step(dve.tensor_reduce(rank[:, :, :], cmp[:, :, :, :], AX.X, ALU.add))
            step(dve.tensor_scalar(rank[:, :, :], rank[:, :, :], 1.5, None, ALU.is_lt))
            step(dve.tensor_tensor(rank[:, :, :], rank[:, :, :], sc[:, :, :], ALU.mult))
            step(dve.tensor_reduce(den[:, :], rank[:, :, :], AX.X, ALU.add))
            step(dve.reciprocal(den[:, :], den[:, :]))
            step(dve.tensor_tensor(rank[:, :, :], rank[:, :, :], den[:, :].unsqueeze(2).to_broadcast([S, B, E]), ALU.mult))
            step(dve.engine_nop())
            dve.wait_ge(mm.sem, mm.base + 2)
            for i in range(2):
                dve.tensor_copy(gt[:, halves(i)], ps[0:E, 1 + i, 0:HT]).then_inc(dv.sem, 1)
            for j in range(2 * KC):
                c, i = divmod(j, 2)
                dve.wait_ge(mm.sem, mm.base + 3 + 2 * E + j)
                dve.tensor_copy(y[:, c, halves(i)], ps[:, 3 + j % 4, 0:HT]).then_inc(dv.sem, 1)

    mm.advance(2 + 2 * E + 2 * KC)
    ac.advance(1 + 2 * E)
    dv.advance(14 + 2 * KC)
    g["const_load"].advance(64)


def values(m, u, v):
    nc, ps, mm, done = m.nc, m.ps, m.sig["mm"], m.sig["act_out"]
    w = m.used
    m.free_at.append(mm.base + B)
    m.used = len(m.free_at)
    with nc.Block() as block:

        @block.sync
        def _(sp):
            m.load_blocks(sp, m.used + RING)

        @block.tensor
        def _(pe):
            m.wait_pair(pe, w)
            for b in range(B):
                product(pe, ps[0:S, b, 0:C], [(lambda a, k=k: u[:, a, k, b * S:(b + 1) * S],
                                               lambda x, k=k: m.pair(w, x)[:, k, :]) for k in range(KC)]).then_inc(mm.sem, 1)

        @block.scalar
        def _(act):
            m.split_high(act, m.used + 1)
            for b in range(B):
                act.wait_ge(mm.sem, mm.base + b + 1)
                act.activation(v[:, b, :], ps[0:S, b, 0:C], ACT.Copy).then_inc(done.sem, 1)

        @block.vector
        def _(dve):
            m.split_low(dve, m.used + 1)

    mm.advance(B)
    done.advance(B)


def retention(m, q, k_, v, st, decay):
    nc, ps, mm, dv = m.nc, m.ps, m.sig["mm"], m.sig["dve_out"]
    x = m.x
    with nc.Block() as block:

        @block.tensor
        def _(pe):
            for b in range(B):
                for k in range(KC):
                    last = pe.matmul(ps[0:S, b // 4, (b % 4) * S:(b % 4 + 1) * S], k_[:, k, b * S:(b + 1) * S],
                                     q[:, k, b * S:(b + 1) * S], start=k == 0, stop=k == KC - 1)
                last.then_inc(mm.sem, 1)
            for b in range(B):
                pe.wait_ge(dv.sem, dv.base + 1 + b // 4)
                if b >= 4:
                    pe.wait_ge(dv.sem, dv.base + 2 + b - 3)
                for c in range(KC):
                    last = pe.matmul(ps[:, 4 + b % 4, c * S:(c + 1) * S], v[:, b, c * P:(c + 1) * P], st[:, b, :],
                                     start=True, stop=True)
                last.then_inc(mm.sem, 1)

        @block.vector
        def _(dve):
            for n in range(2):
                dve.wait_ge(mm.sem, mm.base + 4 * (n + 1))
                dve.tensor_tensor(st[:, 4 * n:4 * n + 4, :], ps[0:S, n, 0:HT].rearrange("s (b t) -> s b t", t=S),
                                  decay[:, :].unsqueeze(1).to_broadcast([S, 4, S]), ALU.mult).then_inc(dv.sem, 1)
            for b in range(B):
                dve.wait_ge(mm.sem, mm.base + B + b + 1)
                xb = x[:, :, b * S:(b + 1) * S]
                dve.tensor_tensor(xb, ps[:, 4 + b % 4, 0:HT].rearrange("p (c t) -> p c t", t=S), xb, ALU.add).then_inc(dv.sem, 1)

    mm.advance(2 * B)
    dv.advance(2 + B)


class Quantised:

    BANKS = 4

    def __init__(self, m, sb):
        self.m, self.raw = m, m.used
        self.w = sb("wq", [P, KC, C], F32)
        self.lora = sb("wlora", [P, KC, C], F32)
        self.sc = sb("wscale", [P, 2, KC, C], F32)
        self.la, self.lb = (sb(n, [32, 2, C], F32) for n in ("la", "lb"))
        self.load = [m.sig["quant_load0"], m.sig["quant_load1"]]

    def wait_loads(self, eng, i):
        eng.wait_ge(self.load[i % 2].sem, 96 * (i // 2 + 1))

    def sync(self, sp, i):
        sem, m = self.load[i % 2].sem, self.m
        for k in range(KC):
            part = m.d["scales"][i, 8 * k:8 * k + 8, :].unsqueeze(1).to_broadcast([8, 16, C])
            sp.dma_start(self.sc[:, i % 2, k, :], part).then_inc(sem, 16)
        sp.dma_start(self.la[:, i % 2, :], m.d["lora_a"][i]).then_inc(sem, 16)
        sp.dma_start(self.lb[:, i % 2, :], m.d["lora_b"][i]).then_inc(sem, 16)

    def tensor(self, pe, i, free=None):
        m = self.m
        self.wait_loads(pe, i)
        for k in range(KC):
            if free is not None:
                free(k)
            pe.matmul(m.ps[:, 8 - KC + k, 0:C], self.la[:, i % 2, k * P:(k + 1) * P], self.lb[:, i % 2, :],
                      start=True, stop=True).then_inc(m.sig["lora_mm"].sem, 1)

    def scalar(self, act, i, k):
        m, dv = self.m, self.m.sig["dve_chain"]
        act.wait_ge(dv.sem, dv.base + 2 * KC + k + 1)
        ins = act.activation(m.pair(self.raw + i, 0)[:, k], self.w[:, k], ACT.Copy)
        if k == KC - 1:
            ins.then_inc(m.sig["w_high"].sem, 1)

    def vector(self, dve, i):
        m, dv, out, lo = self.m, self.m.sig["dve_chain"], self.m.sig["lora_out"], self.m.sig["lora_mm"]
        w, raw = self.w, self.raw + i
        m.wait_block(dve, raw)
        self.wait_loads(dve, i)
        for k in range(KC):
            dve.tensor_scalar(w[:, k, :], m.slot(raw)[:, k, :].bitcast(I32), 1 / 7.5, -1.0, ALU.mult, ALU.add).then_inc(dv.sem, 1)
        for k in range(KC):
            dve.wait_ge(lo.sem, KC * i + k + 1)
            dve.tensor_scalar(self.lora[:, k, :], m.ps[:, 8 - KC + k, 0:C], 1.0, None, ALU.mult).then_inc(out.sem, 1)
        for k in range(KC):
            dve.wait_ge(dv.sem, dv.base + k + 1)
            dve.tensor_tensor(w[:, k, :], w[:, k, :], self.sc[:, i % 2, k, :], ALU.mult).then_inc(dv.sem, 1)
        for k in range(KC):
            dve.wait_ge(dv.sem, dv.base + KC + k + 1)
            dve.wait_ge(out.sem, KC * i + k + 1)
            dve.tensor_tensor(w[:, k, :], w[:, k, :], self.lora[:, k, :], ALU.add).then_inc(dv.sem, 1)

    def vector_low(self, dve, i):
        m = self.m
        dve.wait_ge(m.sig["w_high"].sem, self.raw + i + 1)
        dve.tensor_tensor(m.pair(self.raw + i, 1), self.w[:, :, :], m.pair(self.raw + i, 0).bitcast(F32),
                          ALU.subtract).then_inc(m.sig["w_low"].sem, 1)

    def advance(self, i):
        m = self.m
        m.high = m.low = self.raw + i + 1
        m.sig["dve_chain"].advance(3 * KC)

    def first(self):
        m = self.m
        with m.nc.Block() as block:

            @block.sync
            def _(sp):
                self.sync(sp, 0)
                self.sync(sp, 1)

            @block.tensor
            def _(pe):
                self.tensor(pe, 0)
                self.tensor(pe, 1, lambda k: pe.wait_ge(m.sig["lora_out"].sem, k + 1))

            @block.scalar
            def _(act):
                for k in range(KC):
                    self.scalar(act, 0, k)

            @block.vector
            def _(dve):
                self.vector(dve, 0)
                self.vector_low(dve, 0)

        self.advance(0)


def build(nc, d):
    with ExitStack() as ctx:
        m = Decoder(nc, ctx, d)
        x, par, g = m.x, m.par, m.sig

        def buffers(stack):
            return lambda name, shape, dt: stack.enter_context(nc.sbuf_tensor(name, shape, dt))

        for n in ("w_tk", "w_tv", "w_tr", "w_cr"):
            m.add_block(rows(d[n], 0, 0))
        for second, j in mlp_order():
            m.add_block(rows(d["w_cv"], j * C, 0) if second else rows(d["w_ck"], 0, j * C))
        m.add_block(rows(d["Wq"], 0, 0))
        m.add_block(rows(d["Wk"], 0, 0, KX), KX)
        m.add_block(rows(d["Wv"], 0, 0, KX), KX)
        m.add_block(rows(d["Wo"], 0, 0))
        for e in range(E):
            for second, j in mlp_order():
                m.add_block(rows(d["W2"][e], j * C, 0) if second else rows(d["W1"][e], 0, j * C))
        for n in ("rq", "rk", "rv"):
            m.add_block(rows(d[n], 0, 0))
        for j in range(2):
            m.add_block(rows(d["xWq"], 0, j * C))
        for j in range(2):
            for n in ("xWk", "xWv"):
                m.add_block(rows(d[n], 0, j * C, KX), KX)
            m.add_block(rows(d["xWo"], j * C, 0))
        for i in range(6):
            m.add_block(rows(d["qw"][i], 0, 0), KC, I32)

        free = {"tensor": ("s_mm",), "scalar": ("p_exp", "pt_out"), "vector": ("o_out",)}
        with nc.Block() as block:

            @block.tensor
            def _(pe):
                for s in free["tensor"]:
                    pe.sem_inc(g[s].sem, 1)

            @block.scalar
            def _(act):
                for s in free["scalar"]:
                    act.sem_inc(g[s].sem, 1)
                m.split_high(act, 1)

            @block.sync
            def _(sp):
                sp.dma_start(x[:, :, :], d["x"]).then_inc(g["x_load"].sem, 16)
                sp.dma_start(par[:, :], d["params"]).then_inc(g["param_load"].sem, 16)
                sp.dma_start(m.ident[:, :], d["ident"]).then_inc(g["const_load"].sem, 16)
                m.load_blocks(sp, RING)

            @block.vector
            def _(dve):
                for s in free["vector"]:
                    dve.sem_inc(g[s].sem, 1)
                dve.memset(m.mean_w[:, :], 1.0 / C)
                dve.memset(m.eps[:, :], EPS)
                dve.wait_ge(g["x_load"].sem, 16)
                dve.wait_ge(g["param_load"].sem, 16)
                dve.wait_ge(g["const_load"].sem, 16)
                m.split_low(dve, 1)

        g["const_load"].advance(16)
        for names in free.values():
            for s in names:
                g[s].advance(1)

        def add_to(dst, bias=None, bi=0):
            def evac(dve, c, n, bank):
                to = dst[:, c, halves(n)]
                if bias is None:
                    return dve.tensor_tensor(to, bank, to, ALU.add)
                return dve.scalar_tensor_tensor(to, bank, m.column(bias, bi + c), to, ALU.add, ALU.add)
            return evac

        def copy_to(dst, func=ACT.Copy, **kw):
            def evac(act, c, n, bank):
                return act.activation(dst[:, c, halves(n)], bank, func, **{k: (v(c) if callable(v) else v) for k, v in kw.items()})
            return evac

        with ExitStack() as st:
            sb = buffers(st)
            xl, h = (sb(n, [P, KC, T], F32) for n in ("xl", "h"))
            std = sb("std", [P, T], F32)
            keep = sb("keep", [P, 3 * KC], F32)
            with ExitStack() as st1:
                k_, v_ = (buffers(st1)(n, [P, KC, T], F32) for n in ("tk", "tv"))
                with ExitStack() as st2:
                    sb2 = buffers(st2)
                    tmp = sb2("mixed", [P, KC, T], F32)
                    pair = [sb2(f"mixp{i}", [P, 2, KC, T], F32R) for i in range(2)]
                    layer_norm(m, x, xl, tmp, std)
                    layer_norm(m, xl, h, tmp, std, "ln1_g", "ln1_b")
                    mixed_linears(m, h, [("mix_k", copy_to(k_)), ("mix_v", copy_to(v_)), ("mix_r", copy_to(h, ACT.Sigmoid))],
                                  pair, tmp, keep)
                with ExitStack() as st2:
                    wkv(m, k_, v_, h, xl, buffers(st2))
            with ExitStack() as st1:
                sb1 = buffers(st1)
                r2 = sb1("r2", [P, KC, T], F32)
                hid = sb1("hid", [P, 2, 2, KC, T], F32R)
                pre = sb1("pre", [P, KC, T], F32)
                ck = sb1("ck", [P, 2, KC, T], F32R)
                layer_norm(m, xl, h, pre, std, "ln2_g", "ln2_b")
                mixed_linears(m, h, [("cmix_r", copy_to(r2, ACT.Sigmoid)), ("cmix_k", None)], [hid[:, 0], ck], pre, keep)
                mlp(m, ck, h, pre[:, :, :].rearrange("p k (n t) -> p (k n) t", n=2), hid, 1)
                with nc.Block() as block:
                    ch = g["dve_chain"]

                    @block.vector
                    def _(dve):
                        dve.tensor_tensor(h[:, :, :], h[:, :, :], r2[:, :, :], ALU.mult).then_inc(ch.sem, 1)
                        dve.tensor_tensor(x[:, :, :], x[:, :, :], xl[:, :, :], ALU.add).then_inc(ch.sem, 1)
                        dve.wait_ge(ch.sem, ch.base + 2)
                        dve.tensor_tensor(x[:, :, :], x[:, :, :], h[:, :, :], ALU.add)
                ch.advance(2)
        if STAGES <= 1:
            return finish(m)

        def cross(parts, D, bo, name):
            with ExitStack() as st:
                sb = buffers(st)
                q = sb("q" + name, [P, KC * parts, T], F32)
                bq = sb("bq" + name, [P, KC], F32)
                with ExitStack() as st2:
                    sb2 = buffers(st2)
                    u, tmp = (sb2(n + name, [P, KC, T], F32) for n in ("xu", "xt"))
                    pair = sb2("xp" + name, [P, 2, KC, T], F32R)
                    std = sb2("xs" + name, [P, T], F32)
                    layer_norm(m, x, u, tmp, std, pair=pair)
                    w = m.used
                    if parts == 1:
                        with nc.Block() as block:
                            @block.vector
                            def _(dve):
                                dve.tensor_scalar(bq[:, :], par[:, COL["bq"]:COL["bq"] + KC], D ** -0.5, None, ALU.mult)
                        evac = copy_to(q, ACT.Identity, scale=D ** -0.5, bias=lambda c: bq[:, c:c + 1])
                    else:
                        evac = copy_to(q, ACT.Copy, scale=D ** -0.5)
                    linear(m, pair, [w + i for i in range(parts)], evac)
                for i in range(parts):
                    with ExitStack() as st2:
                        sb2 = buffers(st2)
                        o = sb2(f"o{name}{i}", [P, KC, T], F32)
                        with ExitStack() as st3:
                            attention(m, q[:, i * KC:(i + 1) * KC], o, D, parts == 1, parts == 1, f"{name}{i}", buffers(st3))
                        pair = sb2(f"op{name}{i}", [P, 2, KC, T], F32R)
                        split_pair(m, o, pair)
                        linear(m, pair, [m.used], add_to(x, bo if i == 0 else None), "vector")

        cross(1, 32, "bo", "a")
        if STAGES <= 2:
            return finish(m)

        with ExitStack() as st:
            sb = buffers(st)
            pre, y = (sb(n, [P, KC, T], F32) for n in ("eu", "ey"))
            pair = sb("eup", [P, 2, KC, T], F32R)
            gate = sb("gate", [P, E * T], F32)
            b1 = sb("b1", [P, FF // P], F32)
            with ExitStack() as st2:
                sb2 = buffers(st2)
                std = sb2("es", [P, T], F32)
                layer_norm(m, x, pre, y, std, pair=pair)
                gates(m, pre, gate, y, sb2)
            hid = sb("ehid", [P, 2, 2, KC, T], F32R)
            mlp(m, pair, y, pre[:, :, :].rearrange("p k (n t) -> p (k n) t", n=2), hid, E, gate, b1, clear=False)
            with nc.Block() as block:
                @block.vector
                def _(dve):
                    dve.tensor_tensor(x[:, :, :], x[:, :, :], y[:, :, :], ALU.add)
        if STAGES <= 3:
            return finish(m)

        with ExitStack() as st:
            sb = buffers(st)
            u, q, k_ = (sb(n, [P, KC, T], F32) for n in ("ru", "rqt", "rkt"))
            v = sb("rvt", [S, B, C], F32)
            sT = sb("rst", [S, B, S], F32)
            std = sb("rs", [P, T], F32)
            theta = sb("theta", [P, KC], F32)
            decay = sb("decay", [S, S], F32)
            pair = sb("rp", [P, 2, KC, T], F32R)
            layer_norm(m, x, u, q, std, pair=pair)
            ld = g["const_load"]
            with nc.Block() as block:
                @block.sync
                def _(sp):
                    sp.dma_start(decay[:, :], d["decay"]).then_inc(ld.sem, 16)

                @block.scalar
                def _(act):
                    act.activation(theta[:, :], par[:, COL["theta"]:COL["theta"] + KC], ACT.Exp, scale=0.0)
                    act.wait_ge(ld.sem, ld.base + 16)
            ld.advance(16)
            w = m.used
            scaled = dict(scale=lambda c: theta[:, c:c + 1])
            linear(m, pair, [w], copy_to(q, ACT.Identity, **scaled))
            linear(m, pair, [w + 1], copy_to(k_, ACT.Identity, **scaled))
            values(m, pair, v)
            retention(m, q, k_, v, sT, decay)
        if STAGES <= 4:
            return finish(m)

        cross(2, 64, "xbo", "b")
        if STAGES <= 5:
            return finish(m)

        with ExitStack() as st:
            sb = buffers(st)
            u, h, t_ = (sb(n, [P, KC, T], F32) for n in ("fu", "fh", "ft"))
            std = sb("fs", [P, T], F32)
            pair = sb("fp", [P, 2, KC, T], F32R)
            weights = Quantised(m, sb)
            weights.first()
            layer_norm(m, x, h, t_, std, pair=pair)
            for blk in range(3):
                i = 2 * blk
                if blk > 0:
                    split_pair(m, h, pair)
                linear(m, pair, [m.used], copy_to(u, ACT.Identity, bias=lambda c: m.column("qbias", i * KC + c)),
                       "scalar", weights, i)
                layer_norm(m, u, u, t_, std, "gamma", "beta", ACT.Gelu, blk * KC, pair)
                i = 2 * blk + 1
                linear(m, pair, [m.used], add_to(h, "qbias", i * KC), "vector", weights, i)
            with nc.Block() as block:
                @block.vector
                def _(dve):
                    dve.tensor_tensor(x[:, :, :], x[:, :, :], h[:, :, :], ALU.add)
        finish(m)


STAGES = 99


def finish(m):
    with m.nc.Block() as block:

        @block.sync
        def _(sp):
            sp.dma_start(m.d["out"], m.x[:, :, :]).then_inc(m.sig["store"].sem, 16)
            sp.wait_ge(m.sig["store"].sem, 16)
            for w in range(m.loaded - RING, m.loaded):
                m.wait_block(sp, w)




def kernel(**inputs):
    import numpy as np
    import concourse.bacc as bacc
    from concourse.bass_utils import run_bass_kernel_spmd

    a = {k: np.asarray(v) for k, v in inputs.items()}

    def cols(v):
        return np.asarray(v).reshape(-1, P).T

    L0, X0, F0, R1, X1, F1 = "L0_attn_", "L0_xattn_", "L0_ffn_", "L1_attn_", "L1_xattn_", "L1_ffn_"
    par = {n: a[L0 + n] for n in ("time_decay", "time_first", "ln1_g", "ln1_b", "ln2_g", "ln2_b",
                                  "mix_k", "mix_v", "mix_r", "cmix_k", "cmix_r")}
    par |= {n: a[X0 + n] for n in ("bq", "bk", "bv", "bo")}
    par |= {"theta": a[R1 + "theta"], "xbo": a[X1 + "bo"], "qbias": a[F1 + "biases"],
            "gamma": a[F1 + "ln_gamma"], "beta": a[F1 + "ln_beta"], "b1": a[F0 + "b1"]}
    diff = np.arange(S)[None, :] - np.arange(S)[:, None]
    decay = np.where(diff >= 0, np.float32(0.96875) ** np.maximum(diff, 0).astype(np.float32), np.float32(0))
    arrays = {
        "x": a["x"].reshape(T, KC, P).transpose(2, 1, 0),
        "ctx": a["ctx_768"].reshape(B, NKV, KX, P).transpose(0, 3, 2, 1),
        "params": np.concatenate([cols(par[n]) for n, _ in PARAMS], axis=1),
        "ident": np.eye(P, dtype=np.float32),
        "before": np.broadcast_to(np.tri(E, E, -1, dtype=np.float32), (P, E, E)),
        "pick": np.broadcast_to(np.eye(E, dtype=np.float32)[:, :, None], (E, E, P)),
        "decay": decay.astype(np.float32),
        "centroids": a[F0 + "centroids"].reshape(E, KC, P).transpose(2, 1, 0),
        "W1": a[F0 + "W1"], "W2": a[F0 + "W2"], "b2": a[F0 + "b2"],
        "rq": a[R1 + "weight_q"], "rk": a[R1 + "weight_k"], "rv": a[R1 + "weight_v"],
        "qw": a[F1 + "qweights"].transpose(0, 2, 1),
        "scales": a[F1 + "scales"].transpose(0, 2, 1),
        "lora_a": a[F1 + "lora_a"], "lora_b": a[F1 + "lora_b"].transpose(0, 2, 1),
    }
    arrays |= {n: a[L0 + n] for n in ("w_tk", "w_tv", "w_tr", "w_ck", "w_cv", "w_cr")}
    arrays |= {n: a[X0 + n] for n in ("Wq", "Wk", "Wv", "Wo")}
    arrays |= {"x" + n: a[X1 + n] for n in ("Wq", "Wk", "Wv", "Wo")}
    nc = bacc.Bacc("TRN2", target_bir_lowering=False, num_devices=1)
    given, d = {}, {}
    for n, v in arrays.items():
        given[f"in_{n}"] = v = np.ascontiguousarray(v)
        d[n] = nc.dram_tensor(f"in_{n}", v.shape, mybir.dt.from_np(v.dtype), kind="ExternalInput").ap()
    d["out"] = nc.dram_tensor("out_x", (P, KC, T), F32, kind="ExternalOutput").ap()
    build(nc, d)
    r = run_bass_kernel_spmd(nc, [given], core_ids=[0])
    out = np.asarray(r.results[0]["out_x"])
    return np.ascontiguousarray(out.transpose(2, 1, 0).reshape(B, S, C))
```

```python
from contextlib import ExitStack

import concourse.bass as bass
from concourse import mybir
from concourse.alu_op_type import AluOpType as ALU

F32 = mybir.dt.float32
F32R = mybir.dt.float32r
I32 = mybir.dt.int32
ACT = mybir.ActivationFunctionType
AX = mybir.AxisListType

P = 128
B, S, C = 8, 100, 512
T = B * S
KC = C // P
HT = T // 2
NKV, CKV = 722, 384
KX = CKV // P
KVC = -(-NKV // P)
KVR = NKV - (KVC - 1) * P
HEADS = 16
FF = 4 * C
E = 8
RING = 2
PAIRS = 2
BANK = 512
EPS = 1e-5
NEG_INF = -1e38
CLAMP = 1e4

PARAMS = [("time_decay", KC), ("time_first", KC), ("ln1_g", KC), ("ln1_b", KC), ("ln2_g", KC), ("ln2_b", KC),
          ("mix_k", KC), ("mix_v", KC), ("mix_r", KC), ("cmix_k", KC), ("cmix_r", KC),
          ("bq", KC), ("bk", KC), ("bv", KC), ("bo", KC), ("theta", KC), ("xbo", KC),
          ("b1", E * FF // P), ("qbias", 6 * KC), ("gamma", 3 * KC), ("beta", 3 * KC)]
COL, _n = {}, 0
for _name, _w in PARAMS:
    COL[_name] = _n
    _n += _w
N_PARAMS = _n


class Signal:

    def __init__(self, ctx, nc, name):
        self.sem = ctx.enter_context(nc.semaphore(name))
        self.base = 0

    def advance(self, n):
        self.base += n


class Decoder:

    def __init__(self, nc, ctx, d):
        self.nc, self.d = nc, d
        self.ps = ctx.enter_context(nc.psum_tensor("ps", [P, 8, BANK], F32))
        self.x = ctx.enter_context(nc.sbuf_tensor("x", [P, KC, T], F32))
        self.ring = ctx.enter_context(nc.sbuf_tensor("ring", [P, RING, KC, C], F32))
        self.par = ctx.enter_context(nc.sbuf_tensor("par", [P, N_PARAMS], F32))
        self.mean_w = ctx.enter_context(nc.sbuf_tensor("mean_w", [P, P], F32))
        self.eps = ctx.enter_context(nc.sbuf_tensor("eps", [P, 1], F32))
        self.ident = ctx.enter_context(nc.sbuf_tensor("ident", [P, P], F32))
        self.pairs = ctx.enter_context(nc.sbuf_tensor("pairs", [P, PAIRS, 2, KC, C], F32R))
        names = ("param_load x_load const_load pad ctx_load store mm act_out dve_out dve_chain ln_cen ln_sq ln_std b1_copy"
                 " k_out v_out s_mm s_clip s_max p_exp p_norm p_turn pt_out o_mm o_out act_hid hid_out y_out"
                 " norm_rec w_high w_low in_high in_mid in_low hid_high hid_mul lora_mm lora_out quant_load0 quant_load1 ctx_high ctx_low k_low q_high q_low").split()
        self.sig = {n: Signal(ctx, nc, n) for n in names}
        self.block_load = [Signal(ctx, nc, f"block_load{i}") for i in range(RING)]
        self.blocks = []
        self.loaded = 0
        self.used = 0
        self.free_at = []
        self.high = self.low = 0

    def column(self, name, i):
        c = COL[name] + i
        return self.par[:, c:c + 1]


    def add_block(self, source, kc=KC, dtype=F32):
        self.blocks.append((source, kc, dtype))

    def slot(self, w):
        return self.ring[:, w % RING]

    def wait_block(self, eng, w):
        eng.wait_ge(self.block_load[w % RING].sem, 16 * (w // RING + 1))

    def load_blocks(self, sp, until):
        until = min(until, len(self.blocks))
        while self.loaded < until:
            w = self.loaded
            source, kc, dtype = self.blocks[w]
            if w >= RING:
                sp.wait_ge(self.sig["w_low"].sem, w - RING + 1)
            dst = self.slot(w)[:, 0:kc, :]
            if dtype != F32:
                dst = dst.bitcast(dtype)
            sp.dma_start(dst, source).then_inc(self.block_load[w % RING].sem, 16)
            self.loaded += 1

    def pair(self, w, part):
        return self.pairs[:, w % PAIRS, part]

    def wait_pair(self, eng, w):
        eng.wait_ge(self.sig["w_low"].sem, w + 1)

    def split_high(self, act, until):
        while self.high < min(until, len(self.blocks)) and self.blocks[self.high][2] == F32:
            w = self.high
            kc = self.blocks[w][1]
            self.wait_block(act, w)
            if w >= PAIRS:
                act.wait_ge(self.sig["mm"].sem, self.free_at[w - PAIRS])
            act.activation(self.pair(w, 0)[:, 0:kc], self.slot(w)[:, 0:kc], ACT.Copy).then_inc(self.sig["w_high"].sem, 1)
            self.high += 1

    def split_low(self, dve, until):
        while self.low < min(until, len(self.blocks)) and self.blocks[self.low][2] == F32:
            w = self.low
            kc = self.blocks[w][1]
            dve.wait_ge(self.sig["w_high"].sem, w + 1)
            dve.tensor_tensor(self.pair(w, 1)[:, 0:kc], self.slot(w)[:, 0:kc], self.pair(w, 0)[:, 0:kc].bitcast(F32),
                              ALU.subtract).then_inc(self.sig["w_low"].sem, 1)
            self.low += 1


def rows(w, r0, c0, kc=KC, cols=C):
    return w[r0:r0 + kc * P, c0:c0 + cols].rearrange("(k p) n -> p k n", p=P)


PASSES = ((0, 0), (0, 1), (1, 0))


def product(pe, bank, terms, before=None):
    for t, (w, x) in enumerate(terms):
        if before is not None:
            before(t)
        for i, (a, b) in enumerate(PASSES):
            last = pe.matmul(bank, w(a), x(b), start=t == 0 and i == 0, stop=t == len(terms) - 1 and i == 2)
    return last


def halves(n):
    return slice(n * HT, (n + 1) * HT)


def mlp_order():
    return [(0, 0), (0, 1), (1, 0), (0, 2), (1, 1), (0, 3), (1, 2), (1, 3)]


def layer_norm(m, src, dst, tmp, std, gain=None, bias=None, func=None, gi=0, pair=None):
    nc, ps, g = m.nc, m.ps, m.sig
    mm, cen, sq, sd, out, ch = g["mm"], g["ln_cen"], g["ln_sq"], g["ln_std"], g["dve_out"], g["dve_chain"]
    high, aff = g["in_high"], g["in_mid"]
    with nc.Block() as block:

        @block.tensor
        def _(pe):
            for n in range(2):
                for k in range(KC):
                    last = pe.matmul(ps[:, n, 0:HT], m.mean_w[:, :], src[:, k, halves(n)], start=k == 0, stop=k == KC - 1)
                last.then_inc(mm.sem, 1)
            for n in range(2):
                pe.wait_ge(sq.sem, sq.base + n + 1)
                for k in range(KC):
                    last = pe.matmul(ps[:, 2 + n, 0:HT], m.mean_w[:, :], tmp[:, k, halves(n)], start=k == 0, stop=k == KC - 1)
                last.then_inc(mm.sem, 1)

        @block.vector
        def _(dve):
            for n in range(2):
                dve.wait_ge(mm.sem, mm.base + n + 1)
                dve.tensor_tensor(dst[:, :, halves(n)], src[:, :, halves(n)],
                                  ps[:, n, 0:HT].unsqueeze(1).to_broadcast([P, KC, HT]), ALU.subtract).then_inc(cen.sem, 1)
            for n in range(2):
                dve.wait_ge(sd.sem, sd.base + n + 1)
                dve.reciprocal(std[:, halves(n)], std[:, halves(n)]).then_inc(ch.sem, 1)
                dve.wait_ge(ch.sem, ch.base + n + 1)
                dve.tensor_tensor(dst[:, :, halves(n)], dst[:, :, halves(n)],
                                  std[:, halves(n)].unsqueeze(1).to_broadcast([P, KC, HT]), ALU.mult).then_inc(out.sem, 1)
            if pair is not None:
                for n in range(2):
                    dve.wait_ge(high.sem, high.base + n + 1)
                    dve.tensor_tensor(pair[:, 1, :, halves(n)], dst[:, :, halves(n)],
                                      pair[:, 0, :, halves(n)].bitcast(F32), ALU.subtract)

        @block.scalar
        def _(act):
            for n in range(2):
                act.wait_ge(cen.sem, cen.base + n + 1)
                act.activation(tmp[:, :, halves(n)], dst[:, :, halves(n)], ACT.Square).then_inc(sq.sem, 1)
            for n in range(2):
                act.wait_ge(mm.sem, mm.base + n + 3)
                act.activation(std[:, halves(n)], ps[:, 2 + n, 0:HT], ACT.Sqrt, bias=m.eps[:, 0:1]).then_inc(sd.sem, 1)
            for n in range(2):
                if gain is not None:
                    act.wait_ge(out.sem, out.base + n + 1)
                    for k in range(KC):
                        act.activation(dst[:, k, halves(n)], dst[:, k, halves(n)], func or ACT.Identity,
                                       scale=m.column(gain, gi + k), bias=m.column(bias, gi + k)).then_inc(aff.sem, 1)
                if pair is not None:
                    if gain is None:
                        act.wait_ge(out.sem, out.base + n + 1)
                    else:
                        act.wait_ge(aff.sem, aff.base + KC * (n + 1))
                    act.activation(pair[:, 0, :, halves(n)], dst[:, :, halves(n)], ACT.Copy).then_inc(high.sem, 1)

    if gain is not None:
        aff.advance(2 * KC)
    if pair is not None:
        high.advance(2)
    for s, n in ((mm, 4), (cen, 2), (sq, 2), (sd, 2), (out, 2), (ch, 2)):
        s.advance(n)


def linear(m, src, blocks, evac, engine="scalar", quantised=None, layer=0, whole=None):
    nc, ps, mm = m.nc, m.ps, m.sig["mm"]
    done = m.sig["act_out"] if engine == "scalar" else m.sig["dve_out"]
    G = 2 * KC
    n_groups = G * len(blocks)
    for i, w in enumerate(blocks):
        assert w == len(m.free_at)
        m.free_at.append(mm.base + G * (i + 1))
    m.used = len(m.free_at)
    more = quantised is not None and layer < 5
    out, high, low = m.sig["lora_out"], m.sig["in_high"], m.sig["in_low"]
    with nc.Block() as block:

        @block.sync
        def _(sp):
            m.load_blocks(sp, m.used + RING)
            if quantised is not None and layer < 4:
                quantised.sync(sp, layer + 2)

        @block.tensor
        def _(pe):
            def chunk_ready(k):
                pe.wait_ge(low.sem, low.base + k + 1)

            for j in range(n_groups):
                i, g = divmod(j, G)
                c, n = divmod(g, 2)
                w = blocks[i]
                if g == 0:
                    m.wait_pair(pe, w)
                if j >= 8:
                    pe.wait_ge(done.sem, done.base + j - 7)
                if more and j >= 8 - KC:
                    pe.wait_ge(out.sem, KC * (layer + 1) + j - (8 - KC) + 1)
                product(pe, ps[:, j % 8, 0:HT],
                        before=chunk_ready if whole is not None and j == 0 else None,
                        terms=[(lambda a, k=k: m.pair(w, a)[:, k, c * P:(c + 1) * P], lambda b, k=k: src[:, b, k, halves(n)])
                         for k in range(KC)]).then_inc(mm.sem, 1)
            if quantised is not None and layer < 4:
                quantised.tensor(pe, layer + 2, lambda k: pe.wait_ge(done.sem, done.base + 8 - KC + k + 1))

        def drain(eng, split):
            split(eng, blocks[0] + 1)
            for i in range(len(blocks)):
                split(eng, blocks[i] + 2)
                for g in range(G):
                    j = i * G + g
                    eng.wait_ge(mm.sem, mm.base + j + 1)
                    evac(eng, i * KC + g // 2, g % 2, ps[:, j % 8, 0:HT]).then_inc(done.sem, 1)
                    if more and engine == "scalar" and g % 2 == 1:
                        quantised.scalar(eng, layer + 1, g // 2)

        @block.scalar
        def _(act):
            if whole is not None:
                for k in range(KC):
                    act.activation(src[:, 0, k], whole[:, k], ACT.Copy).then_inc(high.sem, 1)
            if engine == "scalar":
                drain(act, m.split_high)
            else:
                m.split_high(act, m.used + 1)
                if more:
                    for k in range(KC):
                        quantised.scalar(act, layer + 1, k)

        @block.vector
        def _(dve):
            if whole is not None:
                for k in range(KC):
                    dve.wait_ge(high.sem, high.base + k + 1)
                    dve.tensor_tensor(src[:, 1, k], whole[:, k], src[:, 0, k].bitcast(F32), ALU.subtract).then_inc(low.sem, 1)
            if more:
                quantised.vector(dve, layer + 1)
            if engine == "vector":
                drain(dve, m.split_low)
            else:
                m.split_low(dve, m.used + 1)
            if more:
                quantised.vector_low(dve, layer + 1)

    if more:
        quantised.advance(layer + 1)
    if whole is not None:
        high.advance(KC)
        low.advance(KC)
    mm.advance(n_groups)
    done.advance(n_groups)


def mix_chunk_scalar(m, act, i, name, h, tmp, pair):
    mid, high, low = m.sig["in_mid"], m.sig["in_high"], m.sig["in_low"]
    scaled = m.sig["hid_mul"]
    for k in range(KC):
        if i > 0:
            act.wait_ge(low.sem, low.base + (i - 1) * KC + k + 1)
        act.activation(tmp[:, k, :], h[:, k, :], ACT.Identity, scale=m.column(name, k)).then_inc(scaled.sem, 1)
    for k in range(KC):
        act.wait_ge(mid.sem, mid.base + i * KC + k + 1)
        act.activation(pair[:, 0, k, :], tmp[:, k, :], ACT.Copy).then_inc(high.sem, 1)


def mix_chunk_vector(m, dve, i, h, tmp, pair, keep):
    mid, high, low = m.sig["in_mid"], m.sig["in_high"], m.sig["in_low"]
    scaled = m.sig["hid_mul"]
    for k in range(KC):
        dve.wait_ge(scaled.sem, scaled.base + i * KC + k + 1)
        to = tmp[:, k, :].rearrange("p (b s) -> p b s", s=S)
        of = h[:, k, :].rearrange("p (b s) -> p b s", s=S)
        dve.scalar_tensor_tensor(to[:, :, 1:S], of[:, :, 0:S - 1], keep[:, i * KC + k:i * KC + k + 1],
                                 to[:, :, 1:S], ALU.mult, ALU.add).then_inc(mid.sem, 1)
    for k in range(KC):
        dve.wait_ge(high.sem, high.base + i * KC + k + 1)
        dve.tensor_tensor(pair[:, 1, k, :], tmp[:, k, :], pair[:, 0, k, :].bitcast(F32), ALU.subtract).then_inc(low.sem, 1)


def mixed_linears(m, h, mixes, pairs, tmp, keep):
    nc, ps, mm, done, low, ch = m.nc, m.ps, m.sig["mm"], m.sig["act_out"], m.sig["in_low"], m.sig["dve_chain"]
    G = 2 * KC
    w0 = m.used
    linears = sum(e is not None for _, e in mixes)
    for i in range(linears):
        m.free_at.append(mm.base + G * (i + 1))
    m.used = len(m.free_at)
    with nc.Block() as block:

        @block.sync
        def _(sp):
            m.load_blocks(sp, m.used + RING)

        @block.tensor
        def _(pe):
            for i in range(linears):
                m.wait_pair(pe, w0 + i)
                pe.wait_ge(low.sem, low.base + KC * (i + 1))
                for g in range(G):
                    c, n = divmod(g, 2)
                    if i > 0:
                        pe.wait_ge(done.sem, done.base + (i - 1) * G + g + 1)
                    product(pe, ps[:, g, 0:HT],
                            [(lambda a, k=k: m.pair(w0 + i, a)[:, k, c * P:(c + 1) * P],
                              lambda b, k=k: pairs[i % 2][:, b, k, halves(n)]) for k in range(KC)]).then_inc(mm.sem, 1)

        def drain(act, i):
            for g in range(G):
                act.wait_ge(mm.sem, mm.base + i * G + g + 1)
                mixes[i][1](act, g // 2, g % 2, ps[:, g, 0:HT]).then_inc(done.sem, 1)

        @block.scalar
        def _(act):
            for i, (name, _) in enumerate(mixes):
                if i >= 2:
                    act.wait_ge(mm.sem, mm.base + G * (i - 1))
                mix_chunk_scalar(m, act, i, name, h, tmp, pairs[i % 2])
                m.split_high(act, w0 + i + 1)
                if i > 0:
                    drain(act, i - 1)
            if linears == len(mixes):
                m.split_high(act, m.used + 1)
                drain(act, linears - 1)

        @block.vector
        def _(dve):
            for i, (name, _) in enumerate(mixes):
                c = COL[name]
                dve.tensor_scalar(keep[:, i * KC:(i + 1) * KC], m.par[:, c:c + KC], -1.0, 1.0, ALU.mult, ALU.add).then_inc(ch.sem, 1)
            dve.wait_ge(ch.sem, ch.base + len(mixes))
            for i in range(len(mixes)):
                mix_chunk_vector(m, dve, i, h, tmp, pairs[i % 2], keep)
                m.split_low(dve, w0 + i + 1)
            if linears == len(mixes):
                m.split_low(dve, m.used + 1)

    for s in ("in_low", "in_mid", "in_high", "hid_mul"):
        m.sig[s].advance(KC * len(mixes))
    ch.advance(len(mixes))
    mm.advance(G * linears)
    done.advance(G * linears)


def wkv(m, k_, v_, r_, xl, sb):
    nc, dv, ac = m.nc, m.sig["dve_chain"], m.sig["act_out"]
    mx, qq, aa = (sb(n, [P, KC, B, S + 1], F32) for n in ("wkv_m", "wkv_q", "wkv_a"))
    t1, t2 = (sb(n, [P, KC, B, S], F32) for n in ("wkv_t1", "wkv_t2"))
    t3 = qq[:, :, :, 1:]

    def bs(t, c):
        return t[:, c, :].rearrange("p (b s) -> p b s", s=S)

    with nc.Block() as block:

        @block.vector
        def _(dve):
            n = 0

            def out(ins):
                nonlocal n
                n += 1
                ins.then_inc(dv.sem, 1)

            def own():
                dve.wait_ge(dv.sem, dv.base + n)

            def after_act(count):
                dve.wait_ge(ac.sem, ac.base + count)

            out(dve.memset(mx[:, :, :, 0:1], NEG_INF))
            out(dve.memset(qq[:, :, :, 0:1], 1.0))
            out(dve.memset(aa[:, :, :, 0:1], 0.0))
            own()
            for c in range(KC):
                for b in range(B):
                    out(dve.tensor_tensor_scan(mx[:, c, b, 1:], k_[:, c, b * S:(b + 1) * S],
                                               m.column("time_decay", c).to_broadcast([P, S]), NEG_INF, ALU.max, ALU.add))
            own()
            for c in range(KC):
                out(dve.tensor_tensor(t1[:, c], mx[:, c, :, 0:S], mx[:, c, :, 1:], ALU.subtract))
                out(dve.tensor_tensor(t2[:, c], bs(k_, c), mx[:, c, :, 1:], ALU.subtract))
            for c in range(KC):
                after_act(2 * c + 2)
                for b in range(B):
                    out(dve.tensor_tensor_scan(qq[:, c, b, 1:], t1[:, c, b, :], t2[:, c, b, :], 1.0, ALU.mult, ALU.add))
            for c in range(KC):
                after_act(2 * KC + c + 1)
                out(dve.tensor_tensor(mx[:, c], mx[:, c], qq[:, c], ALU.add))
            own()
            for c in range(KC):
                out(dve.tensor_tensor(t3[:, c], mx[:, c, :, 0:S], bs(k_, c), ALU.max))
            own()
            for c in range(KC):
                out(dve.tensor_tensor(t1[:, c], mx[:, c, :, 0:S], t3[:, c], ALU.subtract))
                out(dve.tensor_tensor(t2[:, c], bs(k_, c), t3[:, c], ALU.subtract))
            for c in range(KC):
                after_act(3 * KC + 2 * c + 2)
                out(dve.tensor_tensor(t2[:, c], t2[:, c], bs(v_, c), ALU.mult))
            own()
            for c in range(KC):
                for b in range(B):
                    out(dve.tensor_tensor_scan(aa[:, c, b, 1:], t1[:, c, b, :], t2[:, c, b, :], 0.0, ALU.mult, ALU.add))
            for c in range(KC):
                out(dve.tensor_scalar(k_[:, c, :], k_[:, c, :], m.column("time_first", c), None, ALU.add))
            own()
            for c in range(KC):
                out(dve.tensor_tensor(t3[:, c], mx[:, c, :, 0:S], bs(k_, c), ALU.max))
            own()
            for c in range(KC):
                out(dve.tensor_tensor(t1[:, c], mx[:, c, :, 0:S], t3[:, c], ALU.subtract))
                out(dve.tensor_tensor(t2[:, c], bs(k_, c), t3[:, c], ALU.subtract))
            for c in range(KC):
                after_act(5 * KC + 2 * c + 2)
                out(dve.tensor_tensor(t3[:, c], t1[:, c], t2[:, c], ALU.add))
            own()
            for c in range(KC):
                out(dve.reciprocal(t3[:, c], t3[:, c]))
                out(dve.tensor_tensor(t1[:, c], t1[:, c], aa[:, c, :, 0:S], ALU.mult))
                out(dve.tensor_tensor(t2[:, c], t2[:, c], bs(v_, c), ALU.mult))
            own()
            for c in range(KC):
                out(dve.tensor_tensor(t1[:, c], t1[:, c], t2[:, c], ALU.add))
                out(dve.tensor_tensor(t3[:, c], t3[:, c], bs(r_, c), ALU.mult))
            own()
            for c in range(KC):
                out(dve.tensor_tensor(t1[:, c], t1[:, c], t3[:, c], ALU.mult))
            own()
            for c in range(KC):
                out(dve.tensor_tensor(bs(xl, c), bs(xl, c), t1[:, c], ALU.add))
            wkv.dve_count = n

        @block.scalar
        def _(act):
            scans = B * KC
            d1 = dv.base + 3 + scans
            for c in range(KC):
                for i, t in enumerate((t1, t2)):
                    act.wait_ge(dv.sem, d1 + 2 * c + i + 1)
                    act.activation(t[:, c], t[:, c], ACT.Exp, bias=m.column("time_decay", c)).then_inc(ac.sem, 1)
            d2 = d1 + 2 * KC
            for c in range(KC):
                act.wait_ge(dv.sem, d2 + B * (c + 1))
                act.activation(qq[:, c], qq[:, c], ACT.Ln).then_inc(ac.sem, 1)
            d3 = d2 + scans + 2 * KC
            for c in range(KC):
                for i, t in enumerate((t1, t2)):
                    act.wait_ge(dv.sem, d3 + 2 * c + i + 1)
                    act.activation(t[:, c], t[:, c], ACT.Exp).then_inc(ac.sem, 1)
            d4 = d3 + 2 * KC + KC + scans + 2 * KC
            for c in range(KC):
                for i, t in enumerate((t1, t2)):
                    act.wait_ge(dv.sem, d4 + 2 * c + i + 1)
                    act.activation(t[:, c], t[:, c], ACT.Exp).then_inc(ac.sem, 1)

    dv.advance(wkv.dve_count)
    ac.advance(7 * KC)


def mlp(m, src, y, pre, hid, experts, gate=None, b1=None, clear=True):
    nc, ps = m.nc, m.ps
    mm, ah, hm, hh_, ho, yo, ch, bc = (m.sig[s] for s in ("mm", "act_hid", "hid_mul", "hid_high", "hid_out", "y_out", "dve_chain", "b1_copy"))
    order = mlp_order()
    N = len(order)
    G = 2 * KC
    per = N * G
    half = per // 2
    w0 = m.used
    wh, wl = m.sig["w_high"].sem, m.sig["w_low"].sem
    assert w0 % (RING * PAIRS) == 0 and m.high == m.low == w0 + 1

    def before(i):
        return [k for k, _ in order[:i]].count(order[i][0]) * G

    for e in range(experts):
        for i in range(N):
            m.free_at.append(mm.base + e * per + (i + 1) * G)
    m.used = len(m.free_at)

    def run(eng, body):
        if experts == 1:
            body(0)
        else:
            with eng.Fori(0, experts) as e:
                body(e)

    with nc.Block() as block:

        @block.sync
        def _(sp):
            m.load_blocks(sp, w0 + RING + 1)
            assert m.loaded == w0 + RING + 1
            if experts > 1:
                with sp.Fori(0, experts - 1) as e:
                    for i in range(1, N + 1):
                        ahead, (second, j) = (i + RING) // N, order[(i + RING) % N]
                        sp.wait_ge(wl, w0 + i + 1 + e * N)
                        w = m.d["W2"] if second else m.d["W1"]
                        part = w[e + ahead, j * C:(j + 1) * C, :] if second else w[e + ahead, :, j * C:(j + 1) * C]
                        sp.dma_start(m.slot(i), part.rearrange("(k p) n -> p k n", p=P)).then_inc(m.block_load[i % RING].sem, 16)
                m.loaded += N * (experts - 1)
            m.load_blocks(sp, m.used + RING)

        @block.tensor
        def _(pe):
            def body(e):
                for i, (second, j) in enumerate(order):
                    pe.wait_ge(wl, w0 + i + 1 + e * N)
                    if second:
                        pe.wait_ge(ho.sem, ho.base + e * half + (j + 1) * G)
                    used = yo if second else ah
                    for g in range(G):
                        c, n = divmod(g, 2)
                        at = before(i) + g
                        if at >= 4 or experts > 1:
                            pe.wait_ge(used.sem, used.base + e * half + at - 3)
                        if second:
                            x = lambda b, k: hid[:, j % 2, b, k, halves(n)]
                        else:
                            x = lambda b, k: src[:, b, k, halves(n)]
                        product(pe, ps[:, 4 * second + at % 4, 0:HT],
                                [(lambda a, k=k: m.pair(i, a)[:, k, c * P:(c + 1) * P], lambda b, k=k: x(b, k))
                                 for k in range(KC)]).then_inc(mm.sem, 1)
            run(pe, body)

        @block.scalar
        def _(act):
            def split(e, i):
                act.wait_ge(m.block_load[i % RING].sem, 16 * ((w0 + i) // RING + 1) + e * (16 * N // RING))
                act.wait_ge(mm.sem, mm.base + e * per + (i - 1) * G)
                act.activation(m.pair(i, 0), m.slot(i), ACT.Copy).then_inc(wh, 1)

            def body(e):
                if gate is not None:
                    act.wait_ge(bc.sem, bc.base + e + 1)
                for i, (second, j) in enumerate(order):
                    split(e, i + 1)
                    if second:
                        continue

                    def high(g):
                        c, n = divmod(g, 2)
                        act.wait_ge(hm.sem, hm.base + e * half + before(i) + g + 1)
                        act.activation(hid[:, j % 2, 0, c, halves(n)], pre[:, g, :], ACT.Copy).then_inc(hh_.sem, 1)

                    for g in range(G):
                        c, n = divmod(g, 2)
                        at = before(i) + g
                        act.wait_ge(mm.sem, mm.base + e * per + i * G + g + 1)
                        if at >= G or experts > 1:
                            act.wait_ge(ho.sem, ho.base + e * half + at - G + 1)
                        pin = ps[:, at % 4, 0:HT]
                        if gate is None:
                            ins = act.activation(pre[:, g, :], pin, ACT.Relu)
                        else:
                            ins = act.activation(pre[:, g, :], pin, ACT.Gelu, bias=b1[:, j * KC + c:j * KC + c + 1])
                        ins.then_inc(ah.sem, 1)
                        if g == 0 and (j >= 2 or experts > 1):
                            back = (order.index((1, j - 2)) + 1) * G if j >= 2 else (order.index((1, j + 2)) + 1) * G - per
                            act.wait_ge(mm.sem, mm.base + e * per + back)
                        if g > 0:
                            high(g - 1)
                    high(G - 1)
            run(act, body)

        @block.vector
        def _(dve):
            if clear:
                dve.memset(y[:, :, :], 0.0).then_inc(ch.sem, 1)
                dve.wait_ge(ch.sem, ch.base + 1)

            def copy_b1(e):
                at = COL["b1"] + e * (FF // P)
                dve.tensor_scalar(b1[:, :], m.par[:, bass.ds(at, FF // P)], 1.0, None, ALU.mult).then_inc(bc.sem, 1)

            if gate is not None:
                copy_b1(0)

            def body(e):
                for i, (second, j) in enumerate(order):
                    dve.wait_ge(wh, w0 + i + 2 + e * N)
                    dve.tensor_tensor(m.pair(i + 1, 1), m.slot(i + 1), m.pair(i + 1, 0).bitcast(F32), ALU.subtract).then_inc(wl, 1)
                    if gate is not None and (second, j) == (1, 2):
                        dve.wait_ge(ah.sem, ah.base + e * half + half)
                        copy_b1(e + 1)

                    def low(g):
                        c, n = divmod(g, 2)
                        dve.wait_ge(hh_.sem, hh_.base + e * half + before(i) + g + 1)
                        dve.tensor_tensor(hid[:, j % 2, 1, c, halves(n)], pre[:, g, :],
                                          hid[:, j % 2, 0, c, halves(n)].bitcast(F32), ALU.subtract).then_inc(ho.sem, 1)

                    for g in range(G):
                        c, n = divmod(g, 2)
                        at = before(i) + g
                        if second:
                            dve.wait_ge(mm.sem, mm.base + e * per + i * G + g + 1)
                            if at >= G or experts > 1:
                                dve.wait_ge(yo.sem, yo.base + e * half + at - G + 1)
                            yy = y[:, c, halves(n)]
                            dve.tensor_tensor(yy, ps[:, 4 + at % 4, 0:HT], yy, ALU.add).then_inc(yo.sem, 1)
                        else:
                            dve.wait_ge(ah.sem, ah.base + e * half + at + 1)
                            hh = pre[:, g, :]
                            by = hh if gate is None else gate[:, bass.ds(n * HT + e * T, HT)]
                            dve.tensor_tensor(hh, hh, by, ALU.mult).then_inc(hm.sem, 1)
                            if g > 0:
                                low(g - 1)
                    if not second:
                        low(G - 1)
            run(dve, body)

    m.high = m.low = w0 + experts * N + 1
    bc.advance(experts + 1 if gate is not None else 0)
    mm.advance(experts * per)
    for s in (ah, hm, hh_, ho, yo):
        s.advance(experts * half)
    ch.advance(1 if clear else 0)


SCHEDULE = {32: ("kvkvkvkvkvkvkk", [[12], [], [13], []] + [[g] for g in range(12)], (9, 11, 13), (10, 12, 14), 7),
            64: ("kkvvkvkvkvkvkk", [[11, 12], [13], [0]] + [[2 * g - 1, 2 * g] for g in range(1, 6)], (3, 4, 5), (4, 5, 6), 2)}


def attention(m, q, D, clip, bias, schedule, name, sb):
    nc, ps = m.nc, m.ps
    H = C // D
    HPC = P // D
    NP_ = 4
    LAG_T, LAG_O = 3, 4
    KG, VG = 2 * KC, KVC
    PROJ = KG + VG
    PT_BANK, O_BANK, PROJ_BANK = 4, 6, 7
    FIRST_BANKS = 4
    kinds, groups_at, high_at, low_at, queries_at = schedule
    assert len(groups_at) == H and len(kinds) == PROJ and kinds.count("k") == KG
    own = set(g for i in range(groups_at.index([0])) for g in groups_at[i])
    wk, wv = m.used, m.used + 1
    sg = m.sig
    mm, pad = sg["mm"], sg["pad"]
    m.free_at += [mm.base + B * PROJ] * 2
    m.used = len(m.free_at)
    ctx_t = sb(f"ctxt{name}", [P, KX, NKV], F32)
    ctx = sb(f"ctx{name}", [P, 2, 2, KX, NKV], F32R)
    kt = sb(f"kt{name}", [P, 2, KC, NKV], F32R)
    vv = sb(f"vv{name}", [P, 2, KVC, C], F32)
    qp = sb(f"qp{name}", [P, 2, 2, H, S], F32R)
    pr = sb(f"pr{name}", [S, NP_, KVC * P], F32)
    pt = sb(f"pt{name}", [P, 2, KVC, S], F32)
    smax = sb(f"smax{name}", [S, NP_, 2], F32)
    ssum = sb(f"ssum{name}", [S, NP_], F32)
    spans = (slice(0, BANK), slice(BANK, NKV))

    def at(name, b, per, n):
        return sg[name].base + b * per + n

    def scores(h):
        return ps[0:S, 2 * (h % 2):2 * (h % 2) + 2, :].rearrange("s n k -> s (n k)")[:, 0:NKV]

    def is_key(g):
        return kinds[g] == "k"

    def nth(g):
        return kinds[:g].count(kinds[g])

    def v_rows(c):
        return P if c < KVC - 1 else KVR

    def k_bank(n, bank):
        return ps[:, bank, 0:spans[n].stop - spans[n].start]

    def v_bank(c, bank):
        return ps[0:v_rows(c), bank, 0:C]

    def bank_drained(eng, b, g):
        if is_key(g):
            eng.wait_ge(sg["k_low"].sem, at("k_low", b, KG, nth(g) + 1))
        else:
            eng.wait_ge(sg["v_out"].sem, at("v_out", b, VG, nth(g) + 1))

    def queries_of(b):
        return [q[ri * D:(ri + 1) * D, :, bass.ds(b * S, S)] for ri in range(HPC)]

    def padded(p, part, ri):
        return qp[ri * D:(ri + 1) * D, p, part].rearrange("p (c i) s -> p i c s", i=HPC)[:, ri]

    def groups(b, p, i, first, last):
        mine = [] if first else [(b, p, g) for g in groups_at[i] if g in own]
        return mine + ([] if last else [(b + 1, 1 - p, g) for g in groups_at[i] if g not in own])

    def behind(b, p, i, lag, first):
        if i >= lag:
            return b, p, i - lag
        return None if first else (b - 1, 1 - p, i - lag + H)

    def loop(eng, body):
        body(0, 0, True, False, True)
        with eng.Fori(0, (B - 4) // 2) as i:
            body(i * 2 + 1, 1, False, False, True)
            body(i * 2 + 2, 0, False, False, True)
        body(B - 3, 1, False, False, True)
        body(B - 2, 0, False, False, False)
        body(B - 1, 1, False, True, False)

    with nc.Block() as block:

        @block.sync
        def _(sp):
            m.load_blocks(sp, wk + RING)
            ld = sg["ctx_load"]
            sp.dma_start(ctx_t[:, :, :], m.d["ctx"][0]).then_inc(ld.sem, 16)
            with sp.Fori(0, B - 1) as b:
                sp.wait_ge(sg["ctx_low"].sem, at("ctx_low", b, KX, KX))
                sp.dma_start(ctx_t[:, :, :], m.d["ctx"][b + 1]).then_inc(ld.sem, 16)
            m.load_blocks(sp, m.used + RING)

        @block.tensor
        def _(pe):
            def project(b, p, g, bank=PROJ_BANK):
                if g == 0:
                    pe.wait_ge(sg["ctx_low"].sem, at("ctx_low", b, KX, KX))
                if bank != PROJ_BANK:
                    if g >= FIRST_BANKS:
                        bank_drained(pe, b, g - FIRST_BANKS)
                elif g == 0:
                    pe.wait_ge(sg["k_low"].sem, at("k_low", b, KG, 0))
                else:
                    bank_drained(pe, b, g - 1)
                if is_key(g):
                    c, n = divmod(nth(g), 2)
                    last = product(pe, k_bank(n, bank), [(lambda a, k=k: m.pair(wk, a)[:, k, c * P:(c + 1) * P],
                                                    lambda x, k=k: ctx[:, p, x, k, spans[n]]) for k in range(KX)])
                else:
                    c = nth(g)
                    last = product(pe, v_bank(c, bank), [(lambda a, k=k: ctx[:, p, a, k, c * P:c * P + v_rows(c)],
                                                    lambda x, k=k: m.pair(wv, x)[:, k, :]) for k in range(KX)])
                last.then_inc(mm.sem, 1)

            def transposes(b, p, h):
                pe.wait_ge(sg["p_norm"].sem, at("p_norm", b, H, h + 1))
                pe.wait_ge(sg["pt_out"].sem, at("pt_out", b, H, h))
                for c in range(KVC):
                    last = pe.transpose(ps[:, PT_BANK + c // 3, (c % 3) * S:(c % 3 + 1) * S],
                                        pr[:, h % NP_, c * P:(c + 1) * P], m.ident[0:S, 0:S])
                last.then_inc(sg["p_turn"].sem, 1)

            def output(b, p, h):
                c, r = h // HPC, (h % HPC) * D
                if h == 0:
                    pe.wait_ge(sg["v_out"].sem, at("v_out", b, VG, VG))
                pe.wait_ge(sg["pt_out"].sem, at("pt_out", b, H, h + 1))
                if h % HPC == 0:
                    pe.wait_ge(sg["o_out"].sem, at("o_out", b, KC, c))
                for k in range(KVC):
                    last = pe.matmul(ps[r:r + D, O_BANK, 0:S], vv[:, p, k, h * D:(h + 1) * D],
                                     pt[:, h % 2, k, :], start=k == 0, stop=k == KVC - 1)
                last.then_inc(sg["o_mm"].sem, 1)

            m.wait_pair(pe, wv)
            for g in range(PROJ):
                project(0, 0, g, g % FIRST_BANKS)
            for g in range(PROJ - FIRST_BANKS, PROJ):
                bank_drained(pe, 0, g)

            def body(b, p, first, last, more):
                for i in range(H):
                    todo = groups(b, p, i, first, last)
                    if i == 0:
                        pe.wait_ge(sg["q_low"].sem, at("q_low", b, 1, 1))
                    if i % HPC == 0:
                        pe.wait_ge(sg["k_low"].sem, at("k_low", b, KG, 2 * (i // HPC + 1)))
                    if clip:
                        pe.wait_ge(sg["s_clip"].sem, at("s_clip", b, 2 * H, 2 * (i - 2) + 1))
                    else:
                        pe.wait_ge(sg["p_exp"].sem, at("p_exp", b, H, i - 1))
                    for s in spans:
                        done = product(pe, scores(i)[:, s], [(lambda a: qp[:, p, a, i, :], lambda x: kt[:, x, i // HPC, s])])
                    done.then_inc(sg["s_mm"].sem, 1)
                    for t in todo[:-1]:
                        project(*t)
                    for work, lag in ((transposes, LAG_T), (output, LAG_O)):
                        if behind(b, p, i, lag, first):
                            work(*behind(b, p, i, lag, first))
                    for t in todo[-1:]:
                        project(*t)
                if last:
                    for i in range(H, H + LAG_O):
                        if i < H + LAG_T:
                            transposes(b, p, i - LAG_T)
                        output(b, p, i - LAG_O)
            loop(pe, body)

        @block.gpsimd
        def _(pool):
            pool.memset(vv[:, :, KVC - 1, :], 0.0).then_inc(pad.sem, 1)
            pool.memset(qp[:, 0].bitcast(F32), 0.0).then_inc(pad.sem, 1)
            pool.memset(pr[:, :, NKV:], 0.0).then_inc(pad.sem, 1)
            pool.memset(qp[:, 1].bitcast(F32), 0.0).then_inc(pad.sem, 1)

        @block.scalar
        def _(act):
            m.split_high(act, wv + 1)
            act.wait_ge(pad.sem, pad.base + 1)

            def split(b, p, k):
                if k == 0:
                    act.wait_ge(sg["ctx_load"].sem, at("ctx_load", b, 16, 16))
                    if not isinstance(b, int) or b > 1:
                        act.wait_ge(mm.sem, mm.base + (b - 1) * PROJ)
                act.activation(ctx[:, p, 0, k], ctx_t[:, k], ACT.Copy).then_inc(sg["ctx_high"].sem, 1)

            def drain(b, p, g, bank=PROJ_BANK):
                act.wait_ge(mm.sem, mm.base + b * PROJ + g + 1)
                if is_key(g):
                    c, n = divmod(nth(g), 2)
                    to = kt[:, 0, c, spans[n]]
                    if bias:
                        ins = act.activation(to, k_bank(n, bank), ACT.Identity, bias=m.column("bk", c))
                    else:
                        ins = act.activation(to, k_bank(n, bank), ACT.Copy)
                    ins.then_inc(sg["k_out"].sem, 1)
                else:
                    c = nth(g)
                    act.activation(vv[0:v_rows(c), p, c, :], v_bank(c, bank), ACT.Copy).then_inc(sg["v_out"].sem, 1)

            def copy_turned(b, p, h):
                act.wait_ge(sg["p_turn"].sem, at("p_turn", b, H, h + 1))
                act.wait_ge(sg["o_mm"].sem, at("o_mm", b, H, h - 1))
                act.activation(pt[:, h % 2].rearrange("p (n k) s -> p n (k s)", n=2), ps[:, PT_BANK:PT_BANK + 2, 0:3 * S],
                               ACT.Copy).then_inc(sg["pt_out"].sem, 1)

            for k in range(KX):
                split(0, 0, k)
            for g in range(PROJ):
                drain(0, 0, g, g % FIRST_BANKS)
                if g < KX:
                    split(1, 1, g)

            def body(b, p, first, last, more):
                for i in range(H):
                    todo = groups(b, p, i, first, last)
                    for t in todo[:-1]:
                        drain(*t)
                    if behind(b, p, i, LAG_T, first):
                        copy_turned(*behind(b, p, i, LAG_T, first))
                    for t in todo[-1:]:
                        drain(*t)
                    act.wait_ge(sg["s_max"].sem, at("s_max", b, H, i + 1))
                    act.wait_ge(sg["p_turn"].sem, at("p_turn", b, H, i - NP_ + 1))
                    to = pr[:, i % NP_, 0:NKV]
                    act.activation(to, to if clip else scores(i), ACT.Exp, bias=smax[:, i % NP_, 1:2],
                                   accum_out=ssum[:, i % NP_:i % NP_ + 1]).then_inc(sg["p_exp"].sem, 1)
                    for k in range(KX):
                        if i == high_at[k] and more:
                            split(b + 2, p, k)
                if last:
                    for h in range(H - LAG_T, H):
                        copy_turned(b, p, h)
            loop(act, body)
            m.split_high(act, m.used + 1)

        @block.vector
        def _(dve):
            m.split_low(dve, wv + 1)
            def split(b, p, k):
                dve.wait_ge(sg["ctx_high"].sem, at("ctx_high", b, KX, k + 1))
                dve.tensor_tensor(ctx[:, p, 1, k], ctx_t[:, k], ctx[:, p, 0, k].bitcast(F32),
                                  ALU.subtract).then_inc(sg["ctx_low"].sem, 1)

            def queries(b, p):
                dve.wait_ge(sg["s_mm"].sem, at("s_mm", b, H, -H))
                for ri, of in enumerate(queries_of(b)):
                    dve.tensor_scalar(padded(p, 0, ri), of, 1.0, None, ALU.mult).then_inc(sg["q_high"].sem, 1)
                for ri, of in enumerate(queries_of(b)):
                    dve.wait_ge(sg["q_high"].sem, at("q_high", b, HPC, ri + 1))
                    ins = dve.tensor_tensor(padded(p, 1, ri), of, padded(p, 0, ri).bitcast(F32), ALU.subtract)
                ins.then_inc(sg["q_low"].sem, 1)

            def low(b, p, g, bank=PROJ_BANK):
                if not is_key(g):
                    return
                c, n = divmod(nth(g), 2)
                dve.wait_ge(sg["k_out"].sem, at("k_out", b, KG, nth(g) + 1))
                hi = kt[:, 0, c, spans[n]].bitcast(F32)
                if bias:
                    ins = dve.scalar_tensor_tensor(kt[:, 1, c, spans[n]], k_bank(n, bank), m.column("bk", c), hi, ALU.add, ALU.subtract)
                else:
                    ins = dve.tensor_tensor(kt[:, 1, c, spans[n]], k_bank(n, bank), hi, ALU.subtract)
                ins.then_inc(sg["k_low"].sem, 1)

            def reciprocal(b, p, h):
                dve.wait_ge(sg["p_exp"].sem, at("p_exp", b, H, h + 1))
                s_ = ssum[:, h % NP_:h % NP_ + 1]
                dve.reciprocal(s_, s_).then_inc(sg["norm_rec"].sem, 1)

            def normalise(b, p, h):
                dve.wait_ge(sg["norm_rec"].sem, at("norm_rec", b, H, h + 1))
                dve.tensor_scalar(pr[:, h % NP_, 0:NKV], pr[:, h % NP_, 0:NKV], ssum[:, h % NP_:h % NP_ + 1], None,
                                  ALU.mult).then_inc(sg["p_norm"].sem, 1)

            def output(b, p, h):
                c, after = divmod(h + 1, HPC)
                if after:
                    return
                dve.wait_ge(sg["o_mm"].sem, at("o_mm", b, H, h + 1))
                to = q[:, c - 1, bass.ds(b * S, S)]
                if bias:
                    ins = dve.tensor_scalar(to, ps[:, O_BANK, 0:S], m.column("bv", c - 1), None, ALU.add)
                else:
                    ins = dve.tensor_scalar(to, ps[:, O_BANK, 0:S], 1.0, None, ALU.mult)
                ins.then_inc(sg["o_out"].sem, 1)

            for k in range(KX):
                split(0, 0, k)
            dve.wait_ge(pad.sem, pad.base + 4)
            queries(0, 0)
            for g in range(PROJ):
                low(0, 0, g, g % FIRST_BANKS)
                if g < KX:
                    split(1, 1, g)

            def body(b, p, first, last, more):
                for i in range(H):
                    todo = groups(b, p, i, first, last)
                    before = behind(b, p, i, 1, first)
                    dve.wait_ge(sg["s_mm"].sem, at("s_mm", b, H, i + 1))
                    dve.wait_ge(sg["p_turn"].sem, at("p_turn", b, H, i - NP_ + 1))
                    t, to = smax[:, i % NP_], pr[:, i % NP_, 0:NKV]
                    if clip:
                        x_, n0 = sg["s_clip"], at("s_clip", b, 2 * H, 2 * i)
                        dve.tensor_scalar(to, scores(i), -CLAMP, None, ALU.max, ALU.max, accum_out=t[:, 0:1]).then_inc(x_.sem, 1)
                        if before:
                            reciprocal(*before)
                        dve.wait_ge(x_.sem, n0 + 1)
                        dve.tensor_scalar(t[:, 1:2], t[:, 0:1], CLAMP, -1.0, ALU.min, ALU.mult).then_inc(x_.sem, 1)
                        dve.tensor_scalar(to, to, CLAMP, None, ALU.min).then_inc(sg["s_max"].sem, 1)
                    else:
                        dve.tensor_reduce(t[:, 1:2], scores(i), AX.X, ALU.max, negate=True).then_inc(sg["s_max"].sem, 1)
                        if before:
                            reciprocal(*before)
                    for g in todo[:-1]:
                        low(*g)
                    if before:
                        normalise(*before)
                    if behind(b, p, i, LAG_O, first):
                        output(*behind(b, p, i, LAG_O, first))
                    if i == queries_at and not last:
                        queries(b + 1, 1 - p)
                    for g in todo[-1:]:
                        low(*g)
                    for k in range(KX):
                        if i == low_at[k] and more:
                            split(b + 2, p, k)
                if last:
                    reciprocal(b, p, H - 1)
                    normalise(b, p, H - 1)
                    for h in range(H - LAG_O, H):
                        output(b, p, h)
            loop(dve, body)
            m.split_low(dve, m.used + 1)

    mm.advance(B * PROJ)
    for s, n in (("ctx_load", 16 * B), ("ctx_high", B * KX), ("ctx_low", B * KX), ("k_out", B * KG), ("k_low", B * KG), ("v_out", B * VG),
                 ("q_high", B * HPC), ("q_low", B), ("s_mm", B * H),
                 ("s_clip", 2 * B * H if clip else 0), ("s_max", B * H), ("p_exp", B * H),
                 ("p_norm", B * H), ("norm_rec", B * H), ("p_turn", B * H), ("pt_out", B * H),
                 ("o_mm", B * H), ("o_out", B * KC), ("pad", 4)):
        sg[s].advance(n)


def gates(m, u, gate, y, sb):
    nc, ps, g = m.nc, m.ps, m.sig
    mm, dv, ac, low, pad = g["mm"], g["dve_chain"], g["act_out"], g["in_low"], g["pad"]
    cen = sb("cen", [P, KC, E], F32)
    b2 = sb("b2", [E, C], F32)
    before = sb("before", [P, E, E], F32)
    pick = sb("pick", [E, E, P], F32)
    sc = sb("sc", [S, B, E], F32)
    cmp = sb("cmp", [S, B, E, E], F32)
    eq = sb("eq", [S, B, E, E], F32)
    rank = sb("rank", [S, B, E], F32)
    den = sb("den", [S, B], F32)
    gt = sb("gt", [E, T], F32)
    gt_p = sb("gt_p", [P, 2, T], F32R)
    b2_p = sb("b2_p", [P, 2, C], F32R)
    pick_r = sb("pick_r", [P, E, P], F32R)
    with nc.Block() as block:

        @block.sync
        def _(sp):
            ld = g["const_load"]
            sp.dma_start(cen[:, :, :], m.d["centroids"]).then_inc(ld.sem, 16)
            sp.dma_start(b2[:, :], m.d["b2"]).then_inc(ld.sem, 16)
            sp.dma_start(before[:, :, :], m.d["before"]).then_inc(ld.sem, 16)
            sp.dma_start(pick[:, :, :], m.d["pick"]).then_inc(ld.sem, 16)

        @block.tensor
        def _(pe):
            ld = g["const_load"]
            pe.wait_ge(ld.sem, ld.base + 64)
            for b in range(B):
                for k in range(KC):
                    last = pe.matmul(ps[0:S, 0, b * E:(b + 1) * E], u[:, k, b * S:(b + 1) * S], cen[:, k, :],
                                     start=k == 0, stop=k == KC - 1)
            last.then_inc(mm.sem, 1)
            pe.wait_ge(dv.sem, dv.base + 12)
            for b in range(B):
                last = pe.transpose(ps[0:E, 1 + b // 4, (b % 4) * S:(b % 4 + 1) * S], rank[:, b, :], m.ident[0:S, 0:S])
            last.then_inc(mm.sem, 1)
            pe.wait_ge(low.sem, low.base + 3)
            pe.wait_ge(ac.sem, ac.base + 2)
            for j in range(2 * E):
                e, n = divmod(j, 2)
                if j >= 4:
                    pe.wait_ge(ac.sem, ac.base + 5 + j - 3)
                for part in range(2):
                    last = pe.matmul(ps[:, 3 + j % 4, 0:HT], pick_r[:, e, :], gt_p[:, part, halves(n)],
                                     start=part == 0, stop=part == 1)
                last.then_inc(mm.sem, 1)
            for j in range(2 * KC):
                c, n = divmod(j, 2)
                if j < 4:
                    pe.wait_ge(ac.sem, ac.base + 5 + 2 * E - 3 + j)
                else:
                    pe.wait_ge(dv.sem, dv.base + 14 + j - 3)
                product(pe, ps[:, 3 + j % 4, 0:HT], [(lambda a: b2_p[:, a, c * P:(c + 1) * P],
                                                      lambda b: gt_p[:, b, halves(n)])]).then_inc(mm.sem, 1)

        @block.gpsimd
        def _(pool):
            for t in (pick_r, b2_p, gt_p):
                pool.memset(t[:, :, :].bitcast(F32), 0.0).then_inc(pad.sem, 1)

        @block.scalar
        def _(act):
            act.wait_ge(mm.sem, mm.base + 1)
            act.activation(sc[:, :, :], ps[0:S, 0, 0:B * E].rearrange("s (b e) -> s b e", e=E), ACT.Exp, scale=-1.0).then_inc(ac.sem, 1)
            act.wait_ge(pad.sem, pad.base + 3)
            act.wait_ge(g["const_load"].sem, g["const_load"].base + 64)
            act.activation(pick_r[0:E], pick[:, :, :], ACT.Copy).then_inc(ac.sem, 1)
            act.activation(b2_p[0:E, 0], b2[:, :], ACT.Copy).then_inc(ac.sem, 1)
            for n in range(2):
                act.wait_ge(dv.sem, dv.base + 13 + n)
                act.activation(gt_p[0:E, 0, halves(n)], gt[:, halves(n)], ACT.Copy).then_inc(ac.sem, 1)
            for j in range(2 * E):
                e, n = divmod(j, 2)
                act.wait_ge(mm.sem, mm.base + 3 + j)
                act.activation(gate[:, e * T + n * HT:e * T + (n + 1) * HT], ps[:, 3 + j % 4, 0:HT], ACT.Copy).then_inc(ac.sem, 1)

        @block.vector
        def _(dve):
            n = 0

            def step(ins):
                nonlocal n
                n += 1
                ins.then_inc(dv.sem, 1)
                dve.wait_ge(dv.sem, dv.base + n)

            dve.wait_ge(g["const_load"].sem, g["const_load"].base + 64)
            dve.wait_ge(ac.sem, ac.base + 1)
            step(dve.tensor_scalar(sc[:, :, :], sc[:, :, :], 1.0, None, ALU.add))
            step(dve.reciprocal(sc[:, :, :], sc[:, :, :]))
            for b in range(B):
                mine = sc[:, b, :].unsqueeze(2).to_broadcast([S, E, E])
                other = sc[:, b, :].unsqueeze(1).to_broadcast([S, E, E])
                dve.tensor_tensor(cmp[:, b], other, mine, ALU.is_gt)
                ins = dve.tensor_tensor(eq[:, b], other, mine, ALU.is_equal)
            step(ins)
            step(dve.tensor_tensor(eq[:, :, :, :], eq[:, :, :, :],
                                   before[0:S].unsqueeze(1).to_broadcast([S, B, E, E]), ALU.mult))
            step(dve.tensor_tensor(cmp[:, :, :, :], cmp[:, :, :, :], eq[:, :, :, :], ALU.add))
            step(dve.tensor_reduce(rank[:, :, :], cmp[:, :, :, :], AX.X, ALU.add))
            step(dve.tensor_scalar(rank[:, :, :], rank[:, :, :], 1.5, None, ALU.is_lt))
            step(dve.tensor_tensor(rank[:, :, :], rank[:, :, :], sc[:, :, :], ALU.mult))
            step(dve.tensor_reduce(den[:, :], rank[:, :, :], AX.X, ALU.add))
            step(dve.reciprocal(den[:, :], den[:, :]))
            step(dve.tensor_tensor(rank[:, :, :], rank[:, :, :], den[:, :].unsqueeze(2).to_broadcast([S, B, E]), ALU.mult))
            step(dve.engine_nop())
            dve.wait_ge(mm.sem, mm.base + 2)
            for i in range(2):
                dve.tensor_copy(gt[:, halves(i)], ps[0:E, 1 + i, 0:HT]).then_inc(dv.sem, 1)
            dve.wait_ge(ac.sem, ac.base + 3)
            dve.tensor_tensor(b2_p[0:E, 1], b2[:, :], b2_p[0:E, 0].bitcast(F32), ALU.subtract).then_inc(low.sem, 1)
            for i in range(2):
                dve.wait_ge(ac.sem, ac.base + 4 + i)
                dve.tensor_tensor(gt_p[0:E, 1, halves(i)], gt[:, halves(i)], gt_p[0:E, 0, halves(i)].bitcast(F32),
                                  ALU.subtract).then_inc(low.sem, 1)
            for j in range(2 * KC):
                c, i = divmod(j, 2)
                dve.wait_ge(mm.sem, mm.base + 3 + 2 * E + j)
                dve.tensor_copy(y[:, c, halves(i)], ps[:, 3 + j % 4, 0:HT]).then_inc(dv.sem, 1)

    mm.advance(2 + 2 * E + 2 * KC)
    ac.advance(5 + 2 * E)
    low.advance(3)
    pad.advance(3)
    dv.advance(14 + 2 * KC)
    g["const_load"].advance(64)


def values(m, u, v):
    nc, ps, mm, done = m.nc, m.ps, m.sig["mm"], m.sig["act_out"]
    w = m.used
    m.free_at.append(mm.base + B)
    m.used = len(m.free_at)
    with nc.Block() as block:

        @block.sync
        def _(sp):
            m.load_blocks(sp, m.used + RING)

        @block.tensor
        def _(pe):
            m.wait_pair(pe, w)
            for b in range(B):
                product(pe, ps[0:S, b, 0:C], [(lambda a, k=k: u[:, a, k, b * S:(b + 1) * S],
                                               lambda x, k=k: m.pair(w, x)[:, k, :]) for k in range(KC)]).then_inc(mm.sem, 1)

        @block.scalar
        def _(act):
            m.split_high(act, m.used + 1)
            for b in range(B):
                act.wait_ge(mm.sem, mm.base + b + 1)
                act.activation(v[:, b, :], ps[0:S, b, 0:C], ACT.Copy).then_inc(done.sem, 1)

        @block.vector
        def _(dve):
            m.split_low(dve, m.used + 1)

    mm.advance(B)
    done.advance(B)


def retention(m, q, k_, v, st, decay):
    nc, ps, mm, dv = m.nc, m.ps, m.sig["mm"], m.sig["dve_out"]
    x = m.x
    with nc.Block() as block:

        @block.tensor
        def _(pe):
            for b in range(B):
                for k in range(KC):
                    last = pe.matmul(ps[0:S, b // 4, (b % 4) * S:(b % 4 + 1) * S], k_[:, k, b * S:(b + 1) * S],
                                     q[:, k, b * S:(b + 1) * S], start=k == 0, stop=k == KC - 1)
                last.then_inc(mm.sem, 1)
            for b in range(B):
                pe.wait_ge(dv.sem, dv.base + 1 + b // 4)
                if b >= 4:
                    pe.wait_ge(dv.sem, dv.base + 2 + b - 3)
                for c in range(KC):
                    last = pe.matmul(ps[:, 4 + b % 4, c * S:(c + 1) * S], v[:, b, c * P:(c + 1) * P], st[:, b, :],
                                     start=True, stop=True)
                last.then_inc(mm.sem, 1)

        @block.vector
        def _(dve):
            for n in range(2):
                dve.wait_ge(mm.sem, mm.base + 4 * (n + 1))
                dve.tensor_tensor(st[:, 4 * n:4 * n + 4, :], ps[0:S, n, 0:HT].rearrange("s (b t) -> s b t", t=S),
                                  decay[:, :].unsqueeze(1).to_broadcast([S, 4, S]), ALU.mult).then_inc(dv.sem, 1)
            for b in range(B):
                dve.wait_ge(mm.sem, mm.base + B + b + 1)
                xb = x[:, :, b * S:(b + 1) * S]
                dve.tensor_tensor(xb, ps[:, 4 + b % 4, 0:HT].rearrange("p (c t) -> p c t", t=S), xb, ALU.add).then_inc(dv.sem, 1)

    mm.advance(2 * B)
    dv.advance(2 + B)


class Quantised:

    BANKS = 4

    def __init__(self, m, sb):
        self.m, self.raw = m, m.used
        self.w = sb("wq", [P, KC, C], F32)
        self.lora = sb("wlora", [P, KC, C], F32)
        self.sc = sb("wscale", [P, 2, KC, C], F32)
        self.la, self.lb = (sb(n, [32, 2, C], F32) for n in ("la", "lb"))
        self.load = [m.sig["quant_load0"], m.sig["quant_load1"]]

    def wait_loads(self, eng, i):
        eng.wait_ge(self.load[i % 2].sem, 96 * (i // 2 + 1))

    def sync(self, sp, i):
        sem, m = self.load[i % 2].sem, self.m
        for k in range(KC):
            part = m.d["scales"][i, 8 * k:8 * k + 8, :].unsqueeze(1).to_broadcast([8, 16, C])
            sp.dma_start(self.sc[:, i % 2, k, :], part).then_inc(sem, 16)
        sp.dma_start(self.la[:, i % 2, :], m.d["lora_a"][i]).then_inc(sem, 16)
        sp.dma_start(self.lb[:, i % 2, :], m.d["lora_b"][i]).then_inc(sem, 16)

    def tensor(self, pe, i, free=None):
        m = self.m
        self.wait_loads(pe, i)
        for k in range(KC):
            if free is not None:
                free(k)
            pe.matmul(m.ps[:, 8 - KC + k, 0:C], self.la[:, i % 2, k * P:(k + 1) * P], self.lb[:, i % 2, :],
                      start=True, stop=True).then_inc(m.sig["lora_mm"].sem, 1)

    def scalar(self, act, i, k):
        m, dv = self.m, self.m.sig["dve_chain"]
        act.wait_ge(dv.sem, dv.base + 2 * KC + k + 1)
        ins = act.activation(m.pair(self.raw + i, 0)[:, k], self.w[:, k], ACT.Copy)
        if k == KC - 1:
            ins.then_inc(m.sig["w_high"].sem, 1)

    def vector(self, dve, i):
        m, dv, out, lo = self.m, self.m.sig["dve_chain"], self.m.sig["lora_out"], self.m.sig["lora_mm"]
        w, raw = self.w, self.raw + i
        m.wait_block(dve, raw)
        self.wait_loads(dve, i)
        for k in range(KC):
            dve.tensor_scalar(w[:, k, :], m.slot(raw)[:, k, :].bitcast(I32), 1 / 7.5, -1.0, ALU.mult, ALU.add).then_inc(dv.sem, 1)
        for k in range(KC):
            dve.wait_ge(lo.sem, KC * i + k + 1)
            dve.tensor_scalar(self.lora[:, k, :], m.ps[:, 8 - KC + k, 0:C], 1.0, None, ALU.mult).then_inc(out.sem, 1)
        for k in range(KC):
            dve.wait_ge(dv.sem, dv.base + k + 1)
            dve.tensor_tensor(w[:, k, :], w[:, k, :], self.sc[:, i % 2, k, :], ALU.mult).then_inc(dv.sem, 1)
        for k in range(KC):
            dve.wait_ge(dv.sem, dv.base + KC + k + 1)
            dve.wait_ge(out.sem, KC * i + k + 1)
            dve.tensor_tensor(w[:, k, :], w[:, k, :], self.lora[:, k, :], ALU.add).then_inc(dv.sem, 1)

    def vector_low(self, dve, i):
        m = self.m
        dve.wait_ge(m.sig["w_high"].sem, self.raw + i + 1)
        dve.tensor_tensor(m.pair(self.raw + i, 1), self.w[:, :, :], m.pair(self.raw + i, 0).bitcast(F32),
                          ALU.subtract).then_inc(m.sig["w_low"].sem, 1)

    def advance(self, i):
        m = self.m
        m.high = m.low = self.raw + i + 1
        m.sig["dve_chain"].advance(3 * KC)

    def first(self):
        m = self.m
        with m.nc.Block() as block:

            @block.sync
            def _(sp):
                self.sync(sp, 0)
                self.sync(sp, 1)

            @block.tensor
            def _(pe):
                self.tensor(pe, 0)
                self.tensor(pe, 1, lambda k: pe.wait_ge(m.sig["lora_out"].sem, k + 1))

            @block.scalar
            def _(act):
                for k in range(KC):
                    self.scalar(act, 0, k)

            @block.vector
            def _(dve):
                self.vector(dve, 0)
                self.vector_low(dve, 0)

        self.advance(0)


def build(nc, d):
    with ExitStack() as ctx:
        m = Decoder(nc, ctx, d)
        x, par, g = m.x, m.par, m.sig

        def buffers(stack):
            return lambda name, shape, dt: stack.enter_context(nc.sbuf_tensor(name, shape, dt))

        for n in ("w_tk", "w_tv", "w_tr", "w_cr"):
            m.add_block(rows(d[n], 0, 0))
        for second, j in mlp_order():
            m.add_block(rows(d["w_cv"], j * C, 0) if second else rows(d["w_ck"], 0, j * C))
        m.add_block(rows(d["Wq"], 0, 0))
        m.add_block(rows(d["Wk"], 0, 0, KX), KX)
        m.add_block(rows(d["Wv"], 0, 0, KX), KX)
        m.add_block(rows(d["Wo"], 0, 0))
        for e in range(E):
            for second, j in mlp_order():
                m.add_block(rows(d["W2"][e], j * C, 0) if second else rows(d["W1"][e], 0, j * C))
        for n in ("rq", "rk", "rv"):
            m.add_block(rows(d[n], 0, 0))
        for j in range(2):
            m.add_block(rows(d["xWq"], 0, j * C))
        for j in range(2):
            for n in ("xWk", "xWv"):
                m.add_block(rows(d[n], 0, j * C, KX), KX)
            m.add_block(rows(d["xWo"], j * C, 0))
        for i in range(6):
            m.add_block(rows(d["qw"][i], 0, 0), KC, I32)

        FREE = 2 * HEADS
        free = {"tensor": ("s_mm", "p_turn", "o_mm"), "scalar": ("p_exp", "pt_out", "v_out"), "vector": ("o_out", "s_clip", "k_low")}
        with nc.Block() as block:

            @block.tensor
            def _(pe):
                for s in free["tensor"]:
                    pe.sem_inc(g[s].sem, FREE)

            @block.scalar
            def _(act):
                for s in free["scalar"]:
                    act.sem_inc(g[s].sem, FREE)

            @block.sync
            def _(sp):
                sp.dma_start(x[:, :, :], d["x"]).then_inc(g["x_load"].sem, 16)
                sp.dma_start(par[:, :], d["params"]).then_inc(g["param_load"].sem, 16)
                sp.dma_start(m.ident[:, :], d["ident"]).then_inc(g["const_load"].sem, 16)
                m.load_blocks(sp, RING)

            @block.vector
            def _(dve):
                for s in free["vector"]:
                    dve.sem_inc(g[s].sem, FREE)
                dve.memset(m.mean_w[:, :], 1.0 / C)
                dve.memset(m.eps[:, :], EPS)
                dve.wait_ge(g["x_load"].sem, 16)
                dve.wait_ge(g["param_load"].sem, 16)
                dve.wait_ge(g["const_load"].sem, 16)

        g["const_load"].advance(16)
        for names in free.values():
            for s in names:
                g[s].advance(FREE)

        def add_to(dst, bias=None, bi=0):
            def evac(dve, c, n, bank):
                to = dst[:, c, halves(n)]
                if bias is None:
                    return dve.tensor_tensor(to, bank, to, ALU.add)
                return dve.scalar_tensor_tensor(to, bank, m.column(bias, bi + c), to, ALU.add, ALU.add)
            return evac

        def copy_to(dst, func=ACT.Copy, **kw):
            def evac(act, c, n, bank):
                return act.activation(dst[:, c, halves(n)], bank, func, **{k: (v(c) if callable(v) else v) for k, v in kw.items()})
            return evac

        with ExitStack() as st:
            sb = buffers(st)
            xl, h = (sb(n, [P, KC, T], F32) for n in ("xl", "h"))
            std = sb("std", [P, T], F32)
            keep = sb("keep", [P, 3 * KC], F32)
            with ExitStack() as st1:
                k_, v_ = (buffers(st1)(n, [P, KC, T], F32) for n in ("tk", "tv"))
                with ExitStack() as st2:
                    sb2 = buffers(st2)
                    tmp = sb2("mixed", [P, KC, T], F32)
                    pair = [sb2(f"mixp{i}", [P, 2, KC, T], F32R) for i in range(2)]
                    layer_norm(m, x, xl, tmp, std)
                    layer_norm(m, xl, h, tmp, std, "ln1_g", "ln1_b")
                    mixed_linears(m, h, [("mix_k", copy_to(k_)), ("mix_v", copy_to(v_)), ("mix_r", copy_to(h, ACT.Sigmoid))],
                                  pair, tmp, keep)
                with ExitStack() as st2:
                    wkv(m, k_, v_, h, xl, buffers(st2))
            with ExitStack() as st1:
                sb1 = buffers(st1)
                r2 = sb1("r2", [P, KC, T], F32)
                hid = sb1("hid", [P, 2, 2, KC, T], F32R)
                pre = sb1("pre", [P, KC, T], F32)
                ck = sb1("ck", [P, 2, KC, T], F32R)
                layer_norm(m, xl, h, pre, std, "ln2_g", "ln2_b")
                mixed_linears(m, h, [("cmix_r", copy_to(r2, ACT.Sigmoid)), ("cmix_k", None)], [hid[:, 0], ck], pre, keep)
                mlp(m, ck, h, pre[:, :, :].rearrange("p k (n t) -> p (k n) t", n=2), hid, 1)
                with nc.Block() as block:
                    ch = g["dve_chain"]

                    @block.vector
                    def _(dve):
                        dve.tensor_tensor(h[:, :, :], h[:, :, :], r2[:, :, :], ALU.mult).then_inc(ch.sem, 1)
                        dve.tensor_tensor(x[:, :, :], x[:, :, :], xl[:, :, :], ALU.add).then_inc(ch.sem, 1)
                        dve.wait_ge(ch.sem, ch.base + 2)
                        dve.tensor_tensor(x[:, :, :], x[:, :, :], h[:, :, :], ALU.add)
                ch.advance(2)
        if STAGES <= 1:
            return finish(m)

        def cross(parts, D, bo, name):
            with ExitStack() as st:
                sb = buffers(st)
                q = sb("q" + name, [P, KC * parts, T], F32)
                bq = sb("bq" + name, [P, KC], F32)
                with ExitStack() as st2:
                    sb2 = buffers(st2)
                    u, tmp = (sb2(n + name, [P, KC, T], F32) for n in ("xu", "xt"))
                    pair = sb2("xp" + name, [P, 2, KC, T], F32R)
                    std = sb2("xs" + name, [P, T], F32)
                    layer_norm(m, x, u, tmp, std, pair=pair)
                    w = m.used
                    if parts == 1:
                        with nc.Block() as block:
                            @block.vector
                            def _(dve):
                                dve.tensor_scalar(bq[:, :], par[:, COL["bq"]:COL["bq"] + KC], D ** -0.5, None, ALU.mult)
                        evac = copy_to(q, ACT.Identity, scale=D ** -0.5, bias=lambda c: bq[:, c:c + 1])
                    else:
                        evac = copy_to(q, ACT.Copy, scale=D ** -0.5)
                    linear(m, pair, [w + i for i in range(parts)], evac)
                for i in range(parts):
                    with ExitStack() as st2:
                        sb2 = buffers(st2)
                        o = q[:, i * KC:(i + 1) * KC]
                        with ExitStack() as st3:
                            attention(m, o, D, parts == 1, parts == 1, SCHEDULE[D], f"{name}{i}", buffers(st3))
                        pair = sb2(f"op{name}{i}", [P, 2, KC, T], F32R)
                        linear(m, pair, [m.used], add_to(x, bo if i == 0 else None), "vector", whole=o)

        cross(1, 32, "bo", "a")
        if STAGES <= 2:
            return finish(m)

        with ExitStack() as st:
            sb = buffers(st)
            pre, y = (sb(n, [P, KC, T], F32) for n in ("eu", "ey"))
            pair = sb("eup", [P, 2, KC, T], F32R)
            gate = sb("gate", [P, E * T], F32)
            b1 = sb("b1", [P, FF // P], F32)
            with ExitStack() as st2:
                sb2 = buffers(st2)
                std = sb2("es", [P, T], F32)
                layer_norm(m, x, pre, y, std, pair=pair)
                gates(m, pre, gate, y, sb2)
            hid = sb("ehid", [P, 2, 2, KC, T], F32R)
            mlp(m, pair, y, pre[:, :, :].rearrange("p k (n t) -> p (k n) t", n=2), hid, E, gate, b1, clear=False)
            with nc.Block() as block:
                @block.vector
                def _(dve):
                    dve.tensor_tensor(x[:, :, :], x[:, :, :], y[:, :, :], ALU.add)
        if STAGES <= 3:
            return finish(m)

        with ExitStack() as st:
            sb = buffers(st)
            u, q, k_ = (sb(n, [P, KC, T], F32) for n in ("ru", "rqt", "rkt"))
            v = sb("rvt", [S, B, C], F32)
            sT = sb("rst", [S, B, S], F32)
            std = sb("rs", [P, T], F32)
            theta = sb("theta", [P, KC], F32)
            decay = sb("decay", [S, S], F32)
            pair = sb("rp", [P, 2, KC, T], F32R)
            layer_norm(m, x, u, q, std, pair=pair)
            ld = g["const_load"]
            with nc.Block() as block:
                @block.sync
                def _(sp):
                    sp.dma_start(decay[:, :], d["decay"]).then_inc(ld.sem, 16)

                @block.scalar
                def _(act):
                    act.activation(theta[:, :], par[:, COL["theta"]:COL["theta"] + KC], ACT.Exp, scale=0.0)
                    act.wait_ge(ld.sem, ld.base + 16)
            ld.advance(16)
            w = m.used
            scaled = dict(scale=lambda c: theta[:, c:c + 1])
            linear(m, pair, [w], copy_to(q, ACT.Identity, **scaled))
            linear(m, pair, [w + 1], copy_to(k_, ACT.Identity, **scaled))
            values(m, pair, v)
            retention(m, q, k_, v, sT, decay)
        if STAGES <= 4:
            return finish(m)

        cross(2, 64, "xbo", "b")
        if STAGES <= 5:
            return finish(m)

        with ExitStack() as st:
            sb = buffers(st)
            u, h, t_ = (sb(n, [P, KC, T], F32) for n in ("fu", "fh", "ft"))
            std = sb("fs", [P, T], F32)
            pair = sb("fp", [P, 2, KC, T], F32R)
            weights = Quantised(m, sb)
            weights.first()
            layer_norm(m, x, h, t_, std, pair=pair)
            for blk in range(3):
                i = 2 * blk
                linear(m, pair, [m.used], copy_to(u, ACT.Identity, bias=lambda c: m.column("qbias", i * KC + c)),
                       "scalar", weights, i, whole=h if blk > 0 else None)
                layer_norm(m, u, u, t_, std, "gamma", "beta", ACT.Gelu, blk * KC, pair)
                i = 2 * blk + 1
                linear(m, pair, [m.used], add_to(h, "qbias", i * KC), "vector", weights, i)
            with nc.Block() as block:
                @block.vector
                def _(dve):
                    dve.tensor_tensor(x[:, :, :], x[:, :, :], h[:, :, :], ALU.add)
        finish(m)


STAGES = 99


def finish(m):
    with m.nc.Block() as block:

        @block.sync
        def _(sp):
            sp.dma_start(m.d["out"], m.x[:, :, :]).then_inc(m.sig["store"].sem, 16)
            sp.wait_ge(m.sig["store"].sem, 16)
            for w in range(m.loaded - RING, m.loaded):
                m.wait_block(sp, w)




def kernel(**inputs):
    import numpy as np
    import concourse.bacc as bacc
    from concourse.bass_utils import run_bass_kernel_spmd

    a = {k: np.asarray(v) for k, v in inputs.items()}

    def cols(v):
        return np.asarray(v).reshape(-1, P).T

    L0, X0, F0, R1, X1, F1 = "L0_attn_", "L0_xattn_", "L0_ffn_", "L1_attn_", "L1_xattn_", "L1_ffn_"
    par = {n: a[L0 + n] for n in ("time_decay", "time_first", "ln1_g", "ln1_b", "ln2_g", "ln2_b",
                                  "mix_k", "mix_v", "mix_r", "cmix_k", "cmix_r")}
    par |= {n: a[X0 + n] for n in ("bq", "bk", "bv", "bo")}
    par |= {"theta": a[R1 + "theta"], "xbo": a[X1 + "bo"], "qbias": a[F1 + "biases"],
            "gamma": a[F1 + "ln_gamma"], "beta": a[F1 + "ln_beta"], "b1": a[F0 + "b1"]}
    diff = np.arange(S)[None, :] - np.arange(S)[:, None]
    decay = np.where(diff >= 0, np.float32(0.96875) ** np.maximum(diff, 0).astype(np.float32), np.float32(0))
    arrays = {
        "x": a["x"].reshape(T, KC, P).transpose(2, 1, 0),
        "ctx": a["ctx_768"].reshape(B, NKV, KX, P).transpose(0, 3, 2, 1),
        "params": np.concatenate([cols(par[n]) for n, _ in PARAMS], axis=1),
        "ident": np.eye(P, dtype=np.float32),
        "before": np.broadcast_to(np.tri(E, E, -1, dtype=np.float32), (P, E, E)),
        "pick": np.broadcast_to(np.eye(E, dtype=np.float32)[:, :, None], (E, E, P)),
        "decay": decay.astype(np.float32),
        "centroids": a[F0 + "centroids"].reshape(E, KC, P).transpose(2, 1, 0),
        "W1": a[F0 + "W1"], "W2": a[F0 + "W2"], "b2": a[F0 + "b2"],
        "rq": a[R1 + "weight_q"], "rk": a[R1 + "weight_k"], "rv": a[R1 + "weight_v"],
        "qw": a[F1 + "qweights"].transpose(0, 2, 1),
        "scales": a[F1 + "scales"].transpose(0, 2, 1),
        "lora_a": a[F1 + "lora_a"], "lora_b": a[F1 + "lora_b"].transpose(0, 2, 1),
    }
    arrays |= {n: a[L0 + n] for n in ("w_tk", "w_tv", "w_tr", "w_ck", "w_cv", "w_cr")}
    arrays |= {n: a[X0 + n] for n in ("Wq", "Wk", "Wv", "Wo")}
    arrays |= {"x" + n: a[X1 + n] for n in ("Wq", "Wk", "Wv", "Wo")}
    nc = bacc.Bacc("TRN2", target_bir_lowering=False, num_devices=1)
    given, d = {}, {}
    for n, v in arrays.items():
        given[f"in_{n}"] = v = np.ascontiguousarray(v)
        d[n] = nc.dram_tensor(f"in_{n}", v.shape, mybir.dt.from_np(v.dtype), kind="ExternalInput").ap()
    d["out"] = nc.dram_tensor("out_x", (P, KC, T), F32, kind="ExternalOutput").ap()
    build(nc, d)
    r = run_bass_kernel_spmd(nc, [given], core_ids=[0])
    out = np.asarray(r.results[0]["out_x"])
    return np.ascontiguousarray(out.transpose(2, 1, 0).reshape(B, S, C))
```
